# Optimizing a Trainium2 kernel written in Bass

```python
import numpy as np
import jax
import jax.numpy as jnp

def _softmax(x, axis=-1):
    return jax.nn.softmax(x, axis=axis)

def _gelu(x):
    return jax.nn.gelu(x, approximate=True)

def _silu(x):
    return jax.nn.silu(x)

def _sigmoid(x):
    return jax.nn.sigmoid(x)

def _layernorm(x, axis=-1, eps=1e-05):
    m = jnp.mean(x, axis=axis, keepdims=True)
    v = jnp.var(x, axis=axis, keepdims=True)
    return (x - m) / jnp.sqrt(v + eps)

def _scatter_add(tgt, idx, src, axis=0):
    return tgt.at[idx].add(src)

def _segment_sum(src, seg, n):
    return jax.ops.segment_sum(src, seg, n)
kernel_name = 'mk_seq_postln_d1_jaxref_r4_80aa3b'

def setup_inputs(seed: int=0):
    np.random.seed(seed)
    _w = jnp.asarray

    def _L0_attn_setup():
        import jax, jax.numpy as jnp
        import numpy as np
        GROUP = 64
        MAX_REL = 32

        def _silu(x):
            return x * jax.nn.sigmoid(x)

        def _ln(x, w, b, eps=1e-05):
            m = x.mean(-1, keepdims=True)
            v = ((x - m) ** 2).mean(-1, keepdims=True)
            return (x - m) / jnp.sqrt(v + eps) * w + b

        def _rope(x):
            n, d = (x.shape[-2], x.shape[-1])
            half = d // 2
            pos = jnp.arange(n, dtype=x.dtype)
            inv_freq = 10000.0 ** (-jnp.arange(half, dtype=x.dtype) / half)
            sinusoid = pos[:, None] * inv_freq[None, :]
            sin, cos = (jnp.sin(sinusoid), jnp.cos(sinusoid))
            x1, x2 = (x[..., :half], x[..., half:])
            return jnp.concatenate([x1 * cos - x2 * sin, x2 * cos + x1 * sin], axis=-1)
        key = jax.random.key(seed)
        ks = jax.random.split(key, 8)
        B, N, D, QK, H = (4, 1024, 256, 64, 512)
        s = 0.02
        return {'x': jax.random.normal(ks[0], (B, N, D), dtype=jnp.float32), 'ln1_w': jnp.ones((D,), jnp.float32), 'ln1_b': jnp.zeros((D,), jnp.float32), 'Wqk': jax.random.normal(ks[1], (QK, D), jnp.float32) * s, 'bqk': jnp.zeros((QK,), jnp.float32), 'Wv': jax.random.normal(ks[2], (H, D), jnp.float32) * s, 'bv': jnp.zeros((H,), jnp.float32), 'Wg': jax.random.normal(ks[3], (H, D), jnp.float32) * s, 'bg': jnp.zeros((H,), jnp.float32), 'Wo': jax.random.normal(ks[4], (D, H), jnp.float32) * s, 'bo': jnp.zeros((D,), jnp.float32), 'ln2_w': jnp.ones((D,), jnp.float32), 'ln2_b': jnp.zeros((D,), jnp.float32), 'gamma': jax.random.normal(ks[5], (4, QK), jnp.float32) * 0.02, 'beta': jnp.zeros((4, QK), jnp.float32), 'pos_emb': jax.random.normal(ks[6], (2 * MAX_REL + 1,), jnp.float32)}
    _L0_attn_in = _L0_attn_setup()

    def _L0_ffn_setup():
        import jax, jax.numpy as jnp
        import numpy as np
        import math
        N_EMBD = 256
        HIDDEN = 4 * N_EMBD
        N_EXPERTS = 8
        TOP_K = 2
        B, T = (4, 512)

        def new_gelu(x):
            c = math.sqrt(2.0 / math.pi)
            return 0.5 * x * (1.0 + jnp.tanh(c * (x + 0.044715 * x * x * x)))

        def _moe_forward(x, Wfc_s, bfc_s, Wproj_s, bproj_s, Wr, Wfc, bfc, Wproj, bproj):
            Bb, Tt, C = x.shape
            xf = x.reshape(Bb * Tt, C)
            N = Bb * Tt
            shared = new_gelu(xf @ Wfc_s + bfc_s) @ Wproj_s + bproj_s
            logits = xf @ Wr
            probs = jax.nn.softmax(logits, axis=-1)
            topk_p, topk_i = jax.lax.top_k(probs, TOP_K)
            topk_p = topk_p / jnp.sum(topk_p, axis=-1, keepdims=True)
            gate = jnp.zeros((N, N_EXPERTS), dtype=xf.dtype)
            gate = gate.at[jnp.arange(N)[:, None], topk_i].add(topk_p)
            routed = jnp.zeros_like(xf)
            for e in range(N_EXPERTS):
                h = new_gelu(xf @ Wfc[e] + bfc[e]) @ Wproj[e] + bproj[e]
                routed = routed + h * gate[:, e:e + 1]
            return (shared + routed).reshape(Bb, Tt, C)
        key = jax.random.key(seed)
        ks = jax.random.split(key, 10)
        s = 0.02
        return {'x': jax.random.normal(ks[0], (B, T, N_EMBD), dtype=jnp.float32), 'Wfc_s': jax.random.normal(ks[1], (N_EMBD, HIDDEN), dtype=jnp.float32) * s, 'bfc_s': jnp.zeros((HIDDEN,), dtype=jnp.float32), 'Wproj_s': jax.random.normal(ks[2], (HIDDEN, N_EMBD), dtype=jnp.float32) * s, 'bproj_s': jnp.zeros((N_EMBD,), dtype=jnp.float32), 'Wr': jax.random.normal(ks[3], (N_EMBD, N_EXPERTS), dtype=jnp.float32) * s, 'Wfc': jax.random.normal(ks[4], (N_EXPERTS, N_EMBD, HIDDEN), dtype=jnp.float32) * s, 'bfc': jnp.zeros((N_EXPERTS, HIDDEN), dtype=jnp.float32), 'Wproj': jax.random.normal(ks[5], (N_EXPERTS, HIDDEN, N_EMBD), dtype=jnp.float32) * s, 'bproj': jnp.zeros((N_EXPERTS, N_EMBD), dtype=jnp.float32)}
    _L0_ffn_in = _L0_ffn_setup()
    _d = {'L0_attn_x': _L0_attn_in['x'], 'L0_attn_ln1_w': _L0_attn_in['ln1_w'], 'L0_attn_ln1_b': _L0_attn_in['ln1_b'], 'L0_attn_Wqk': _L0_attn_in['Wqk'], 'L0_attn_bqk': _L0_attn_in['bqk'], 'L0_attn_Wv': _L0_attn_in['Wv'], 'L0_attn_bv': _L0_attn_in['bv'], 'L0_attn_Wg': _L0_attn_in['Wg'], 'L0_attn_bg': _L0_attn_in['bg'], 'L0_attn_Wo': _L0_attn_in['Wo'], 'L0_attn_bo': _L0_attn_in['bo'], 'L0_attn_ln2_w': _L0_attn_in['ln2_w'], 'L0_attn_ln2_b': _L0_attn_in['ln2_b'], 'L0_attn_gamma': _L0_attn_in['gamma'], 'L0_attn_beta': _L0_attn_in['beta'], 'L0_attn_pos_emb': _L0_attn_in['pos_emb'], 'L0_ffn_Wfc_s': _L0_ffn_in['Wfc_s'], 'L0_ffn_bfc_s': _L0_ffn_in['bfc_s'], 'L0_ffn_Wproj_s': _L0_ffn_in['Wproj_s'], 'L0_ffn_bproj_s': _L0_ffn_in['bproj_s'], 'L0_ffn_Wr': _L0_ffn_in['Wr'], 'L0_ffn_Wfc': _L0_ffn_in['Wfc'], 'L0_ffn_bfc': _L0_ffn_in['bfc'], 'L0_ffn_Wproj': _L0_ffn_in['Wproj'], 'L0_ffn_bproj': _L0_ffn_in['bproj']}
    _x0 = _d['L0_attn_x']
    _d['L0_attn_x'] = jax.random.normal(jax.random.fold_in(jax.random.key(seed), 1), (8, 512, 256), dtype=_x0.dtype)
    del _x0
    return _d

def reference(L0_attn_x, L0_attn_ln1_w, L0_attn_ln1_b, L0_attn_Wqk, L0_attn_bqk, L0_attn_Wv, L0_attn_bv, L0_attn_Wg, L0_attn_bg, L0_attn_Wo, L0_attn_bo, L0_attn_ln2_w, L0_attn_ln2_b, L0_attn_gamma, L0_attn_beta, L0_attn_pos_emb, L0_ffn_Wfc_s, L0_ffn_bfc_s, L0_ffn_Wproj_s, L0_ffn_bproj_s, L0_ffn_Wr, L0_ffn_Wfc, L0_ffn_bfc, L0_ffn_Wproj, L0_ffn_bproj):

    def _L0_attn_ref(x, ln1_w, ln1_b, Wqk, bqk, Wv, bv, Wg, bg, Wo, bo, ln2_w, ln2_b, gamma, beta, pos_emb):
        import jax, jax.numpy as jnp
        import numpy as np
        GROUP = 64
        MAX_REL = 32

        def _silu(x):
            return x * jax.nn.sigmoid(x)

        def _ln(x, w, b, eps=1e-05):
            m = x.mean(-1, keepdims=True)
            v = ((x - m) ** 2).mean(-1, keepdims=True)
            return (x - m) / jnp.sqrt(v + eps) * w + b

        def _rope(x):
            n, d = (x.shape[-2], x.shape[-1])
            half = d // 2
            pos = jnp.arange(n, dtype=x.dtype)
            inv_freq = 10000.0 ** (-jnp.arange(half, dtype=x.dtype) / half)
            sinusoid = pos[:, None] * inv_freq[None, :]
            sin, cos = (jnp.sin(sinusoid), jnp.cos(sinusoid))
            x1, x2 = (x[..., :half], x[..., half:])
            return jnp.concatenate([x1 * cos - x2 * sin, x2 * cos + x1 * sin], axis=-1)
        b, n, d = x.shape
        G = GROUP
        x = _ln(x, ln1_w, ln1_b)
        qk = _silu(x @ Wqk.T + bqk)
        v = _silu(x @ Wv.T + bv)
        heads = qk[..., None, :] * gamma + beta
        quad_q, lin_q, quad_k, lin_k = (heads[..., i, :] for i in range(4))
        quad_q, lin_q, quad_k, lin_k = map(_rope, (quad_q, lin_q, quad_k, lin_k))
        g = n // G
        rs = lambda t: t.reshape(b, g, G, t.shape[-1])
        qq, lq, qkk, lk, vg = map(rs, (quad_q, lin_q, quad_k, lin_k, v))
        idx = jnp.arange(G)
        dist = jnp.clip(jnp.abs(idx[:, None] - idx[None, :]), 0, MAX_REL)
        bias = pos_emb[dist]
        quad_att = jnp.einsum('bgid,bgjd->bgij', qq, qkk) / G + bias
        attn = jax.nn.relu(quad_att) ** 2
        quad_out = jnp.einsum('bgij,bgje->bgie', attn, vg)
        lin_kv = jnp.einsum('bgnd,bgne->bde', lk, vg) / n
        lin_out = jnp.einsum('bgnd,bde->bgne', lq, lin_kv)
        qo = quad_out.reshape(b, n, -1)
        lo = lin_out.reshape(b, n, -1)
        gate = _silu(x @ Wg.T + bg)
        out = gate * (qo + lo)
        out = out @ Wo.T + bo
        return _ln(out, ln2_w, ln2_b)

    def _L0_ffn_ref(x, Wfc_s, bfc_s, Wproj_s, bproj_s, Wr, Wfc, bfc, Wproj, bproj):
        import jax, jax.numpy as jnp
        import numpy as np
        import math
        N_EMBD = 256
        HIDDEN = 4 * N_EMBD
        N_EXPERTS = 8
        TOP_K = 2
        B, T = (4, 512)

        def new_gelu(x):
            c = math.sqrt(2.0 / math.pi)
            return 0.5 * x * (1.0 + jnp.tanh(c * (x + 0.044715 * x * x * x)))

        def _moe_forward(x, Wfc_s, bfc_s, Wproj_s, bproj_s, Wr, Wfc, bfc, Wproj, bproj):
            Bb, Tt, C = x.shape
            xf = x.reshape(Bb * Tt, C)
            N = Bb * Tt
            shared = new_gelu(xf @ Wfc_s + bfc_s) @ Wproj_s + bproj_s
            logits = xf @ Wr
            probs = jax.nn.softmax(logits, axis=-1)
            topk_p, topk_i = jax.lax.top_k(probs, TOP_K)
            topk_p = topk_p / jnp.sum(topk_p, axis=-1, keepdims=True)
            gate = jnp.zeros((N, N_EXPERTS), dtype=xf.dtype)
            gate = gate.at[jnp.arange(N)[:, None], topk_i].add(topk_p)
            routed = jnp.zeros_like(xf)
            for e in range(N_EXPERTS):
                h = new_gelu(xf @ Wfc[e] + bfc[e]) @ Wproj[e] + bproj[e]
                routed = routed + h * gate[:, e:e + 1]
            return (shared + routed).reshape(Bb, Tt, C)
        return _moe_forward(x, Wfc_s, bfc_s, Wproj_s, bproj_s, Wr, Wfc, bfc, Wproj, bproj)
    x = L0_attn_x
    x = _layernorm(x + _L0_attn_ref(x, L0_attn_ln1_w, L0_attn_ln1_b, L0_attn_Wqk, L0_attn_bqk, L0_attn_Wv, L0_attn_bv, L0_attn_Wg, L0_attn_bg, L0_attn_Wo, L0_attn_bo, L0_attn_ln2_w, L0_attn_ln2_b, L0_attn_gamma, L0_attn_beta, L0_attn_pos_emb), axis=-1)
    x = _layernorm(x + _L0_ffn_ref(x, L0_ffn_Wfc_s, L0_ffn_bfc_s, L0_ffn_Wproj_s, L0_ffn_bproj_s, L0_ffn_Wr, L0_ffn_Wfc, L0_ffn_bfc, L0_ffn_Wproj, L0_ffn_bproj), axis=-1)
    return x

_drawn_inputs = setup_inputs


def setup_inputs(seed=0):
    import zlib

    import numpy as np

    out = dict(_drawn_inputs(seed))
    spreads = {'L0_attn_ln1_w': (1.0, 0.2),
     'L0_attn_ln1_b': (0.0, 0.1),
     'L0_attn_bqk': (0.0, 2.0),
     'L0_attn_bv': (0.0, 0.1),
     'L0_attn_bg': (0.0, 0.1),
     'L0_attn_bo': (0.0, 0.1),
     'L0_attn_ln2_w': (1.0, 0.2),
     'L0_attn_ln2_b': (0.0, 0.1),
     'L0_attn_beta': (0.0, 0.8),
     'L0_ffn_bfc_s': (0.0, 0.1),
     'L0_ffn_bproj_s': (0.0, 0.1),
     'L0_ffn_bfc': (0.0, 0.323),
     'L0_ffn_bproj': (0.0, 0.1)}
    factors = {'L0_attn_Wqk': 8.0, 'L0_attn_gamma': 8.0}
    for name, (base, spread) in spreads.items():
        noise = np.random.default_rng([zlib.crc32(name.encode()), seed]).standard_normal(out[name].shape)
        drawn = base * np.exp(spread * noise) if base else spread * noise
        out[name] = jnp.asarray(drawn.astype(out[name].dtype))
    for name, factor in factors.items():
        out[name] = (out[name] * factor).astype(out[name].dtype)
    return out
```

```python
from contextlib import ExitStack

import numpy as np

import concourse.bass as bass
from concourse import mybir

F32 = mybir.dt.float32
F32R = mybir.dt.float32r
BF16 = mybir.dt.bfloat16
I32 = mybir.dt.int32
U32 = mybir.dt.uint32
ALU = mybir.AluOpType
ACT = mybir.ActivationFunctionType
AX = mybir.AxisListType.X

P = 128
B, T, D = 8, 512, 256
N = B * T
QK = 64
E = 512
G = 64
MAX_REL = 32
HID = 1024
NE = 8
KD = D // P
KE = E // P
KH = HID // P
TT = T // P
NT = N // P
S = 512
ST = S // P
SHARED = N // S
ROUTED = (2 * N - NE) // S + NE
SLOTS = ROUTED * S
ROW = D + 2
NOWHERE = float(4 * N)
EPS = 1e-5
RSQRT_SEED = float(0x5F3759DF)
BQK, GQ, GK, BQ, BK, L1W, L1B, BG = 0, 2, 4, 6, 8, 10, 12, 14
NVEC = 18


def need(engine, sem, n):
    if not isinstance(n, int) or n > 0:
        engine.wait_ge(sem, n)


class Links:

    def __init__(self, engine, sem):
        self.engine, self.sem, self.base, self.k, self.loop = engine, sem, 0, 0, None

    def __call__(self, instruction):
        self.k += 1
        instruction.then_inc(self.sem, 1)
        self.engine.wait_ge(self.sem, self.base + self.k)

    def total(self):
        return self.base + self.k

    def at(self, base):
        self.base, self.k = base, 0

    def enter(self, step, first, per_step):
        if not self.loop:
            self.loop = (self.total(), per_step)
        self.at(self.loop[0] + (step - first) * per_step)

    def leave(self):
        assert self.k == self.loop[1], (self.k, self.loop)

    def end(self, steps):
        self.at(self.loop[0] + steps * self.loop[1])
        self.loop = None


def rsqrt(nc, link, y, half, v, tmp):
    link(nc.vector.tensor_single_scalar(half, v.bitcast(I32), 1, ALU.logical_shift_right))
    link(nc.vector.tensor_scalar(y.bitcast(I32), half, -1.0, RSQRT_SEED, ALU.mult, ALU.add))
    for _ in range(3):
        link(nc.vector.tensor_tensor(tmp, y, y, ALU.mult))
        link(nc.vector.scalar_tensor_tensor(tmp, tmp, -0.5, v, ALU.mult, ALU.mult))
        link(nc.vector.scalar_tensor_tensor(y, tmp, 1.5, y, ALU.add, ALU.mult))


def moments(nc, link, st, mean, var, tmp):
    part = lambda i: st[:, :, i]
    nc.vector.tensor_tensor(mean, part(1), part(4), ALU.add)
    nc.vector.tensor_tensor(tmp, part(1), part(4), ALU.subtract)
    link(nc.vector.tensor_tensor(var, part(2), part(5), ALU.add))
    nc.vector.tensor_scalar(mean, mean, 0.5, None, ALU.mult)
    nc.vector.scalar_tensor_tensor(tmp, tmp, 0.25, tmp, ALU.mult, ALU.mult)
    link(nc.vector.tensor_scalar(var, var, 1.0 / D, EPS, ALU.mult, ALU.add))
    link(nc.vector.tensor_tensor(var, var, tmp, ALU.add))


def build(nc, a, out):
    ctx = ExitStack()

    def sem(name):
        return ctx.enter_context(nc.semaphore(name))

    XHL = nc.dram_tensor("x1_parts", (B, P, 2 * KD * T), F32, kind="Internal").ap()
    X1D = nc.dram_tensor("x1_rows", (N, D), F32, kind="Internal").ap()
    XS = nc.dram_tensor("slot_rows", (SLOTS, ROW), F32, kind="Internal").ap()
    YY = nc.dram_tensor("expert_results", (2 * N, D), F32, kind="Internal").ap()

    with ctx:
        keep = lambda n, s, t: ctx.enter_context(nc.sbuf_tensor("k_" + n, s, t))
        ident = keep("ident", [P, P], F32)
        ones2 = keep("ones2", [2, P], F32R)
        mask2 = keep("mask2", [2, 2], F32)
        logits = keep("logits", [P, NT, NE], F32)
        wstage = keep("wstage", [P, 2, KD * HID], F32)
        wfc1 = [keep(f"wfc1{p}", [P, KD, HID], F32R) for p in "hl"]
        wpj1 = [keep(f"wpj1{p}", [P, KH, D], F32R) for p in "hl"]
        bfc = [keep(f"bfc{i}", [P, KH], F32) for i in range(2)]
        bpj_raw = [keep(f"bpj_raw{i}", [2, D], F32) for i in range(2)]
        bpj = [keep(f"bpj{i}", [2, D], F32R) for i in range(2)]
        row_t = keep("row_t", [2, E], F32)
        row_h = keep("row_h", [2, E], F32R)

        attention(nc, a, locals())
        experts(nc, a, out, locals())


def attention(nc, a, shared):
    ident, ones2, mask2, logits = (shared[k] for k in ("ident", "ones2", "mask2", "logits"))
    wstage, wfc1, wpj1, bpj_raw, bpj = (shared[k] for k in ("wstage", "wfc1", "wpj1", "bpj_raw", "bpj"))
    row_t, row_h = shared["row_t"], shared["row_h"]
    bfc = shared["bfc"]
    XHL, X1D, XS = shared["XHL"], shared["X1D"], shared["XS"]
    with ExitStack() as ctx:
        sb = lambda n, s, t=F32: ctx.enter_context(nc.sbuf_tensor("s_" + n, s, t))
        sem = lambda n: ctx.enter_context(nc.semaphore(n))
        pair = lambda n, s: [sb(n + p, s, F32R) for p in "hl"]

        vec = sb("vec", [P, NVEC])
        rope = sb("rope", [P, 2, T])
        offs = sb("offs", [P, 2, T])
        bias = sb("bias", [P, G])
        ln2 = sb("ln2", [P, 2, D])
        wr = sb("wr", [P, KD, NE])
        wqk, wv, wg, wo = (pair(n, s) for n, s in (("wqk", [P, 2, KD, P]), ("wv", [P, KD, E]),
                                                   ("wg", [P, KD, E]), ("wo", [P, KE, D])))
        rows_raw = sb("rows_raw", [2, 2, E])
        bv2 = sb("bv2", [2, E], F32R)
        bo2 = sb("bo2", [2, D], F32R)
        ones_raw = sb("ones_raw", [2, P])
        empty = sb("empty", [P, ROW])
        x_in = sb("x_in", [P, TT, D])
        x_res = sb("x_res", [P, TT, D])
        xn = sb("xn", [P, TT, D])
        xT = sb("xT", [P, KD, T])
        xTh, xTl = pair("xT", [P, KD, T])
        v = sb("v", [P, TT, E])
        qk = sb("qk", [P, 2, T])
        qkr = sb("qkr", [P, 2, T])
        heads = sb("heads", [P, 2, T])
        kT = sb("kT", [P, TT, P])
        att = sb("att", [P, TT, P])
        kv = sb("kv", [P, E])
        u = sb("u", [P, KE, T])
        uh, ul = pair("u", [P, KE, T])
        z = sb("z", [P, TT, D])
        x1 = sb("x1", [P, TT, D])
        x1T = sb("x1T", [P, KD, T])
        x1h, x1l = pair("x1", [P, KD, T])
        st = sb("st", [P, 2 * TT, 6])
        mean = sb("mean", [P, 2 * TT])
        var, rs, tmp = sb("var", [P, 2 * TT]), sb("rs", [P, 2 * TT]), sb("tmp", [P, 2 * TT])
        half = sb("half", [P, 2 * TT], I32)
        raw = wstage[:, :, :].rearrange("p a n -> p (a n)")
        raw_v, raw_g = raw[:, 0:1024].rearrange("p (k n) -> p k n", k=KD), raw[:, 1024:2048].rearrange("p (k n) -> p k n", k=KD)
        raw_qk = raw[:, 2048:2560].rearrange("p (s k n) -> p s k n", s=2, k=KD)
        raw_o = raw[:, 2560:3584].rearrange("p (k n) -> p k n", k=KE)

        bank = [ctx.enter_context(nc.psum_tensor(f"bank{i}", [P, 512], F32)) for i in range(8)]

        ld_c, ld_v, ld_x, ld_r = sem("consts_loaded"), sem("weights_loaded"), sem("x_loaded"), sem("residual_loaded")
        ld_s = sem("shared_weights_loaded")
        filled = sem("slots_emptied")
        wh_rd, wl_rd, split_s = sem("weights_hi_ready"), sem("weights_lo_ready"), sem("shared_weights_split")
        dve_own, act_own = sem("vector_own"), sem("scalar_own")
        xn_ready, xT_mm, xT_ev, xTh_rd, xTl_rd = (sem(n) for n in ("xn_ready", "xT_transposed", "xT_evacuated", "xTh_ready", "xTl_ready"))
        v_mm, v_ev, q_mm, q_ev, qkr_rd, heads_rd = (sem(n) for n in ("v_product", "v_ready", "qk_product", "qk_ready", "qk_roped", "heads_ready"))
        o_mm, o_ev, g_mm, g_ev = (sem(n) for n in ("o_product", "o_evacuated", "gate_product", "gate_ready"))
        kT_mm, kT_ev, sc_mm, att_rd, kv_mm, kv_ev = (sem(n) for n in ("kT_transposed", "kT_ready", "scores_product", "att_ready", "kv_product", "kv_ready"))
        u_mm, u_ml, uh_rd, ul_rd = (sem(n) for n in ("u_product", "u_gated", "uh_ready", "ul_ready"))
        res_rd, res_used, x1_rd, x1T_mm, x1T_ev, lg_mm, lg_ev = (sem(n) for n in (
            "residual_ready", "residual_used", "x1_ready", "x1T_transposed", "x1T_evacuated", "logits_product", "logits_ready"))
        x1h_rd, x1l_rd, sh_st, x1_st = (sem(n) for n in ("x1h_ready", "x1l_ready", "parts_stored", "x1_stored"))
        tab_rd = sem("tables_ready")

        block = ctx.enter_context(nc.Block())
        x_view = a["x"].rearrange("(b t p) d -> b p t d", b=B, p=P)
        x1_view = X1D.rearrange("(b t p) d -> b p t d", b=B, p=P)

        def bidx(ap, b):
            return ap[bass.ds(b, 1)].rearrange("b p t d -> (b p) t d")

        @block.sync
        def _(sp):
            sp.dma_start(x_in[:, :, :], bidx(x_view, 0)).then_inc(ld_x, 16)
            for dst, src in ((raw_v, "wv"), (raw_qk, "wqk"), (raw_g, "wg"), (raw_o, "wo")):
                sp.dma_start(dst, a[src]).then_inc(ld_v, 16)
            consts = ((vec[:, :], a["vec"]), (ident[:, :], a["ident"]), (rope[:, :, :], a["rope"]),
                      (ln2[:, :, :], a["ln2"]), (wr[:, :, :], a["wr"]), (rows_raw[:, :, :], a["rows"]),
                      (ones_raw[:, :], a["ones"]), (mask2[:, :], a["mask2"]), (empty[:, :], a["empty"]),
                      (bfc[1][:, :], a["bfc"][NE]), (bpj_raw[1][:, :], a["bproj"][NE]))
            for dst, src in consts:
                sp.dma_start(dst, src).then_inc(ld_c, 16)
            skew = a["ext"][G - 1:G - 1 + (2 * G - 2) * G].rearrange("(j n) -> j n", n=2 * G - 2)[:, 0:G]
            for h in range(2):
                sp.dma_start(bias[h * G:(h + 1) * G, :], skew).then_inc(ld_c, 16)
            for q in range(4):
                rows = SLOTS // P // 4
                dst = XS[q * rows * P:(q + 1) * rows * P, :].rearrange("(p r) w -> p r w", r=rows)
                if q == 0:
                    sp.wait_ge(ld_c, 16 * (len(consts) + 2))
                sp.dma_start(dst, empty[:, :].rearrange("p (o w) -> p o w", o=1).to_broadcast([P, rows, ROW])).then_inc(filled, 16)
            sp.wait_ge(xn_ready, 1)
            sp.dma_start(x_in[:, :, :], bidx(x_view, 1)).then_inc(ld_x, 16)
            sp.wait_ge(wl_rd, 4)
            sp.dma_start(wstage[:, :, :], a["wall"][NE]).then_inc(ld_s, 16)

            def step(b, first=False, last=False, tail=False):
                if not tail:
                    need(sp, res_used, b)
                    sp.dma_start(x_res[:, :, :], bidx(x_view, b)).then_inc(ld_r, 16)
                if not (last or tail):
                    sp.wait_ge(xn_ready, b + 2)
                    if not (isinstance(b, int) and b + 2 >= B):
                        sp.dma_start(x_in[:, :, :], bidx(x_view, b + 2)).then_inc(ld_x, 16)
                if not first:
                    sp.wait_ge(x1_rd, b)
                    sp.dma_start(bidx(x1_view, b - 1), x1[:, :, :]).then_inc(x1_st, 16)
                    dst = XHL[bass.ds(b - 1, 1)].rearrange("b p n -> (b p) n")
                    sp.wait_ge(x1h_rd, 2 * b)
                    sp.dma_start(dst[:, 0:KD * T], x1h[:, :, :].bitcast(F32).rearrange("p k n -> p (k n)")).then_inc(sh_st, 16)
                    sp.wait_ge(x1l_rd, 2 * b)
                    sp.dma_start(dst[:, KD * T:], x1l[:, :, :].bitcast(F32).rearrange("p k n -> p (k n)")).then_inc(sh_st, 16)

            step(0, first=True)
            step(1)
            with sp.Fori(2, B - 2) as b:
                step(b)
            step(B - 2)
            step(B - 1, last=True)
            step(B, tail=True)
            sp.wait_ge(x1_st, 16 * B)
            sp.wait_ge(sh_st, 32 * B)
            sp.wait_ge(filled, 64)

        @block.gpsimd
        def _(pool):
            nc.gpsimd.memset(att[:, :, :], 0.0).then_inc(tab_rd, 1)
            pool.wait_ge(ld_s, 16)
            for c in range(2):
                w = (wfc1, wpj1)[c]
                src = wstage[:, c, :].rearrange("p (k n) -> p k n", k=w[0].shape[1])
                nc.gpsimd.tensor_scalar(w[0][:, :, :], src, 1.0, 0.0, ALU.mult, ALU.add).then_inc(split_s, 1)
                pool.wait_ge(split_s, 2 * c + 1)
                nc.gpsimd.tensor_tensor(w[1][:, :, :], src, w[0][:, :, :].bitcast(F32), ALU.subtract).then_inc(split_s, 1)

            def step(b):
                pool.wait_ge(ld_r, 16 * (b + 1))
                nc.gpsimd.tensor_tensor(x_res[:, :, :], x_res[:, :, :],
                                        ln2[:, 1:2, :].to_broadcast([P, TT, D]), ALU.add).then_inc(res_rd, 1)

            pool.wait_ge(ld_c, 16 * 13)
            with pool.Fori(0, B) as b:
                step(b)
            pool.wait_ge(split_s, 4)

        @block.scalar
        def _(act):
            copy = lambda o, i: nc.scalar.activation(o, i, ACT.Copy)
            act.wait_ge(ld_c, 16 * 13)
            act.wait_ge(ld_v, 64)
            for n, (w, r) in enumerate(((wv, raw_v), (wqk, raw_qk), (wg, raw_g), (wo, raw_o))):
                copy(w[0][:], r).then_inc(wh_rd, 1)

            def x_transposed(b):
                for c in range(KD):
                    act.wait_ge(xT_mm, 2 * b + c + 1)
                    nc.scalar.activation(xT[:, c, :], bank[(7, 0)[c]][:, :], ACT.Identity, scale=vec[:, L1W + c:L1W + c + 1],
                                         bias=vec[:, L1B + c:L1B + c + 1]).then_inc(xT_ev, 1)
                for c in range(KD):
                    act.wait_ge(xT_ev, 2 * b + c + 1)
                    copy(xTh[:, c, :], xT[:, c, :]).then_inc(xTh_rd, 1)

            def step(b, first=False, last=False, tail=False):
                if not tail:
                    for t in range(TT):
                        act.wait_ge(v_mm, 4 * b + t + 1)
                        nc.scalar.activation(v[:, t, :], bank[t][:, :], ACT.Silu).then_inc(v_ev, 1)
                    for s in range(2):
                        act.wait_ge(q_mm, 2 * b + s + 1)
                        need(act, qkr_rd, 2 * (b - 1) + s + 1)
                        nc.scalar.activation(qk[:, s, :], bank[4 + s][:, :], ACT.Silu,
                                             bias=vec[:, BQK + s:BQK + s + 1]).then_inc(q_ev, 1)
                    for m in range(KE):
                        act.wait_ge(g_mm, 4 * b + m + 1)
                        nc.scalar.activation(u[:, m, :], bank[m][:, :], ACT.Silu,
                                             bias=vec[:, BG + m:BG + m + 1]).then_inc(g_ev, 1)
                    act.wait_ge(kT_mm, b + 1)
                    copy(kT[:, :, :].rearrange("p t n -> p (t n)"), bank[4][:, :]).then_inc(kT_ev, 1)
                    act.wait_ge(kv_mm, b + 1)
                    nc.scalar.activation(kv[QK:P, :], bank[6][QK:P, :], ACT.Copy, scale=1.0 / T).then_inc(kv_ev, 1)
                    if not last:
                        x_transposed(b + 1)
                    for m in range(KE):
                        act.wait_ge(u_ml, 4 * b + m + 1)
                        copy(uh[:, m, :], u[:, m, :]).then_inc(uh_rd, 1)
                if not first:
                    for c in range(KD):
                        act.wait_ge(x1T_mm, 2 * (b - 1) + c + 1)
                        need(act, x1l_rd, 2 * (b - 2) + c + 1)
                        copy(x1T[:, c, :], bank[5 + c][:, :]).then_inc(x1T_ev, 1)
                    need(act, sh_st, 32 * (b - 1))
                    for c in range(KD):
                        act.wait_ge(x1T_ev, 2 * (b - 1) + c + 1)
                        copy(x1h[:, c, :], x1T[:, c, :]).then_inc(x1h_rd, 1)
                    act.wait_ge(lg_mm, b)
                    copy(logits[:, bass.ds((b - 1) * TT, TT), :].rearrange("p t e -> p (t e)"), bank[7][:, 0:TT * NE]).then_inc(lg_ev, 1)

            x_transposed(0)
            step(0, first=True)
            step(1)
            with act.Fori(2, B - 1) as b:
                step(b)
            step(B - 1, last=True)
            step(B, tail=True)

        @block.vector
        def _(dve):
            link = Links(dve, dve_own)
            tt = nc.vector.tensor_tensor
            stt = nc.vector.scalar_tensor_tensor

            def norm(o, i, k):
                return nc.vector.tensor_scalar(o, i, mean[:, k:k + 1], rs[:, k:k + 1], ALU.subtract, ALU.mult)

            def rstd(lo, hi):
                moments(nc, link, st[:, lo:hi, :], mean[:, lo:hi], var[:, lo:hi], tmp[:, lo:hi])
                rsqrt(nc, link, rs[:, lo:hi], half[:, lo:hi], var[:, lo:hi], tmp[:, lo:hi])

            def stats(tiles, k, wait=None):
                for t, ap in enumerate(tiles):
                    if wait:
                        wait(t)
                    last = nc.vector.bn_stats(st[:, k + t, :], ap)
                link(last)

            def x_normed(b):
                need(dve, xT_mm, 2 * b)
                for t in range(TT):
                    last = norm(xn[:, t, :], x_in[:, t, :], t)
                last.then_inc(xn_ready, 1)

            def xT_rest(b):
                for c in range(KD):
                    dve.wait_ge(xTh_rd, 2 * b + c + 1)
                    tt(xTl[:, c, :], xT[:, c, :], xTh[:, c, :].bitcast(F32), ALU.subtract).then_inc(xTl_rd, 1)

            def two_rows(dst, src, n):
                link(nc.vector.tensor_copy(row_h[:, 0:n], src))
                link(tt(row_t[:, 0:n], src, row_h[:, 0:n].bitcast(F32), ALU.subtract))
                link(nc.vector.tensor_scalar(row_t[:, 0:n], row_t[:, 0:n], mask2[:, 1:2], None, ALU.mult))
                link(stt(dst, row_h[:, 0:n].bitcast(F32), mask2[:, 0:1], row_t[:, 0:n], ALU.mult, ALU.add))

            def step(b, first=False, last=False, tail=False):
                if not (last or tail):
                    dve.wait_ge(ld_x, 16 * (b + 2))
                    stats([x_in[:, t, :] for t in range(TT)], 0)
                if not tail:
                    for s in range(2):
                        dve.wait_ge(q_ev, 2 * b + s + 1)
                        last_i = tt(qkr[:, s, :], qk[:, s, :], rope[:, s, :], ALU.mult)
                        last_i.then_inc(qkr_rd, 1)
                    dve.wait_ge(qkr_rd, 2 * b + 1)
                    stt(heads[:, 0, :], qkr[:, 0, :], vec[:, GQ:GQ + 1], offs[:, 0, :], ALU.mult, ALU.add)
                    link(stt(heads[:, 1, :], qkr[:, 0, :], vec[:, GK:GK + 1], offs[:, 1, :], ALU.mult, ALU.add))
                    dve.wait_ge(qkr_rd, 2 * b + 2)
                    stt(heads[:, 1, :], qkr[:, 1, :], vec[:, GK + 1:GK + 2], heads[:, 1, :], ALU.mult, ALU.add).then_inc(heads_rd, 1)
                    stt(heads[:, 0, :], qkr[:, 1, :], vec[:, GQ + 1:GQ + 2], heads[:, 0, :], ALU.mult, ALU.add).then_inc(heads_rd, 1)
                if not first:
                    yo = [bank[6 + t // 2][:, t % 2 * D:t % 2 * D + D] for t in range(TT)]
                    stats(yo, TT, lambda t: t % 2 or dve.wait_ge(o_mm, 2 * (b - 1) + t // 2 + 1))
                if not (last and first):
                    rstd(TT if (last or tail) else 0, TT if first else 2 * TT)
                if not first:
                    for t in range(TT):
                        norm(z[:, t, :], yo[t], TT + t).then_inc(o_ev, 1)
                if not (last or tail):
                    x_normed(b + 1)
                if not first:
                    dve.wait_ge(o_ev, 4 * b)
                    link(tt(z[:, :, :], z[:, :, :], ln2[:, 0:1, :].to_broadcast([P, TT, D]), ALU.mult))
                    dve.wait_ge(res_rd, b)
                    tt(z[:, :, :], z[:, :, :], x_res[:, :, :], ALU.add).then_inc(res_used, 1)
                    dve.wait_ge(res_used, b)
                    stats([z[:, t, :] for t in range(TT)], TT)
                    rstd(TT, 2 * TT)
                    need(dve, x1_st, 16 * (b - 1))
                    for t in range(TT):
                        last_i = norm(x1[:, t, :], z[:, t, :], TT + t)
                    last_i.then_inc(x1_rd, 1)
                if not tail:
                    dve.wait_ge(sc_mm, b + 1)
                    sc = bank[5][:, :].rearrange("p (t n) -> p t n", t=TT)
                    for g in range(P // G):
                        r = slice(g * G, (g + 1) * G)
                        last_i = stt(att[r, :, r], sc[r, :, r], 1.0 / G,
                                     bias[r, :].rearrange("p (o n) -> p o n", o=1).to_broadcast([G, TT, G]), ALU.mult, ALU.add)
                    link(last_i)
                    for g in range(P // G):
                        r = slice(g * G, (g + 1) * G)
                        last_i = stt(att[r, :, r], att[r, :, r], 0.0, att[r, :, r], ALU.max, ALU.mult)
                    last_i.then_inc(att_rd, 1)
                    if not last:
                        xT_rest(b + 1)

                    def rest(m):
                        dve.wait_ge(uh_rd, 4 * b + m + 1)
                        tt(ul[:, m, :], u[:, m, :], uh[:, m, :].bitcast(F32), ALU.subtract).then_inc(ul_rd, 1)

                    for m in range(KE):
                        dve.wait_ge(u_mm, 4 * b + m + 1)
                        tt(u[:, m, :], u[:, m, :], bank[1 + m][:, :], ALU.mult).then_inc(u_ml, 1)
                        if m:
                            rest(m - 1)
                    rest(KE - 1)
                if not first:
                    for c in range(KD):
                        dve.wait_ge(x1h_rd, 2 * (b - 1) + c + 1)
                        tt(x1l[:, c, :], x1T[:, c, :], x1h[:, c, :].bitcast(F32), ALU.subtract).then_inc(x1l_rd, 1)

            dve.wait_ge(ld_x, 16)
            stats([x_in[:, t, :] for t in range(TT)], 0)
            rstd(0, TT)
            x_normed(0)
            for n, (w, r) in enumerate(((wv, raw_v), (wqk, raw_qk), (wg, raw_g), (wo, raw_o))):
                dve.wait_ge(wh_rd, n + 1)
                tt(w[1][:], r, w[0][:].bitcast(F32), ALU.subtract).then_inc(wl_rd, 1)
            dve.wait_ge(ld_c, 16 * 13)
            link(nc.vector.tensor_copy(ones2[:, :], ones_raw[:, :]))
            two_rows(bv2[:, :], rows_raw[:, 0, :], E)
            two_rows(bo2[:, :], rows_raw[:, 1, 0:D], D)
            two_rows(bpj[1][:, :], bpj_raw[1][:, :], D)
            for k, c in enumerate((BQ, BK)):
                link(nc.vector.tensor_scalar(offs[:, k, :], rope[:, 0, :], vec[:, c:c + 1], None, ALU.mult))
                link(stt(offs[:, k, :], rope[:, 1, :], vec[:, c + 1:c + 2], offs[:, k, :], ALU.mult, ALU.add))
            nc.vector.tensor_copy(tmp[:, 0:1], offs[:, 0, 0:1]).then_inc(tab_rd, 1)
            xT_rest(0)
            step(0, first=True)
            step(1)
            with dve.Fori(2, B - 1) as b:
                link.enter(b, 2, STEP_LINKS)
                step(b)
                link.leave()
            link.end(B - 3)
            step(B - 1, last=True)
            step(B, tail=True)

        @block.tensor
        def _(pe):
            mm, tr = nc.tensor.matmul, nc.tensor.transpose

            def three(o, wh, wl, xh, xl, start, stop):
                mm(o, wh, xl, start=start, stop=False)
                mm(o, wl, xh, start=False, stop=False)
                return mm(o, wh, xh, start=False, stop=stop)

            def transposes(src, banks, done):
                for c in range(KD):
                    for t in range(TT):
                        last = tr(bank[banks[c]][:, t * P:(t + 1) * P], src[:, t, c * P:(c + 1) * P], ident[:, :])
                    last.then_inc(done, 1)

            def step(b, first=False, last=False, tail=False):
                if not tail:
                    pe.wait_ge(xTh_rd, 2 * b + 2)
                    pe.wait_ge(xTl_rd, 2 * b + 2)
                    for t in range(TT):
                        if t:
                            need(pe, u_ml, 4 * (b - 1) + t)
                        cols = slice(t * P, (t + 1) * P)
                        mm(bank[t][:, :], ones2[:, :], bv2[:, :], start=True, stop=False)
                        for k in range(KD):
                            last_i = three(bank[t][:, :], xTh[:, k, cols], xTl[:, k, cols], wv[0][:, k, :], wv[1][:, k, :],
                                           False, k == KD - 1)
                        last_i.then_inc(v_mm, 1)
                    for s in range(2):
                        if s == 0:
                            need(pe, u_ml, 4 * b)
                        else:
                            need(pe, x1T_ev, 2 * (b - 2) + 1)
                        for k in range(KD):
                            last_i = three(bank[4 + s][:, :], wqk[0][:, s, k, :], wqk[1][:, s, k, :], xTh[:, k, :], xTl[:, k, :],
                                           k == 0, k == KD - 1)
                        last_i.then_inc(q_mm, 1)
                if not first:
                    pe.wait_ge(ul_rd, 4 * b)
                    for t in range(TT):
                        if t == 0:
                            need(pe, x1T_ev, 2 * (b - 1))
                        if t == 2:
                            need(pe, lg_ev, b - 1)
                        cols = slice(t * P, (t + 1) * P)
                        o = bank[6 + t // 2][:, t % 2 * D:t % 2 * D + D]
                        mm(o, ones2[:, :], bo2[:, :], start=True, stop=False)
                        for m in range(KE):
                            last_i = three(o, uh[:, m, cols], ul[:, m, cols], wo[0][:, m, :], wo[1][:, m, :], False, m == KE - 1)
                        if t % 2:
                            last_i.then_inc(o_mm, 1)
                if not tail:
                    for m in range(KE):
                        pe.wait_ge(v_ev, 4 * b + m + 1)
                        rows = slice(m * P, (m + 1) * P)
                        for k in range(KD):
                            last_i = three(bank[m][:, :], wg[0][:, k, rows], wg[1][:, k, rows], xTh[:, k, :], xTl[:, k, :],
                                           k == 0, k == KD - 1)
                        last_i.then_inc(g_mm, 1)
                    pe.wait_ge(heads_rd, 2 * b + 1)
                    for t in range(TT):
                        last_i = tr(bank[4][:, t * P:(t + 1) * P], heads[:, 1, t * P:(t + 1) * P], ident[:, :])
                    last_i.then_inc(kT_mm, 1)
                    pe.wait_ge(heads_rd, 2 * b + 2)
                    for t in range(TT):
                        cols = slice(t * P, (t + 1) * P)
                        last_i = mm(bank[5][:, cols], heads[0:QK, 1, cols], heads[0:QK, 0, cols], start=True, stop=True)
                    last_i.then_inc(sc_mm, 1)
                    pe.wait_ge(kT_ev, b + 1)
                    need(pe, o_ev, 4 * (b - 1) + 2)
                    for t in range(TT):
                        last_i = mm(bank[6][:, :], kT[:, t, :], v[:, t, :], start=t == 0, stop=t == TT - 1)
                    last_i.then_inc(kv_mm, 1)
                    if not last:
                        pe.wait_ge(xn_ready, b + 2)
                        need(pe, o_ev, 4 * b)
                        pe.wait_ge(g_ev, 4 * b + 1)
                        transposes(xn, (7, 0), xT_mm)
                    pe.wait_ge(att_rd, b + 1)
                    pe.wait_ge(kv_ev, b + 1)
                    for m in range(KE):
                        if m < 3:
                            pe.wait_ge(g_ev, 4 * b + m + 2)
                        rows = slice(m * P, (m + 1) * P)
                        o = bank[1 + m]
                        mm(o[:, :], kv[QK:P, rows], heads[QK:P, 0, :], start=True, stop=False)
                        for t in range(TT):
                            cols = slice(t * P, (t + 1) * P)
                            last_i = mm(o[:, cols], v[:, t, rows], att[:, t, :], start=False, stop=t == TT - 1)
                        last_i.then_inc(u_mm, 1)
                if not first:
                    pe.wait_ge(x1_rd, b)
                    transposes(x1, (5, 6), x1T_mm)
                    pe.wait_ge(x1T_ev, 2 * b)
                    if not (last or tail):
                        pe.wait_ge(xT_ev, 2 * (b + 1) + 1)
                    for t in range(TT):
                        for c in range(KD):
                            last_i = mm(bank[7][:, t * NE:(t + 1) * NE], x1T[:, c, t * P:(t + 1) * P], wr[:, c, :],
                                        start=c == 0, stop=c == KD - 1)
                    last_i.then_inc(lg_mm, 1)

            pe.wait_ge(ld_c, 16 * 13)
            pe.wait_ge(xn_ready, 1)
            transposes(xn, (7, 0), xT_mm)
            pe.wait_ge(tab_rd, 2)
            pe.wait_ge(wl_rd, 4)
            step(0, first=True)
            step(1)
            with pe.Fori(2, B - 1) as b:
                step(b)
            step(B - 1, last=True)
            step(B, tail=True)


STEP_LINKS = 34
BLOCK_LINKS = 11


def experts(nc, a, out, shared):
    ident, ones2, mask2, logits = (shared[k] for k in ("ident", "ones2", "mask2", "logits"))
    wstage, wfc1, wpj1, bfc, bpj_raw, bpj = (shared[k] for k in ("wstage", "wfc1", "wpj1", "bfc", "bpj_raw", "bpj"))
    row_t, row_h = shared["row_t"], shared["row_h"]
    XHL, X1D, XS, YY = (shared[k] for k in ("XHL", "X1D", "XS", "YY"))
    with ExitStack() as ctx:
        sb = lambda n, s, t=F32: ctx.enter_context(nc.sbuf_tensor("s_" + n, s, t))
        sem = lambda n: ctx.enter_context(nc.semaphore(n))

        wfc = [[sb(f"wfc0{p}", [P, KD, HID], F32R) for p in "hl"], wfc1]
        wpj = [[sb(f"wpj0{p}", [P, KH, D], F32R) for p in "hl"], wpj1]
        rows = sb("rows", [P, NT, ROW])
        acc = sb("acc", [P, NT, D])
        xh = [sb(f"blk_xh{i}", [P, KD, S], F32R) for i in range(2)]
        xl = [sb(f"blk_xl{i}", [P, KD, S], F32R) for i in range(2)]
        xb = sb("xb", [P, ST, ROW])
        RING = 4
        h = [sb(f"h{i}", [P, S]) for i in range(2)]
        hh = [sb(f"hh{i}", [P, S], F32R) for i in range(RING)]
        hl = [sb(f"hl{i}", [P, S], F32R) for i in range(RING)]
        y = sb("y", [P, ST, D])
        dest = [sb(f"dest{i}", [P, ST], I32) for i in range(2)]
        gate = [sb(f"gate{i}", [P, ST]) for i in range(2)]
        rt = [y[:, i, :].rearrange("p (e t) -> p e t", e=NE) for i in range(4)]
        choice = [xb[:, i, 0:NE * NT].rearrange("p (e t) -> p e t", e=NE) for i in range(2)]
        both = sb("both", [P, NE * NT], BF16)
        cnt = sb("cnt", [P, 8, NT])
        small = sb("small", [P, ROUTED, NE])
        nblk, start = sb("nblk", [P, NE]), sb("start", [P, NE])
        pos = [sb(f"pos{i}", [P, NT], I32) for i in range(2)]
        owner_f = sb("owner_f", [P, ROUTED])
        owner = sb("owner", [P, ROUTED], I32)
        cst = sb("cst", [P, a["route"].shape[1]])
        tri = sb("tri", [P, 2, P])
        trib = sb("trib", [P, 2, P], BF16)
        st = sb("mst", [P, NT, 6])
        mean = sb("mmean", [P, NT])
        var, rs, tmp = sb("mvar", [P, NT]), sb("mrs", [P, NT]), sb("mtmp", [P, NT])
        half = sb("mhalf", [P, NT], I32)

        fcb = [ctx.enter_context(nc.psum_tensor(f"fc_bank{i}", [P, 512], F32)) for i in range(4)]
        yb = [[ctx.enter_context(nc.psum_tensor(f"y_bank{i}{k}", [P, 512], F32)) for k in range(2)] for i in range(2)]

        ld_c, ld_rows, ld_xT = sem("route_consts_loaded"), sem("rows_loaded"), [sem(f"parts_loaded{i}") for i in range(2)]
        ld_w = [sem(f"expert_{n}_loaded") for n in ("fc", "pj")]
        ld_b, ld_xb, ld_y = [sem(f"expert_biases_loaded{i}") for i in range(2)], sem("slots_loaded"), [sem(f"results_loaded{i}") for i in range(2)]
        w_rd, bpj_rd = [sem(f"expert_{n}_split") for n in ("fc", "pj")], sem("expert_bias_split")
        fc_mm, h_ev, hh_rd, hl_rd, pj_mm = (sem(n) for n in ("fc_product", "h_ready", "hh_ready", "hl_ready", "proj_product"))
        t_mm, xh_rd, xl_rd = sem("slots_transposed"), sem("slots_hi_ready"), sem("slots_lo_ready")
        y_ev, y_out = sem("y_evacuated"), sem("results_scattered")
        cum_rd, tri_rd, st_rd = sem("counts_read"), sem("masks_ready"), sem("statistics_ready")
        meta_rd = sem("slots_meta_ready")
        acc_rd = sem("acc_ready")
        e_rd, both_rd, cum_mm, own_rd = sem("exp_ready"), sem("choices_ready"), sem("counts_product"), sem("owners_ready")
        d_rd, rows_rd = sem("logits_shifted"), sem("rows_ready")
        sent = [sem(f"rows_sent{i}") for i in range(2)]
        dve_own = sem("vector_own2")
        tot_rd, o_rd, o_out = sem("totals_ready"), sem("out_ready"), sem("out_stored")
        yy_rd = sem("pairs_summed")

        block = ctx.enter_context(nc.Block())
        x1_view = X1D.rearrange("(t p) d -> p t d", p=P)
        xs_view = XS.rearrange("(r t p) w -> r p t w", t=ST, p=P)
        yy_view = YY.rearrange("(k t p) d -> k p t d", k=2, p=P)
        out_view = out.rearrange("(b t p) d -> b p t d", b=B, p=P)

        PLAIN = [("fc", j) for j in range(KH)]
        WITH_T = PLAIN[0:3] + [("T", 0)] + PLAIN[3:5] + [("T", 1)] + PLAIN[5:8]

        def par(n, routed):
            return n % 2 if not routed else n % 2

        def order(blocks_fn, engine):
            blocks_fn(0, 0, PLAIN, 0)
            blocks_fn(1, 1, PLAIN, 0)
            with engine.Fori(0, SHARED // 2 - 2) as m:
                for i in range(2):
                    blocks_fn(m * 2 + 2 + i, i, PLAIN, 0)
            blocks_fn(SHARED - 2, 0, PLAIN, 0)
            blocks_fn(SHARED - 1, 1, WITH_T, 0, r_next=0)
            blocks_fn(SHARED, 0, WITH_T, 2, r=0, r_next=1)
            blocks_fn(SHARED + 1, 1, WITH_T, 0, r=1, r_next=2)
            with engine.Fori(0, ROUTED // 2 - 1) as m:
                for i in range(2):
                    r = m * 2 + 2 + i
                    blocks_fn(r + SHARED, i, WITH_T, 2 * (1 - i), r=r, r_next=r + 1)
            r = ROUTED - 1
            blocks_fn(r + SHARED, 0, PLAIN, 2, r=r)

        @block.sync
        def _(sp):
            def parts(n, i):
                src = XHL[bass.ds(n, 1)].rearrange("b p (q n) -> (b p) q n", q=2)
                for q, dst in enumerate((xh, xl)):
                    sp.dma_start(dst[i][:, :, :].bitcast(F32).rearrange("p k n -> p (k n)"), src[:, q, :]).then_inc(ld_xT[i], 16)

            parts(0, 0)
            sp.dma_start(cst[:, :], a["route"]).then_inc(ld_c, 16)
            sp.dma_start(tri[:, :, :], a["tri"]).then_inc(ld_c, 16)
            parts(1, 1)
            sp.dma_start(rows[:, :, 0:D], x1_view).then_inc(ld_rows, 16)
            with sp.Fori(1, SHARED // 2) as m:
                for i in range(2):
                    sp.wait_ge(fc_mm, (m * 2 + i - 1) * KH)
                    parts(m * 2 + i, i)
            sp.wait_ge(own_rd, 1)

            def expert(r, i):
                e = sp.value_load(owner[0:1, bass.ds(r, 1)], min_val=0, max_val=NE - 1)
                w = a["wall"][bass.ds(e, 1)].rearrange("e p a n -> (e p) a n")
                for c in range(2):
                    need(sp, w_rd[c], r * 4)
                    sp.dma_start(wstage[:, c, :], w[:, c, :]).then_inc(ld_w[c], 16)
                    if c == 0:
                        if isinstance(r, int) and r == 0:
                            for k in range(2):
                                sp.wait_ge(sent[k], 16 * NT)
                        need(sp, t_mm, r * 2)
                        need(sp, meta_rd, r)
                        sp.dma_start(xb[:, :, :], xs_view[bass.ds(r, 1)].rearrange("r p t w -> (r p) t w")).then_inc(ld_xb, 16)
                sp.wait_ge(h_ev, (r + SHARED - 1) * KH)
                sp.dma_start(bfc[i][:, :], a["bfc"][bass.ds(e, 1)].rearrange("e p n -> (e p) n")).then_inc(ld_b[i], 16)
                sp.dma_start(bpj_raw[i][:, :], a["bproj"][bass.ds(e, 1)].rearrange("e p n -> (e p) n")).then_inc(ld_b[i], 16)

            expert(0, 0)
            expert(1, 1)
            with sp.Fori(0, ROUTED // 2 - 1) as m:
                for i in range(2):
                    expert(m * 2 + 2 + i, i)
            expert(ROUTED - 1, 0)

            sp.wait_ge(y_out, 16 * ST * ROUTED)

            def results(b, i):
                for k in range(2):
                    src = yy_view[k].rearrange("p (b t) d -> b p t d", t=TT)[bass.ds(b, 1)].rearrange("b p t d -> (b p) t d")
                    sp.dma_start(wstage[:, i, k * TT * D:(k + 1) * TT * D].rearrange("p (t d) -> p t d", t=TT), src).then_inc(ld_y[i], 16)

            results(0, 0)
            results(1, 1)
            with sp.Fori(1, B // 2) as m:
                for i in range(2):
                    sp.wait_ge(tot_rd, m * 2 + i - 1)
                    results(m * 2 + i, i)
            with sp.Fori(0, B) as b:
                sp.wait_ge(o_rd, (b + 1) * TT)
                sp.dma_start(out_view[bass.ds(b, 1)].rearrange("b p t d -> (b p) t d"),
                             acc[:, bass.ds(b * TT, TT), :]).then_inc(o_out, 16)
            sp.wait_ge(o_out, 16 * B)

        @block.gpsimd
        def _(pool):
            for k in range(2):
                if k == 0:
                    pool.wait_ge(own_rd, 1)
                    pool.wait_ge(ld_rows, 16)
                else:
                    pool.wait_ge(sent[0], 16 * NT)
                nc.gpsimd.tensor_scalar(rows[:, :, D], cst[:, TOK:TOK + NT], 1.0, float(k * N), ALU.mult, ALU.add)
                nc.gpsimd.tensor_scalar(rows[:, :, D + 1], cnt[:, 4 + k, :], 1.0, 0.0, ALU.mult, ALU.add).then_inc(rows_rd, 1)
                pool.wait_ge(rows_rd, k + 1)
                for t in range(NT):
                    pool.indirect_dma_start(XS, bass.IndirectOffsetOnAxis(pos[k][:, t:t + 1].bitcast(U32), 0),
                                            rows[:, t, :], None).then_inc(sent[k], 16)

            def scatter(r, i):
                for t in range(ST):
                    pool.wait_ge(y_ev, r * ST + t + 1)
                    pool.indirect_dma_start(YY, bass.IndirectOffsetOnAxis(dest[i][:, t:t + 1].bitcast(U32), 0), y[:, t, :], None,
                                            bounds_check=2 * N - 1, oob_is_err=False).then_inc(y_out, 16)

            for r in range(ROUTED):
                scatter(r, r % 2)

            with pool.Fori(0, B // 2) as m:
                for i in range(2):
                    pool.wait_ge(ld_y[i], m * 32 + 32)
                    nc.gpsimd.tensor_tensor(wstage[:, i, 0:TT * D], wstage[:, i, 0:TT * D], wstage[:, i, TT * D:], ALU.add).then_inc(yy_rd, 1)

        @block.scalar
        def _(act):
            def y_results(r, i):
                act.wait_ge(pj_mm, (r + SHARED + 1) * KH)
                act.wait_ge(meta_rd, r + 1)
                need(act, y_out, r * 16 * ST)
                for t in range(ST):
                    nc.scalar.activation(y[:, t, :], yb[i][t // 2][:, t % 2 * D:t % 2 * D + D], ACT.Copy,
                                         scale=gate[i][:, t:t + 1]).then_inc(y_ev, 1)

            def tokens(n, i, plan, bank0, r=None, r_next=None):
                for k, (kind, j) in enumerate(plan):
                    b = fcb[(bank0 + k) % 4]
                    if kind == "T":
                        act.wait_ge(t_mm, r_next * 2 + j + 1)
                        nc.scalar.activation(xh[1 - i][:, j, :], b[:, :], ACT.Copy).then_inc(xh_rd, 1)
                        continue
                    if j == 0 and r is not None:
                        act.wait_ge(ld_b[i], (r - i) * 16 + 32)
                    act.wait_ge(fc_mm, n * KH + j + 1)
                    need(act, hl_rd, n * KH + j - 1)
                    nc.scalar.activation(h[j % 2][:, :], b[:, :], ACT.Gelu_apprx_tanh,
                                         bias=bfc[1 if r is None else i][:, j:j + 1]).then_inc(h_ev, 1)
                    act.wait_ge(h_ev, n * KH + j + 1)
                    need(act, pj_mm, n * KH + j + 1 - RING)
                    nc.scalar.activation(hh[j % RING][:, :], h[j % 2][:, :], ACT.Copy).then_inc(hh_rd, 1)
                    if n is not None and isinstance(n, int) and n == 0 and j == 0:
                        act.wait_ge(d_rd, 1)
                        nc.scalar.activation(rt[1][:, :, :], rt[0][:, :, :], ACT.Exp).then_inc(e_rd, 1)
                    if j == 2 and r is not None and not (isinstance(r, int) and r == 0):
                        y_results(r - 1, 1 - i)

            order(tokens, act)
            y_results(ROUTED - 1, 0)

        @block.vector
        def _(dve):
            link = Links(dve, dve_own)
            tt, ts, stt, red = nc.vector.tensor_tensor, nc.vector.tensor_scalar, nc.vector.scalar_tensor_tensor, nc.vector.tensor_reduce
            per_expert = lambda ap: ap.rearrange("p (e t) -> p e t", e=1).to_broadcast([P, NE, NT])
            per_token = lambda ap: ap.rearrange("p (e t) -> p e t", t=1).to_broadcast([P, NE, NT])
            over_experts = lambda ap: ap.rearrange("p e t -> p t e")

            def shifted_logits():
                link(red(cnt[:, 0, :], logits[:, :, :], AX, ALU.max))
                tt(rt[0][:, :, :], logits[:, :, :].rearrange("p t e -> p e t"), per_expert(cnt[:, 0, :]), ALU.subtract).then_inc(d_rd, 1)

            def probabilities():
                dve.wait_ge(e_rd, 1)
                link(red(cnt[:, 1, :], over_experts(rt[1][:, :, :]), AX, ALU.add))
                link(nc.vector.reciprocal(cnt[:, 1, :], cnt[:, 1, :]))
                link(tt(rt[0][:, :, :], rt[1][:, :, :], per_expert(cnt[:, 1, :]), ALU.mult))

            def choose(k):
                link(red(cnt[:, 2 + k, :], over_experts(rt[0][:, :, :]), AX, ALU.max))
                link(tt(rt[2][:, :, :], rt[0][:, :, :], per_expert(cnt[:, 2 + k, :]), ALU.is_equal))
                link(tt(rt[2][:, :, :], rt[2][:, :, :], per_token(cst[:, KEY:KEY + NE]), ALU.mult))
                link(red(cnt[:, 6, :], over_experts(rt[2][:, :, :]), AX, ALU.max))
                link(tt(choice[k][:, :, :], rt[2][:, :, :], per_expert(cnt[:, 6, :]), ALU.is_equal))
                if k == 0:
                    link(stt(rt[0][:, :, :], choice[0][:, :, :], -2.0, rt[0][:, :, :], ALU.mult, ALU.add))

            def gates():
                tt(both[:, :], choice[0][:, :, :].rearrange("p e t -> p (e t)"), choice[1][:, :, :].rearrange("p e t -> p (e t)"),
                   ALU.add).then_inc(both_rd, 1)
                link(tt(cnt[:, 7, :], cnt[:, 2, :], cnt[:, 3, :], ALU.add))
                link(nc.vector.reciprocal(cnt[:, 7, :], cnt[:, 7, :]))
                for k in range(2):
                    last = tt(cnt[:, 4 + k, :], cnt[:, 2 + k, :], cnt[:, 7, :], ALU.mult)
                link(last)

            def counts():
                dve.wait_ge(cum_mm, 1)
                c = yb[1][0]
                nc.vector.tensor_copy(rt[3][:, :, :].rearrange("p e t -> p (e t)"), c[:, 0:NE * NT])
                link(nc.vector.tensor_copy(rt[1][:, :, :].rearrange("p e t -> p (e t)"), c[:, NE * NT:]))
                nc.vector.tensor_copy(cnt[:, 6, 0:1], rt[1][:, 0, 0:1]).then_inc(cum_rd, 1)
                link(nc.vector.tensor_tensor_scan(rt[2][:, :, :].rearrange("p e t -> p (e t)"), cst[:, GO_ON:GO_ON + NE * NT],
                                                  rt[1][:, :, :].rearrange("p e t -> p (e t)"), 0.0, ALU.mult, ALU.add))

            def starts():
                total = rt[2][:, :, NT - 1]
                link(tt(small[:, 0:NE, :], total.rearrange("p (e k) -> p e k", k=1).to_broadcast([P, NE, NE]),
                        cst[:, FULL:FULL + NE].rearrange("p (e k) -> p e k", e=1).to_broadcast([P, NE, NE]), ALU.is_gt))
                link(red(nblk[:, :], small[:, 0:NE, :], AX, ALU.add))
                link(tt(small[:, 0:NE, :], nblk[:, :].rearrange("p (e k) -> p e k", e=1).to_broadcast([P, NE, NE]),
                        cst[:, BEFORE:BEFORE + NE * NE].rearrange("p (e k) -> p e k", k=NE), ALU.mult))
                link(red(start[:, :], small[:, 0:NE, :], AX, ALU.add))

            def slots():
                link(tt(rt[2][:, :, :], rt[2][:, :, :], rt[1][:, :, :], ALU.subtract))
                link(tt(rt[2][:, :, :], rt[2][:, :, :], rt[3][:, :, :], ALU.add))
                link(stt(rt[2][:, :, :], per_token(start[:, :]), float(S), rt[2][:, :, :], ALU.mult, ALU.add))
                for k in range(2):
                    link(tt(rt[k][:, :, :], choice[k][:, :, :], rt[2][:, :, :], ALU.mult))
                for k in range(2):
                    last = red(cnt[:, 6 + k, :], over_experts(rt[k][:, :, :]), AX, ALU.add)
                link(last)
                for k in range(2):
                    last = nc.vector.tensor_copy(pos[k][:, :], cnt[:, 6 + k, :])
                link(last)

            def owners():
                link(tt(small[:, :, :], cst[:, BLOCK:BLOCK + ROUTED].rearrange("p (r k) -> p r k", k=1).to_broadcast([P, ROUTED, NE]),
                        start[:, :].rearrange("p (r k) -> p r k", r=1).to_broadcast([P, ROUTED, NE]), ALU.is_ge))
                link(red(owner_f[:, :], small[:, :, :], AX, ALU.add))
                ts(owner[:, :], owner_f[:, :], -1.0, None, ALU.add).then_inc(own_rd, 1)

            def split_piece(r, i, piece):
                c, q = piece // 4, piece % 4
                n = KD * HID // 4
                if q == 0:
                    dve.wait_ge(ld_w[c], r * 16 + 16)
                    dve.wait_ge((fc_mm, pj_mm)[c], (r + SHARED - 1) * KH)
                w = [p[:].rearrange("p k n -> p (k n)")[:, q * n:(q + 1) * n] for p in (wfc, wpj)[c][i]]
                src = wstage[:, c, q * n:(q + 1) * n]
                link(nc.vector.tensor_copy(w[0], src))
                tt(w[1], src, w[0].bitcast(F32), ALU.subtract).then_inc(w_rd[c], 1)

            def slots_meta(r, i):
                dve.wait_ge(ld_xb, r * 16 + 16)
                need(dve, y_out, (r - 1) * 16 * ST)
                nc.vector.tensor_copy(dest[i][:, :], xb[:, :, D])
                nc.vector.tensor_copy(gate[i][:, :], xb[:, :, D + 1]).then_inc(meta_rd, 1)
                dve.wait_ge(ld_b[i], (r - i) * 16 + 32)
                link(nc.vector.tensor_copy(row_h[:, 0:D], bpj_raw[i][:, :]))
                link(tt(row_t[:, 0:D], bpj_raw[i][:, :], row_h[:, 0:D].bitcast(F32), ALU.subtract))
                link(ts(row_t[:, 0:D], row_t[:, 0:D], mask2[:, 1:2], None, ALU.mult))
                stt(bpj[i][:, :], row_h[:, 0:D].bitcast(F32), mask2[:, 0:1], row_t[:, 0:D], ALU.mult, ALU.add).then_inc(bpj_rd, 1)

            beside = {(0, 0): lambda: (shifted_logits(), probabilities()), (0, 1): lambda: choose(0),
                      (0, 2): lambda: choose(1), (0, 3): gates,
                      (1, 0): counts, (1, 2): starts, (1, 3): slots, (1, 4): owners}

            def tokens(n, i, plan, bank0, r=None, r_next=None):
                for k, (kind, j) in enumerate(plan):
                    if kind == "T":
                        dve.wait_ge(xh_rd, r_next * 2 + j + 1)
                        tt(xl[1 - i][:, j, :], fcb[(bank0 + k) % 4][:, :], xh[1 - i][:, j, :].bitcast(F32), ALU.subtract).then_inc(xl_rd, 1)
                        continue
                    dve.wait_ge(hh_rd, n * KH + j + 1)
                    tt(hl[j % RING][:, :], h[j % 2][:, :], hh[j % RING][:, :].bitcast(F32), ALU.subtract).then_inc(hl_rd, 1)
                    if isinstance(n, int) and (n, j) in beside:
                        beside[n, j]()
                    if j == 2 and (r is None or (isinstance(r, int) and r == 0)) and not (isinstance(n, int) and n == 0):
                        dve.wait_ge(pj_mm, n * KH)
                        if isinstance(n, int) and n == 1:
                            dve.wait_ge(ld_rows, 16)
                        for t in range(ST):
                            tok = bass.ds((n - 1) * ST + t, 1)
                            tt(acc[:, tok, :].rearrange("p o d -> p (o d)"), yb[1 - i][t // 2][:, t % 2 * D:t % 2 * D + D],
                               rows[:, tok, 0:D].rearrange("p o d -> p (o d)"), ALU.add).then_inc(acc_rd, 1)
                    if r_next is not None:
                        split_piece(r_next, 1 - i, j)
                if r_next is not None:
                    slots_meta(r_next, 1 - i)

            dve.wait_ge(ld_c, 32)
            nc.vector.tensor_copy(trib[:, :, :], tri[:, :, :]).then_inc(tri_rd, 1)

            def counted(n, *args, **kw):
                if isinstance(n, int):
                    if link.loop:
                        link.end(SHARED - 4 if n < SHARED else ROUTED - 3)
                    tokens(n, *args, **kw)
                else:
                    link.enter(n, *((2, 0) if kw.get("r") is None else (SHARED + 2, BLOCK_LINKS)))
                    tokens(n, *args, **kw)
                    link.leave()

            order(counted, dve)

            def total(b, i):
                dve.wait_ge(yy_rd, b + 1)
                dst = acc[:, bass.ds(b * TT, TT), :].rearrange("p t d -> p (t d)")
                tt(dst, dst, wstage[:, i, 0:TT * D], ALU.add).then_inc(tot_rd, 1)
                dve.wait_ge(tot_rd, b + 1)
                for t in range(TT):
                    at = bass.ds(b * TT + t, 1)
                    last = nc.vector.bn_stats(st[:, at, :].rearrange("p o d -> p (o d)"), acc[:, at, :].rearrange("p o d -> p (o d)"))
                last.then_inc(st_rd, 1)

            with dve.Fori(0, B // 2) as m:
                for i in range(2):
                    total(m * 2 + i, i)
            dve.wait_ge(st_rd, B)
            moments(nc, link, st[:, :, :], mean[:, :], var[:, :], tmp[:, :])
            rsqrt(nc, link, rs[:, :], half[:, :], var[:, :], tmp[:, :])
            with dve.Fori(0, NT) as t:
                at = bass.ds(t, 1)
                row = acc[:, at, :].rearrange("p o d -> p (o d)")
                ts(row, row, mean[:, at], rs[:, at], ALU.subtract, ALU.mult).then_inc(o_rd, 1)

        @block.tensor
        def _(pe):
            mm = nc.tensor.matmul

            def project(n, i, j, r):
                w = 1 if r is None else i
                pe.wait_ge(hl_rd, n * KH + j + 1)
                if j == 0:
                    if r is not None:
                        pe.wait_ge(bpj_rd, r + 1)
                        pe.wait_ge(w_rd[1], (r + 1) * 4)
                    if r is None or (isinstance(r, int) and r < 2):
                        need(pe, acc_rd, (n - 1) * ST)
                    else:
                        pe.wait_ge(y_ev, (r - 1) * ST)
                    if isinstance(n, int) and n == 1:
                        pe.wait_ge(cum_rd, 1)
                for t in range(ST):
                    o = yb[i][t // 2][:, t % 2 * D:t % 2 * D + D]
                    cols = slice(t * P, (t + 1) * P)
                    if j == 0:
                        mm(o, ones2[:, :], bpj[w][:, :], start=t % 2 == 0, stop=False, skip_group_check=True)
                    hs = (hh[j % RING], hl[j % RING], hh[j % RING])
                    for p, ws in enumerate((1, 0, 0)):
                        last = mm(o, hs[p][:, cols], wpj[w][ws][:, j, :], start=False,
                                  stop=j == KH - 1 and p == 2, skip_group_check=True)
                last.then_inc(pj_mm, 1)

            def tokens(n, i, plan, bank0, r=None, r_next=None):
                w = 1 if r is None else i
                first = isinstance(n, int) and n == 0
                before = PLAIN if r is None else WITH_T
                for k, (kind, j) in enumerate(plan):
                    if k >= 4:
                        okind, oj = plan[k - 4]
                        if okind == "fc":
                            pe.wait_ge(h_ev, n * KH + oj + 1)
                        else:
                            pe.wait_ge(xl_rd, r_next * 2 + oj + 1)
                    elif not first:
                        okind, oj = before[k - 4]
                        if okind == "fc":
                            pe.wait_ge(h_ev, (n - 1) * KH + oj + 1)
                        else:
                            pe.wait_ge(xl_rd, r * 2 + oj + 1)
                    b = fcb[(bank0 + k) % 4]
                    if kind == "T":
                        if j == 0:
                            pe.wait_ge(ld_xb, r_next * 16 + 16)
                        for t in range(ST):
                            last = nc.tensor.transpose(b[:, t * P:(t + 1) * P], xb[:, t, j * P:(j + 1) * P], ident[:, :])
                        last.then_inc(t_mm, 1)
                        continue
                    if j == 0:
                        if r is None:
                            pe.wait_ge(ld_xT[i], (n - i) * 16 + 32)
                        else:
                            pe.wait_ge(xl_rd, r * 2 + 2)
                            pe.wait_ge(w_rd[0], (r + 1) * 4)
                    rows_ = slice(j * P, (j + 1) * P)
                    for c in range(KD):
                        for p, (ws, xs) in enumerate(((0, xl), (1, xh), (0, xh))):
                            last = mm(b[:, :], wfc[w][ws][:, c, rows_], xs[i][:, c, :], start=c == 0 and p == 0,
                                      stop=c == KD - 1 and p == 2)
                    last.then_inc(fc_mm, 1)
                    if j >= 2:
                        project(n, i, j - 2, r)
                    elif not first:
                        if r is None:
                            project(n - 1, 1 - i, KH - 2 + j, None)
                        else:
                            project(n - 1, 1 - i, KH - 2 + j, None if isinstance(r, int) and r == 0 else r - 1)
                if first:
                    pe.wait_ge(both_rd, 1)
                    pe.wait_ge(tri_rd, 1)
                    c = yb[1][0]
                    mm(c[:, 0:NE * NT], trib[:, 0, :], both[:, :], start=True, stop=True)
                    mm(c[:, NE * NT:], trib[:, 1, :], both[:, :], start=True, stop=True).then_inc(cum_mm, 1)

            order(tokens, pe)
            for j in (KH - 2, KH - 1):
                project(SHARED + ROUTED - 1, 0, j, ROUTED - 1)


KEY = 0
FULL = KEY + NE
BEFORE = FULL + NE
BLOCK = BEFORE + NE * NE
TOK = BLOCK + ROUTED
GO_ON = TOK + NT


def constants():
    route = np.zeros((P, GO_ON + NE * NT), np.float32)
    route[:, KEY:KEY + NE] = NE - np.arange(NE)
    route[:, FULL:FULL + NE] = S * np.arange(NE)
    route[:, BEFORE:BEFORE + NE * NE] = np.tril(np.ones((NE, NE)), -1).reshape(-1)
    route[:, BLOCK:BLOCK + ROUTED] = np.arange(ROUTED)
    route[:, TOK:TOK + NT] = np.arange(P)[:, None] + P * np.arange(NT)
    route[:, GO_ON:] = (np.arange(NE * NT) % NT != 0)
    tri = np.stack([np.triu(np.ones((P, P)), 1), np.ones((P, P))], 1).astype(np.float32)
    half = QK // 2
    freq = np.float32(10000.0) ** (-np.arange(half, dtype=np.float32) / np.float32(half))
    angle = (np.arange(T, dtype=np.float32)[:, None] * freq[None, :]).T.astype(np.float64)
    cos, sin = np.cos(angle), np.sin(angle)
    rope = np.stack([np.concatenate([cos] * 4), np.concatenate([-sin, sin] * 2)], 1).astype(np.float32)
    empty = np.zeros((P, ROW), np.float32)
    empty[:, D] = NOWHERE
    return {"route": route, "tri": tri, "rope": rope, "empty": empty, "ident": np.eye(P, dtype=np.float32),
            "ones": np.ones((2, P), np.float32), "mask2": np.eye(2, dtype=np.float32)}


def layout(i):
    f = {k: np.asarray(v) for k, v in i.items()}
    A, F = "L0_attn_", "L0_ffn_"
    halves = lambda x: np.concatenate([x[..., QK // 2:], x[..., :QK // 2]], -1)
    twice = lambda x, y: np.stack([np.concatenate([x, y]), np.concatenate([halves(x), halves(y)])], 1)
    chunks = lambda x: x.reshape(-1, P, x.shape[-1]).transpose(1, 0, 2)
    g, be, bqk = f[A + "gamma"], f[A + "beta"], f[A + "bqk"]
    vec = np.concatenate([twice(bqk, bqk), twice(g[0], g[1]), twice(g[2], g[3]), twice(be[0], be[1]), twice(be[2], be[3]),
                          f[A + "ln1_w"].reshape(KD, P).T, f[A + "ln1_b"].reshape(KD, P).T, f[A + "bg"].reshape(KE, P).T], 1)
    wqk = f[A + "Wqk"].T
    wqk = np.stack([chunks(np.concatenate([w, w], 1)) for w in (wqk, halves(wqk))], 1)
    rows = np.zeros((2, 2, E), np.float32)
    rows[:, 0, :] = f[A + "bv"]
    rows[:, 1, 0:D] = f[A + "bo"]
    pe = f[A + "pos_emb"]
    far = np.repeat(pe[MAX_REL:MAX_REL + 1], G - 1 - MAX_REL)
    ext = np.concatenate([far, pe[MAX_REL:0:-1], pe[0:MAX_REL + 1], far])
    wall = np.stack([np.stack([chunks(a).reshape(P, -1), chunks(b).reshape(P, -1)], 1)
                     for a, b in [*zip(f[F + "Wfc"], f[F + "Wproj"]), (f[F + "Wfc_s"], f[F + "Wproj_s"])]])
    bfc = np.concatenate([f[F + "bfc"], f[F + "bfc_s"][None]]).reshape(NE + 1, KH, P).transpose(0, 2, 1)
    bproj = np.repeat(np.concatenate([f[F + "bproj"], f[F + "bproj_s"][None]])[:, None, :], 2, 1)
    return {"x": f[A + "x"].reshape(N, D), "vec": vec, "wqk": wqk, "wv": chunks(f[A + "Wv"].T), "wg": chunks(f[A + "Wg"].T),
            "wo": chunks(f[A + "Wo"].T), "rows": rows, "ext": np.tile(ext, G),
            "ln2": np.repeat(np.stack([f[A + "ln2_w"], f[A + "ln2_b"]])[None], P, 0), "wr": chunks(f[F + "Wr"]),
            "wall": wall, "bfc": bfc, "bproj": bproj}


def kernel(**inputs):
    import concourse.bacc as bacc
    from concourse.bass_utils import run_bass_kernel_spmd

    nc = bacc.Bacc("TRN2", target_bir_lowering=False, num_devices=1)
    arrays = {k: np.ascontiguousarray(v) for k, v in {**layout(inputs), **constants()}.items()}
    aps = {k: nc.dram_tensor(k, v.shape, mybir.dt.from_np(v.dtype), kind="ExternalInput").ap() for k, v in arrays.items()}
    out = nc.dram_tensor("out", (N, D), F32, kind="ExternalOutput").ap()
    build(nc, aps, out)
    r = run_bass_kernel_spmd(nc, [arrays], core_ids=[0])
    return r.results[0]["out"].reshape(B, T, D)
```

```python
from contextlib import ExitStack

import numpy as np

import concourse.bass as bass
from concourse import mybir

F32 = mybir.dt.float32
F32R = mybir.dt.float32r
BF16 = mybir.dt.bfloat16
I32 = mybir.dt.int32
U32 = mybir.dt.uint32
ALU = mybir.AluOpType
ACT = mybir.ActivationFunctionType
AX = mybir.AxisListType.X

P = 128
B, T, D = 8, 512, 256
N = B * T
QK = 64
E = 512
G = 64
MAX_REL = 32
HID = 1024
NE = 8
KD = D // P
KE = E // P
KH = HID // P
TT = T // P
NT = N // P
S = 512
ST = S // P
HS = S // 2
HT = HS // P
SHARED = N // S
UNITS = (2 * N - NE) // HS + NE
BIG = (UNITS - NE) // 2
SMALL = UNITS - 2 * BIG
ROUTED = BIG + SMALL
SLOTS = UNITS * HS
ROW = D + 2
NOWHERE = float(4 * N)
EPS = 1e-5
RSQRT_SEED = float(0x5F3759DF)
BQK, GQ, GK, BQ, BK, L1W, L1B, BG = 0, 2, 4, 6, 8, 10, 12, 14
NVEC = 18


def is_int(n):
    return isinstance(n, int)


def size(r, small):
    return HT if (r >= BIG if is_int(r) else small) else ST


def tiles(r, small):
    if r >= BIG if is_int(r) else small:
        return BIG * (ST - HT) + r * HT
    return r * ST


def need(engine, sem, n):
    if not is_int(n) or n > 0:
        engine.wait_ge(sem, n)


class Links:

    def __init__(self, engine, sem):
        self.engine, self.sem, self.base, self.k, self.loop = engine, sem, 0, 0, None

    def __call__(self, instruction):
        self.k += 1
        instruction.then_inc(self.sem, 1)
        self.engine.wait_ge(self.sem, self.base + self.k)

    def total(self):
        return self.base + self.k

    def at(self, base):
        self.base, self.k = base, 0

    def enter(self, step, first, per_step):
        if not self.loop:
            self.loop = (self.total(), per_step)
        self.at(self.loop[0] + (step - first) * per_step)

    def leave(self):
        assert self.k == self.loop[1], (self.k, self.loop)

    def end(self, steps):
        self.at(self.loop[0] + steps * self.loop[1])
        self.loop = None


def rsqrt(nc, link, y, half, v, tmp):
    link(nc.vector.tensor_single_scalar(half, v.bitcast(I32), 1, ALU.logical_shift_right))
    link(nc.vector.tensor_scalar(y.bitcast(I32), half, -1.0, RSQRT_SEED, ALU.mult, ALU.add))
    for _ in range(3):
        link(nc.vector.tensor_tensor(tmp, y, y, ALU.mult))
        link(nc.vector.scalar_tensor_tensor(tmp, tmp, -0.5, v, ALU.mult, ALU.mult))
        link(nc.vector.scalar_tensor_tensor(y, tmp, 1.5, y, ALU.add, ALU.mult))


def moments(nc, link, st, mean, var, tmp):
    part = lambda i: st[:, :, i]
    nc.vector.tensor_tensor(mean, part(1), part(4), ALU.add)
    nc.vector.tensor_tensor(tmp, part(1), part(4), ALU.subtract)
    link(nc.vector.tensor_tensor(var, part(2), part(5), ALU.add))
    nc.vector.tensor_scalar(mean, mean, 0.5, None, ALU.mult)
    nc.vector.scalar_tensor_tensor(tmp, tmp, 0.25, tmp, ALU.mult, ALU.mult)
    link(nc.vector.tensor_scalar(var, var, 1.0 / D, EPS, ALU.mult, ALU.add))
    link(nc.vector.tensor_tensor(var, var, tmp, ALU.add))


def build(nc, a, out):
    ctx = ExitStack()

    def sem(name):
        return ctx.enter_context(nc.semaphore(name))

    XHL = nc.dram_tensor("x1_parts", (B, P, 2 * KD * T), F32, kind="Internal").ap()
    X1D = nc.dram_tensor("x1_rows", (N, D), F32, kind="Internal").ap()
    XS = nc.dram_tensor("slot_rows", (SLOTS, ROW), F32, kind="Internal").ap()
    YY = nc.dram_tensor("expert_results", (2 * N, D), F32, kind="Internal").ap()

    with ctx:
        keep = lambda n, s, t: ctx.enter_context(nc.sbuf_tensor("k_" + n, s, t))
        ident = keep("ident", [P, P], F32)
        ones2 = keep("ones2", [2, P], F32R)
        mask2 = keep("mask2", [2, 2], F32)
        logits = keep("logits", [P, NT, NE], F32)
        wstage = keep("wstage", [P, 2, KD * HID], F32)
        wfc1 = [keep(f"wfc1{p}", [P, KD, HID], F32R) for p in "hl"]
        wpj1 = [keep(f"wpj1{p}", [P, KH, D], F32R) for p in "hl"]
        bfc = [keep(f"bfc{i}", [P, KH], F32) for i in range(2)]
        bpj_raw = [keep(f"bpj_raw{i}", [2, D], F32) for i in range(2)]
        bpj = [keep(f"bpj{i}", [2, D], F32R) for i in range(2)]
        row_t = keep("row_t", [2, E], F32)
        row_h = keep("row_h", [2, E], F32R)

        attention(nc, a, locals())
        experts(nc, a, out, locals())


def attention(nc, a, shared):
    ident, ones2, mask2, logits = (shared[k] for k in ("ident", "ones2", "mask2", "logits"))
    wstage, wfc1, wpj1, bpj_raw, bpj = (shared[k] for k in ("wstage", "wfc1", "wpj1", "bpj_raw", "bpj"))
    row_t, row_h = shared["row_t"], shared["row_h"]
    bfc = shared["bfc"]
    XHL, X1D, XS = shared["XHL"], shared["X1D"], shared["XS"]
    with ExitStack() as ctx:
        sb = lambda n, s, t=F32: ctx.enter_context(nc.sbuf_tensor("s_" + n, s, t))
        sem = lambda n: ctx.enter_context(nc.semaphore(n))
        pair = lambda n, s: [sb(n + p, s, F32R) for p in "hl"]

        vec = sb("vec", [P, NVEC])
        rope = sb("rope", [P, 2, T])
        offs = sb("offs", [P, 2, T])
        bias = sb("bias", [P, G])
        ln2 = sb("ln2", [P, 2, D])
        wr = sb("wr", [P, KD, NE])
        wqk, wv, wg, wo = (pair(n, s) for n, s in (("wqk", [P, 2, KD, P]), ("wv", [P, KD, E]),
                                                   ("wg", [P, KD, E]), ("wo", [P, KE, D])))
        wrh, wrl = pair("wr", [P, KD, NE])
        rows_raw = sb("rows_raw", [2, 2, E])
        bv2 = sb("bv2", [2, E], F32R)
        bo2 = sb("bo2", [2, D], F32R)
        ones_raw = sb("ones_raw", [2, P])
        empty = sb("empty", [P, ROW])
        x_in = sb("x_in", [P, TT, D])
        x_res = sb("x_res", [P, TT, D])
        xn = sb("xn", [P, TT, D])
        xT = sb("xT", [P, KD, T])
        xTh, xTl = pair("xT", [P, KD, T])
        v = sb("v", [P, TT, E])
        qk = sb("qk", [P, 2, T])
        qkr = sb("qkr", [P, 2, T])
        heads = sb("heads", [P, 2, T])
        kT = sb("kT", [P, TT, P])
        att = sb("att", [P, TT, P])
        kv = sb("kv", [P, E])
        u = sb("u", [P, KE, T])
        uh, ul = pair("u", [P, KE, T])
        z = sb("z", [P, TT, D])
        x1 = sb("x1", [P, TT, D])
        x1T = sb("x1T", [P, KD, T])
        x1h, x1l = pair("x1", [P, KD, T])
        st = sb("st", [P, 2 * TT, 6])
        mean = sb("mean", [P, 2 * TT])
        var, rs, tmp = sb("var", [P, 2 * TT]), sb("rs", [P, 2 * TT]), sb("tmp", [P, 2 * TT])
        half = sb("half", [P, 2 * TT], I32)
        raw = wstage[:, :, :].rearrange("p a n -> p (a n)")
        raw_v, raw_g = raw[:, 0:1024].rearrange("p (k n) -> p k n", k=KD), raw[:, 1024:2048].rearrange("p (k n) -> p k n", k=KD)
        raw_qk = raw[:, 2048:2560].rearrange("p (s k n) -> p s k n", s=2, k=KD)
        raw_o = raw[:, 2560:3584].rearrange("p (k n) -> p k n", k=KE)

        bank = [ctx.enter_context(nc.psum_tensor(f"bank{i}", [P, 512], F32)) for i in range(8)]

        ld_v0, ld_c0, ld_c1, ld_c = sem("norm_consts_loaded"), sem("bias_rows_loaded"), sem("rope_loaded"), sem("consts_loaded")
        ld_w = [sem(f"{n}_loaded") for n in ("wv", "wqk", "wg", "wo")]
        ld_x, ld_r = sem("x_loaded"), sem("residual_loaded")
        ld_s = sem("shared_weights_loaded")
        filled = sem("slots_emptied")
        wh_rd, wl_rd, split_s = sem("weights_hi_ready"), sem("weights_lo_ready"), sem("shared_weights_split")
        dve_own, act_own = sem("vector_own"), sem("scalar_own")
        xn_ready, xT_mm, xT_ev, xTh_rd, xTl_rd = (sem(n) for n in ("xn_ready", "xT_transposed", "xT_evacuated", "xTh_ready", "xTl_ready"))
        v_mm, v_ev, q_mm, q_ev, qkr_rd, heads_rd = (sem(n) for n in ("v_product", "v_ready", "qk_product", "qk_ready", "qk_roped", "heads_ready"))
        o_mm, o_ev, g_mm, g_ev = (sem(n) for n in ("o_product", "o_evacuated", "gate_product", "gate_ready"))
        kT_mm, kT_ev, sc_mm, att_rd, kv_mm, kv_ev = (sem(n) for n in ("kT_transposed", "kT_ready", "scores_product", "att_ready", "kv_product", "kv_ready"))
        u_mm, u_ml, uh_rd, ul_rd = (sem(n) for n in ("u_product", "u_gated", "uh_ready", "ul_ready"))
        res_rd, res_used, x1_rd, x1T_mm, x1T_ev, lg_mm, lg_ev = (sem(n) for n in (
            "residual_ready", "residual_used", "x1_ready", "x1T_transposed", "x1T_evacuated", "logits_product", "logits_ready"))
        x1h_rd, x1l_rd, sh_st, x1_st = (sem(n) for n in ("x1h_ready", "x1l_ready", "parts_stored", "x1_stored"))
        tab_rd = sem("tables_ready")

        block = ctx.enter_context(nc.Block())
        x_view = a["x"].rearrange("(b t p) d -> b p t d", b=B, p=P)
        x1_view = X1D.rearrange("(b t p) d -> b p t d", b=B, p=P)

        EMPTYINGS = B - 2
        EMPTY_ROWS = SLOTS // P // EMPTYINGS
        assert EMPTY_ROWS * EMPTYINGS * P == SLOTS
        CONSTS = 7

        def stages(b):
            is_main, ahead = (not is_int(b) or b < B), (not is_int(b) or b < B - 1)
            return is_main, ahead, not is_int(b) or 1 <= b <= B, not is_int(b) or b >= 2

        def steps(engine, step, last_in_loop=B - 1):
            for b in range(3):
                step(b)
            with engine.Fori(3, last_in_loop) as b:
                step(b)
            for b in range(last_in_loop, B + 2):
                step(b)

        def bidx(ap, b):
            return ap[bass.ds(b, 1)].rearrange("b p t d -> (b p) t d")

        weights, raws = (wv, wqk, wg, wo), (raw_v, raw_qk, raw_g, raw_o)

        @block.sync
        def _(sp):
            sp.dma_start(x_in[:, :, :], bidx(x_view, 0)).then_inc(ld_x, 16)
            def load(done, *pairs):
                for dst, src in pairs:
                    sp.dma_start(dst, src).then_inc(done, 16)

            load(ld_v0, (vec[:, :], a["vec"]), (ident[:, :], a["ident"]))
            load(ld_w[0], (raw_v, a["wv"]))
            load(ld_c0, (rows_raw[:, :, :], a["rows"]), (ones_raw[:, :], a["ones"]), (mask2[:, :], a["mask2"]))
            load(ld_w[1], (raw_qk, a["wqk"]))
            load(ld_c1, (rope[:, :, :], a["rope"]))
            load(ld_w[2], (raw_g, a["wg"]))
            sp.wait_ge(xn_ready, 1)
            sp.dma_start(x_in[:, :, :], bidx(x_view, 1)).then_inc(ld_x, 16)
            load(ld_w[3], (raw_o, a["wo"]))
            load(ld_c, (ln2[:, :, :], a["ln2"]), (wr[:, :, :], a["wr"]), (empty[:, :], a["empty"]),
                 (bfc[1][:, :], a["bfc"][NE]), (bpj_raw[1][:, :], a["bproj"][NE]))
            skew = a["ext"][G - 1:G - 1 + (2 * G - 2) * G].rearrange("(j n) -> j n", n=2 * G - 2)[:, 0:G]
            for h in range(2):
                sp.dma_start(bias[h * G:(h + 1) * G, :], skew).then_inc(ld_c, 16)
            sp.wait_ge(wl_rd, 4)
            sp.dma_start(wstage[:, :, :], a["wall"][NE]).then_inc(ld_s, 16)

            def step(b):
                main, ahead, o, last = stages(b)
                if is_int(b) and b == 0:
                    sp.wait_ge(ld_c, 16 * CONSTS)
                if not is_int(b) or b < EMPTYINGS:
                    dst = XS.rearrange("(q p r) w -> q p r w", p=P, r=EMPTY_ROWS)[bass.ds(b, 1)].rearrange("q p r w -> (q p) r w")
                    sp.dma_start(dst, empty[:, :].rearrange("p (o w) -> p o w", o=1).to_broadcast([P, EMPTY_ROWS, ROW])).then_inc(filled, 16)
                if o:
                    need(sp, res_used, b - 1)
                    sp.dma_start(x_res[:, :, :], bidx(x_view, b - 1)).then_inc(ld_r, 16)
                c = b - 2
                if last:
                    sp.wait_ge(x1_rd, c + 1)
                    sp.dma_start(bidx(x1_view, c), x1[:, :, :]).then_inc(x1_st, 16)
                if ahead:
                    sp.wait_ge(xn_ready, b + 2)
                    if not is_int(b) or b + 2 < B:
                        sp.dma_start(x_in[:, :, :], bidx(x_view, b + 2)).then_inc(ld_x, 16)
                if last:
                    dst = XHL[bass.ds(c, 1)].rearrange("b p n -> (b p) n")
                    sp.wait_ge(x1h_rd, 2 * c + 2)
                    sp.dma_start(dst[:, 0:KD * T], x1h[:, :, :].bitcast(F32).rearrange("p k n -> p (k n)")).then_inc(sh_st, 16)
                    sp.wait_ge(x1l_rd, 2 * c + 2)
                    sp.dma_start(dst[:, KD * T:], x1l[:, :, :].bitcast(F32).rearrange("p k n -> p (k n)")).then_inc(sh_st, 16)

            steps(sp, step, B - 2)
            sp.wait_ge(x1_st, 16 * B)
            sp.wait_ge(sh_st, 32 * B)
            sp.wait_ge(filled, 16 * EMPTYINGS)

        @block.gpsimd
        def _(pool):
            nc.gpsimd.memset(att[:, :, :], 0.0).then_inc(tab_rd, 1)
            pool.wait_ge(ld_s, 16)
            for c in range(2):
                w = (wfc1, wpj1)[c]
                src = wstage[:, c, :].rearrange("p (k n) -> p k n", k=w[0].shape[1])
                nc.gpsimd.tensor_scalar(w[0][:, :, :], src, 1.0, 0.0, ALU.mult, ALU.add).then_inc(split_s, 1)
                pool.wait_ge(split_s, 2 * c + 1)
                nc.gpsimd.tensor_tensor(w[1][:, :, :], src, w[0][:, :, :].bitcast(F32), ALU.subtract).then_inc(split_s, 1)

            def step(b):
                pool.wait_ge(ld_r, 16 * (b + 1))
                nc.gpsimd.tensor_tensor(x_res[:, :, :], x_res[:, :, :],
                                        ln2[:, 1:2, :].to_broadcast([P, TT, D]), ALU.add).then_inc(res_rd, 1)

            pool.wait_ge(ld_c, 16 * CONSTS)
            with pool.Fori(0, B) as b:
                step(b)
            pool.wait_ge(split_s, 4)

        @block.scalar
        def _(act):
            copy = lambda o, i: nc.scalar.activation(o, i, ACT.Copy)
            def weights_hi(n):
                act.wait_ge(ld_w[n], 16)
                copy(weights[n][0][:], raws[n]).then_inc(wh_rd, 1)

            def x_transposed(b):
                for c in range(KD):
                    act.wait_ge(xT_mm, 2 * b + c + 1)
                    nc.scalar.activation(xT[:, c, :], bank[(7, 0)[c]][:, :], ACT.Identity, scale=vec[:, L1W + c:L1W + c + 1],
                                         bias=vec[:, L1B + c:L1B + c + 1]).then_inc(xT_ev, 1)
                for c in range(KD):
                    act.wait_ge(xT_ev, 2 * b + c + 1)
                    copy(xTh[:, c, :], xT[:, c, :]).then_inc(xTh_rd, 1)

            def step(b):
                main, ahead, o, last = stages(b)
                if main:
                    for t in range(TT):
                        act.wait_ge(v_mm, 4 * b + t + 1)
                        nc.scalar.activation(v[:, t, :], bank[t][:, :], ACT.Silu).then_inc(v_ev, 1)
                    for s in range(2):
                        act.wait_ge(q_mm, 2 * b + s + 1)
                        need(act, qkr_rd, 2 * (b - 1) + s + 1)
                        nc.scalar.activation(qk[:, s, :], bank[4 + s][:, :], ACT.Silu,
                                             bias=vec[:, BQK + s:BQK + s + 1]).then_inc(q_ev, 1)
                    act.wait_ge(kT_mm, b + 1)
                    copy(kT[:, :, :].rearrange("p t n -> p (t n)"), bank[4][:, :]).then_inc(kT_ev, 1)
                    for m in range(KE):
                        act.wait_ge(g_mm, 4 * b + m + 1)
                        nc.scalar.activation(u[:, m, :], bank[m][:, :], ACT.Silu,
                                             bias=vec[:, BG + m:BG + m + 1]).then_inc(g_ev, 1)
                    act.wait_ge(kv_mm, b + 1)
                    nc.scalar.activation(kv[QK:P, :], bank[6][QK:P, :], ACT.Copy, scale=1.0 / T).then_inc(kv_ev, 1)
                if ahead:
                    x_transposed(b + 1)
                c = b - 2
                if last:
                    for k in range(KD):
                        act.wait_ge(x1T_mm, 2 * c + k + 1)
                        need(act, x1l_rd, 2 * (c - 1) + k + 1)
                        copy(x1T[:, k, :], bank[4 + k][:, :]).then_inc(x1T_ev, 1)
                    need(act, sh_st, 32 * c)
                    for k in range(KD):
                        act.wait_ge(x1T_ev, 2 * c + k + 1)
                        copy(x1h[:, k, :], x1T[:, k, :]).then_inc(x1h_rd, 1)
                if main:
                    for m in range(KE):
                        act.wait_ge(u_ml, 4 * b + m + 1)
                        copy(uh[:, m, :], u[:, m, :]).then_inc(uh_rd, 1)
                if last:
                    act.wait_ge(lg_mm, c + 1)
                    copy(logits[:, bass.ds(c * TT, TT), :].rearrange("p t e -> p (t e)"), bank[7][:, 0:TT * NE]).then_inc(lg_ev, 1)

            weights_hi(0)
            act.wait_ge(ld_v0, 32)
            x_transposed(0)
            for n in (1, 2, 3):
                weights_hi(n)
            steps(act, step)

        @block.vector
        def _(dve):
            link = Links(dve, dve_own)
            tt = nc.vector.tensor_tensor
            stt = nc.vector.scalar_tensor_tensor

            def norm(o, i, k):
                return nc.vector.tensor_scalar(o, i, mean[:, k:k + 1], rs[:, k:k + 1], ALU.subtract, ALU.mult)

            def rstd(lo, hi):
                moments(nc, link, st[:, lo:hi, :], mean[:, lo:hi], var[:, lo:hi], tmp[:, lo:hi])
                rsqrt(nc, link, rs[:, lo:hi], half[:, lo:hi], var[:, lo:hi], tmp[:, lo:hi])

            def stats(tiles, k, wait=None):
                for t, ap in enumerate(tiles):
                    if wait:
                        wait(t)
                    last = nc.vector.bn_stats(st[:, k + t, :], ap)
                link(last)

            def x_normed(b):
                need(dve, xT_mm, 2 * b)
                for t in range(TT):
                    last = norm(xn[:, t, :], x_in[:, t, :], t)
                last.then_inc(xn_ready, 1)

            def xT_rest(b):
                for c in range(KD):
                    dve.wait_ge(xTh_rd, 2 * b + c + 1)
                    tt(xTl[:, c, :], xT[:, c, :], xTh[:, c, :].bitcast(F32), ALU.subtract).then_inc(xTl_rd, 1)

            def two_rows(dst, src, n, before=0):
                need(dve, tab_rd, before)
                link(nc.vector.tensor_copy(row_h[:, 0:n], src))
                link(tt(row_t[:, 0:n], src, row_h[:, 0:n].bitcast(F32), ALU.subtract))
                link(nc.vector.tensor_scalar(row_t[:, 0:n], row_t[:, 0:n], mask2[:, 1:2], None, ALU.mult))
                stt(dst, row_h[:, 0:n].bitcast(F32), mask2[:, 0:1], row_t[:, 0:n], ALU.mult, ALU.add).then_inc(tab_rd, 1)

            def step(b):
                main, ahead, o, last = stages(b)
                c = b - 2
                if last:
                    dve.wait_ge(o_ev, 4 * c + 4)
                    link(tt(z[:, :, :], z[:, :, :], ln2[:, 0:1, :].to_broadcast([P, TT, D]), ALU.mult))
                    dve.wait_ge(res_rd, c + 1)
                    tt(z[:, :, :], z[:, :, :], x_res[:, :, :], ALU.add).then_inc(res_used, 1)
                    dve.wait_ge(res_used, c + 1)
                    stats([z[:, t, :] for t in range(TT)], TT)
                if ahead:
                    dve.wait_ge(ld_x, 16 * (b + 2))
                    stats([x_in[:, t, :] for t in range(TT)], 0)
                if ahead or last:
                    rstd(0 if ahead else TT, 2 * TT if last else TT)
                if last:
                    need(dve, x1_st, 16 * c)
                    for t in range(TT):
                        last_i = norm(x1[:, t, :], z[:, t, :], TT + t)
                    last_i.then_inc(x1_rd, 1)
                if main:
                    for s in range(2):
                        dve.wait_ge(q_ev, 2 * b + s + 1)
                        last_i = tt(qkr[:, s, :], qk[:, s, :], rope[:, s, :], ALU.mult)
                        last_i.then_inc(qkr_rd, 1)
                    dve.wait_ge(qkr_rd, 2 * b + 1)
                    stt(heads[:, 0, :], qkr[:, 0, :], vec[:, GQ:GQ + 1], offs[:, 0, :], ALU.mult, ALU.add)
                    link(stt(heads[:, 1, :], qkr[:, 0, :], vec[:, GK:GK + 1], offs[:, 1, :], ALU.mult, ALU.add))
                    dve.wait_ge(qkr_rd, 2 * b + 2)
                    stt(heads[:, 1, :], qkr[:, 1, :], vec[:, GK + 1:GK + 2], heads[:, 1, :], ALU.mult, ALU.add).then_inc(heads_rd, 1)
                    stt(heads[:, 0, :], qkr[:, 1, :], vec[:, GQ + 1:GQ + 2], heads[:, 0, :], ALU.mult, ALU.add).then_inc(heads_rd, 1)
                if o:
                    yo = [bank[6 + t // 2][:, t % 2 * D:t % 2 * D + D] for t in range(TT)]
                    stats(yo, TT, lambda t: t % 2 or dve.wait_ge(o_mm, 2 * (b - 1) + t // 2 + 1))
                    rstd(TT, 2 * TT)
                    for t in range(TT):
                        norm(z[:, t, :], yo[t], TT + t).then_inc(o_ev, 1)
                if ahead:
                    x_normed(b + 1)
                if main:
                    if is_int(b) and b == 0:
                        dve.wait_ge(ld_c, 16 * CONSTS)
                    dve.wait_ge(sc_mm, b + 1)
                    sc = bank[5][:, :].rearrange("p (t n) -> p t n", t=TT)
                    for g in range(P // G):
                        r = slice(g * G, (g + 1) * G)
                        last_i = stt(att[r, :, r], sc[r, :, r], 1.0 / G,
                                     bias[r, :].rearrange("p (o n) -> p o n", o=1).to_broadcast([G, TT, G]), ALU.mult, ALU.add)
                    link(last_i)
                    for g in range(P // G):
                        r = slice(g * G, (g + 1) * G)
                        last_i = stt(att[r, :, r], att[r, :, r], 0.0, att[r, :, r], ALU.max, ALU.mult)
                    last_i.then_inc(att_rd, 1)
                if ahead:
                    xT_rest(b + 1)

                def x1_rest():
                    for k in range(KD):
                        dve.wait_ge(x1h_rd, 2 * c + k + 1)
                        tt(x1l[:, k, :], x1T[:, k, :], x1h[:, k, :].bitcast(F32), ALU.subtract).then_inc(x1l_rd, 1)

                def rest(m):
                    dve.wait_ge(uh_rd, 4 * b + m + 1)
                    tt(ul[:, m, :], u[:, m, :], uh[:, m, :].bitcast(F32), ALU.subtract).then_inc(ul_rd, 1)

                if main:
                    for m in range(KE):
                        dve.wait_ge(u_mm, 4 * b + m + 1)
                        tt(u[:, m, :], u[:, m, :], bank[1 + m][:, :], ALU.mult).then_inc(u_ml, 1)
                        if m:
                            rest(m - 1)
                        elif last:
                            x1_rest()
                    rest(KE - 1)
                elif last:
                    x1_rest()

            dve.wait_ge(ld_x, 16)
            stats([x_in[:, t, :] for t in range(TT)], 0)
            rstd(0, TT)
            x_normed(0)

            def weights_lo(n):
                dve.wait_ge(wh_rd, n + 1)
                tt(weights[n][1][:], raws[n], weights[n][0][:].bitcast(F32), ALU.subtract).then_inc(wl_rd, 1)

            weights_lo(0)
            dve.wait_ge(ld_c0, 48)
            nc.vector.tensor_copy(ones2[:, :], ones_raw[:, :])
            two_rows(bv2[:, :], rows_raw[:, 0, :], E)
            xT_rest(0)
            weights_lo(1)
            dve.wait_ge(ld_v0, 32)
            dve.wait_ge(ld_c1, 16)
            for k, c in enumerate((BQ, BK)):
                link(nc.vector.tensor_scalar(offs[:, k, :], rope[:, 0, :], vec[:, c:c + 1], None, ALU.mult))
                link(stt(offs[:, k, :], rope[:, 1, :], vec[:, c + 1:c + 2], offs[:, k, :], ALU.mult, ALU.add))
            weights_lo(2)
            step(0)
            weights_lo(3)
            two_rows(bo2[:, :], rows_raw[:, 1, 0:D], D, 2)
            dve.wait_ge(ld_c, 16 * CONSTS)
            two_rows(bpj[1][:, :], bpj_raw[1][:, :], D, 3)
            link(nc.vector.tensor_copy(wrh[:, :, :], wr[:, :, :]))
            tt(wrl[:, :, :], wr[:, :, :], wrh[:, :, :].bitcast(F32), ALU.subtract).then_inc(tab_rd, 1)
            step(1)
            step(2)
            with dve.Fori(3, B - 1) as b:
                link.enter(b, 3, STEP_LINKS)
                step(b)
                link.leave()
            link.end(B - 4)
            for b in range(B - 1, B + 2):
                step(b)

        @block.tensor
        def _(pe):
            mm, tr = nc.tensor.matmul, nc.tensor.transpose

            def three(o, wh, wl, xh, xl, start, stop):
                mm(o, wh, xl, start=start, stop=False)
                mm(o, wl, xh, start=False, stop=False)
                return mm(o, wh, xh, start=False, stop=stop)

            def transposes(src, banks, done):
                for c in range(KD):
                    for t in range(TT):
                        last = tr(bank[banks[c]][:, t * P:(t + 1) * P], src[:, t, c * P:(c + 1) * P], ident[:, :])
                    last.then_inc(done, 1)

            def step(b):
                main, ahead, o, last = stages(b)
                c = b - 2
                at = lambda n: is_int(b) and b == n
                if main:
                    if at(0):
                        pe.wait_ge(wl_rd, 1)
                    pe.wait_ge(xTh_rd, 2 * b + 2)
                    pe.wait_ge(xTl_rd, 2 * b + 2)
                    for t in range(TT):
                        if t:
                            need(pe, u_ml, 4 * (b - 1) + t)
                        cols = slice(t * P, (t + 1) * P)
                        mm(bank[t][:, :], ones2[:, :], bv2[:, :], start=True, stop=False)
                        for k in range(KD):
                            last_i = three(bank[t][:, :], xTh[:, k, cols], xTl[:, k, cols], wv[0][:, k, :], wv[1][:, k, :],
                                           False, k == KD - 1)
                        last_i.then_inc(v_mm, 1)
                    for s in range(2):
                        if at(0):
                            pe.wait_ge(wl_rd, 2)
                        if s == 0:
                            need(pe, u_ml, 4 * b)
                        else:
                            need(pe, x1T_ev, 2 * (c - 1) + 2)
                        for k in range(KD):
                            last_i = three(bank[4 + s][:, :], wqk[0][:, s, k, :], wqk[1][:, s, k, :], xTh[:, k, :], xTl[:, k, :],
                                           k == 0, k == KD - 1)
                        last_i.then_inc(q_mm, 1)
                if o:
                    if at(1):
                        pe.wait_ge(wl_rd, 4)
                        pe.wait_ge(tab_rd, 3)
                    pe.wait_ge(ul_rd, 4 * b)
                    for t in range(TT):
                        if t == 2:
                            need(pe, lg_ev, c)
                        cols = slice(t * P, (t + 1) * P)
                        out = bank[6 + t // 2][:, t % 2 * D:t % 2 * D + D]
                        mm(out, ones2[:, :], bo2[:, :], start=True, stop=False)
                        for m in range(KE):
                            last_i = three(out, uh[:, m, cols], ul[:, m, cols], wo[0][:, m, :], wo[1][:, m, :], False, m == KE - 1)
                        if t % 2:
                            last_i.then_inc(o_mm, 1)
                if main:
                    pe.wait_ge(heads_rd, 2 * b + 1)
                    for t in range(TT):
                        last_i = tr(bank[4][:, t * P:(t + 1) * P], heads[:, 1, t * P:(t + 1) * P], ident[:, :])
                    last_i.then_inc(kT_mm, 1)
                    pe.wait_ge(heads_rd, 2 * b + 2)
                    for t in range(TT):
                        cols = slice(t * P, (t + 1) * P)
                        last_i = mm(bank[5][:, cols], heads[0:QK, 1, cols], heads[0:QK, 0, cols], start=True, stop=True)
                    last_i.then_inc(sc_mm, 1)
                    if at(0):
                        pe.wait_ge(wl_rd, 3)
                    for m in range(KE):
                        pe.wait_ge(v_ev, 4 * b + m + 1)
                        rows = slice(m * P, (m + 1) * P)
                        for k in range(KD):
                            last_i = three(bank[m][:, :], wg[0][:, k, rows], wg[1][:, k, rows], xTh[:, k, :], xTl[:, k, :],
                                           k == 0, k == KD - 1)
                        last_i.then_inc(g_mm, 1)
                    pe.wait_ge(kT_ev, b + 1)
                    need(pe, o_ev, 4 * (b - 1) + 2)
                    for t in range(TT):
                        last_i = mm(bank[6][:, :], kT[:, t, :], v[:, t, :], start=t == 0, stop=t == TT - 1)
                    last_i.then_inc(kv_mm, 1)
                if ahead:
                    pe.wait_ge(xn_ready, b + 2)
                    need(pe, o_ev, 4 * b)
                    pe.wait_ge(g_ev, 4 * b + 1)
                    transposes(xn, (7, 0), xT_mm)
                if main:
                    pe.wait_ge(att_rd, b + 1)
                if last:
                    pe.wait_ge(x1_rd, c + 1)
                    if not main:
                        pe.wait_ge(x1T_ev, 2 * c)
                    transposes(x1, (4, 5), x1T_mm)
                if main:
                    pe.wait_ge(kv_ev, b + 1)
                    for m in range(KE):
                        if m < 3:
                            pe.wait_ge(g_ev, 4 * b + m + 2)
                        elif last:
                            pe.wait_ge(x1T_ev, 2 * c + 1)
                        rows = slice(m * P, (m + 1) * P)
                        out = bank[1 + m]
                        mm(out[:, :], kv[QK:P, rows], heads[QK:P, 0, :], start=True, stop=False)
                        for t in range(TT):
                            cols = slice(t * P, (t + 1) * P)
                            last_i = mm(out[:, cols], v[:, t, rows], att[:, t, :], start=False, stop=t == TT - 1)
                        last_i.then_inc(u_mm, 1)
                if last:
                    if at(2):
                        pe.wait_ge(tab_rd, 5)
                    pe.wait_ge(x1l_rd, 2 * c + 2)
                    if ahead:
                        pe.wait_ge(xT_ev, 2 * (b + 1) + 1)
                    if at(B):
                        pe.wait_ge(o_ev, 4 * B)
                    if at(B + 1):
                        pe.wait_ge(lg_ev, c)
                    for t in range(TT):
                        cols = slice(t * P, (t + 1) * P)
                        for k in range(KD):
                            last_i = three(bank[7][:, t * NE:(t + 1) * NE], x1h[:, k, cols], x1l[:, k, cols],
                                           wrh[:, k, :], wrl[:, k, :], k == 0, k == KD - 1)
                    last_i.then_inc(lg_mm, 1)

            pe.wait_ge(ld_v0, 32)
            pe.wait_ge(xn_ready, 1)
            transposes(xn, (7, 0), xT_mm)
            pe.wait_ge(tab_rd, 2)
            steps(pe, step)


STEP_LINKS = 34
PAIR_LINKS = 15
SMALL_LINKS = 3
BLOCK_LINKS = 11


def experts(nc, a, out, shared):
    ident, ones2, mask2, logits = (shared[k] for k in ("ident", "ones2", "mask2", "logits"))
    wstage, wfc1, wpj1, bfc, bpj_raw, bpj = (shared[k] for k in ("wstage", "wfc1", "wpj1", "bfc", "bpj_raw", "bpj"))
    row_t, row_h = shared["row_t"], shared["row_h"]
    XHL, X1D, XS, YY = (shared[k] for k in ("XHL", "X1D", "XS", "YY"))
    with ExitStack() as ctx:
        sb = lambda n, s, t=F32: ctx.enter_context(nc.sbuf_tensor("s_" + n, s, t))
        sem = lambda n: ctx.enter_context(nc.semaphore(n))

        wfc = [[sb(f"wfc0{p}", [P, KD, HID], F32R) for p in "hl"], wfc1]
        wpj = [[sb(f"wpj0{p}", [P, KH, D], F32R) for p in "hl"], wpj1]
        rows = sb("rows", [P, NT, ROW])
        acc = sb("acc", [P, NT, D])
        xh = [sb(f"blk_xh{i}", [P, KD, S], F32R) for i in range(2)]
        xl = [sb(f"blk_xl{i}", [P, KD, S], F32R) for i in range(2)]
        xb = sb("xb", [P, ST, ROW])
        RING = 4
        h = [sb(f"h{i}", [P, S]) for i in range(2)]
        hh = [sb(f"hh{i}", [P, S], F32R) for i in range(RING)]
        hl = [sb(f"hl{i}", [P, S], F32R) for i in range(RING)]
        y = sb("y", [P, ST, D])
        dest = [sb(f"dest{i}", [P, ST], I32) for i in range(2)]
        gate = [sb(f"gate{i}", [P, ST]) for i in range(2)]
        PAIRS = NT * ROW // (2 * TT * D)
        pairs = [rows[:, :, :].rearrange("p t n -> p (t n)")[:, i * 2 * TT * D:(i + 1) * 2 * TT * D] for i in range(PAIRS)]
        rt = [y[:, i, :].rearrange("p (e t) -> p e t", e=NE) for i in range(4)]
        choice = [xb[:, i, 0:NE * NT].rearrange("p (e t) -> p e t", e=NE) for i in range(2)]
        both = sb("both", [P, NE * NT], BF16)
        cnt = sb("cnt", [P, 8, NT])
        small_t = sb("small", [P, max(NE * MOST, BIG * NE)])
        n_big, n_small, start_big, start_small = (sb(n, [P, NE]) for n in ("n_big", "n_small", "start_big", "start_small"))
        pos = [sb(f"pos{i}", [P, NT], I32) for i in range(2)]
        owner_f = sb("owner_f", [P, ROUTED])
        owner = sb("owner", [P, ROUTED], I32)
        cst = sb("cst", [P, a["route"].shape[1]])
        tri = sb("tri", [P, 2, P])
        trib = sb("trib", [P, 2, P], BF16)
        st = sb("mst", [P, 2 * TT, 6])
        m_now, r_now, var, tmp = (sb(n, [P, 2 * TT]) for n in ("m_now", "r_now", "mvar", "mtmp"))
        half = sb("mhalf", [P, 2 * TT], I32)
        mean, rs = sb("mmean", [P, NT]), sb("mrs", [P, NT])

        fcb = [ctx.enter_context(nc.psum_tensor(f"fc_bank{i}", [P, 512], F32)) for i in range(4)]
        yb = [[ctx.enter_context(nc.psum_tensor(f"y_bank{i}{k}", [P, 512], F32)) for k in range(2)] for i in range(2)]

        ld_c, ld_rows, ld_xT = sem("route_consts_loaded"), sem("rows_loaded"), [sem(f"parts_loaded{i}") for i in range(2)]
        ld_w = [sem(f"expert_{n}_loaded") for n in ("fc", "pj")]
        ld_b, ld_xb, ld_y = [sem(f"expert_biases_loaded{i}") for i in range(2)], sem("slots_loaded"), [sem(f"results_loaded{i}") for i in range(PAIRS)]
        whi_rd = [sem(f"expert_{n}_hi_ready") for n in ("fc", "pj")]
        w_rd, bpj_rd = [sem(f"expert_{n}_split") for n in ("fc", "pj")], sem("expert_bias_split")
        fc_mm, h_ev, hh_rd, hl_rd, pj_mm = (sem(n) for n in ("fc_product", "h_ready", "hh_ready", "hl_ready", "proj_product"))
        t_mm, xh_rd, xl_rd = sem("slots_transposed"), sem("slots_hi_ready"), sem("slots_lo_ready")
        y_ev, y_out = sem("y_evacuated"), sem("results_scattered")
        cum_rd, tri_rd, st_rd = sem("counts_read"), sem("masks_ready"), sem("statistics_ready")
        meta_rd = sem("slots_meta_ready")
        acc_rd = sem("acc_ready")
        e_rd, both_rd, cum_mm, own_rd = sem("exp_ready"), sem("choices_ready"), sem("counts_product"), sem("owners_ready")
        d_rd, rows_rd = sem("logits_shifted"), sem("rows_ready")
        sent = [sem(f"rows_sent{i}") for i in range(2)]
        dve_own = sem("vector_own2")
        tot_rd, o_rd, o_out = sem("totals_ready"), sem("out_ready"), sem("out_stored")
        yy_rd = sem("pairs_summed")

        block = ctx.enter_context(nc.Block())
        x1_view = X1D.rearrange("(t p) d -> p t d", p=P)
        xs_view = (XS[0:BIG * S, :].rearrange("(r t p) w -> r p t w", t=ST, p=P),
                   XS[BIG * S:, :].rearrange("(r t p) w -> r p t w", t=HT, p=P))
        yy_view = YY.rearrange("(k t p) d -> k p t d", k=2, p=P)
        out_view = out.rearrange("(b t p) d -> b p t d", b=B, p=P)

        PLAIN = [("fc", j) for j in range(KH)]
        WITH_T = PLAIN[0:3] + [("T", 0)] + PLAIN[3:5] + [("T", 1)] + PLAIN[5:8]

        def pool_splits(r, small):
            return BIG < r < ROUTED if is_int(r) else small

        def order(blocks_fn, engine):
            blocks_fn(0, 0, PLAIN, 0)
            blocks_fn(1, 1, PLAIN, 0)
            with engine.Fori(0, SHARED // 2 - 2) as m:
                for i in range(2):
                    blocks_fn(m * 2 + 2 + i, i, PLAIN, 0)
            blocks_fn(SHARED - 2, 0, PLAIN, 0)
            blocks_fn(SHARED - 1, 1, WITH_T, 0, r_next=0)
            blocks_fn(SHARED, 0, WITH_T, 2, r=0, r_next=1)
            blocks_fn(SHARED + 1, 1, WITH_T, 0, r=1, r_next=2)
            for first, rounds, small in ((2, (BIG - 3) // 2, False), (BIG + 1, (SMALL - 3) // 2, True)):
                with engine.Fori(0, rounds) as m:
                    for i in range(2):
                        r = m * 2 + first + i
                        blocks_fn(r + SHARED, i, WITH_T, 2 * (1 - i), r=r, r_next=r + 1, small=small)
                for r in (first + 2 * rounds, first + 2 * rounds + 1):
                    more = r < ROUTED - 1
                    blocks_fn(r + SHARED, r % 2, WITH_T if more else PLAIN, 2 * (1 - r % 2), r=r, r_next=r + 1 if more else None)

        @block.sync
        def _(sp):
            def parts(n, i):
                src = XHL[bass.ds(n, 1)].rearrange("b p (q n) -> (b p) q n", q=2)
                for q, dst in enumerate((xh, xl)):
                    sp.dma_start(dst[i][:, :, :].bitcast(F32).rearrange("p k n -> p (k n)"), src[:, q, :]).then_inc(ld_xT[i], 16)

            parts(0, 0)
            sp.dma_start(cst[:, :], a["route"]).then_inc(ld_c, 16)
            sp.dma_start(tri[:, :, :], a["tri"]).then_inc(ld_c, 16)
            parts(1, 1)
            sp.dma_start(rows[:, :, 0:D], x1_view).then_inc(ld_rows, 16)
            with sp.Fori(1, SHARED // 2) as m:
                for i in range(2):
                    sp.wait_ge(fc_mm, (m * 2 + i - 1) * KH)
                    parts(m * 2 + i, i)
            sp.wait_ge(own_rd, 1)

            def expert(r, i, small=False):
                e = sp.value_load(owner[0:1, bass.ds(r, 1)], min_val=0, max_val=NE - 1)
                w = a["wall"][bass.ds(e, 1)].rearrange("e p a n -> (e p) a n")
                for c in range(2):
                    need(sp, w_rd[c], r * 4)
                    sp.dma_start(wstage[:, c, :], w[:, c, :]).then_inc(ld_w[c], 16)
                    if c == 0:
                        if is_int(r) and r == 0:
                            for k in range(2):
                                sp.wait_ge(sent[k], 16 * NT)
                        need(sp, t_mm, r * 2)
                        need(sp, meta_rd, r)
                        nt = size(r, small)
                        src = xs_view[0][bass.ds(r, 1)] if nt == ST else xs_view[1][bass.ds(r - BIG, 1)]
                        sp.dma_start(xb[:, 0:nt, :], src.rearrange("r p t w -> (r p) t w")).then_inc(ld_xb, 16)
                sp.wait_ge(h_ev, (r + SHARED - 1) * KH)
                sp.dma_start(bfc[i][:, :], a["bfc"][bass.ds(e, 1)].rearrange("e p n -> (e p) n")).then_inc(ld_b[i], 16)
                sp.dma_start(bpj_raw[i][:, :], a["bproj"][bass.ds(e, 1)].rearrange("e p n -> (e p) n")).then_inc(ld_b[i], 16)

            expert(0, 0)
            expert(1, 1)
            for first, rounds, small in ((2, (BIG - 3) // 2, False), (BIG + 1, (SMALL - 3) // 2, True)):
                with sp.Fori(0, rounds) as m:
                    for i in range(2):
                        expert(m * 2 + first + i, i, small)
                for r in (first + 2 * rounds, first + 2 * rounds + 1):
                    expert(r, r % 2)

            sp.wait_ge(y_out, 16 * UNITS * HT)

            def results(b, i, k):
                src = yy_view[k].rearrange("p (b t) d -> b p t d", t=TT)[bass.ds(b, 1)].rearrange("b p t d -> (b p) t d")
                sp.dma_start(pairs[i][:, k * TT * D:(k + 1) * TT * D].rearrange("p (t d) -> p t d", t=TT), src).then_inc(ld_y[i], 16)

            for i in range(PAIRS):
                for k in range(2):
                    results(i, i, k)
            with sp.Fori(1, B // PAIRS) as m:
                for i in range(PAIRS):
                    before = (m - 1) * PAIRS + i
                    sp.wait_ge(yy_rd, before + 1)
                    results(m * PAIRS + i, i, 1)
                    sp.wait_ge(o_rd, (before + 1) * TT)
                    results(m * PAIRS + i, i, 0)
            sp.wait_ge(o_out, 16 * B)

        @block.gpsimd
        def _(pool):
            for k in range(2):
                if k == 0:
                    pool.wait_ge(own_rd, 1)
                    pool.wait_ge(ld_rows, 16)
                else:
                    pool.wait_ge(sent[0], 16 * NT)
                nc.gpsimd.tensor_scalar(rows[:, :, D], cst[:, TOK:TOK + NT], 1.0, float(k * N), ALU.mult, ALU.add)
                nc.gpsimd.tensor_scalar(rows[:, :, D + 1], cnt[:, 4 + k, :], 1.0, 0.0, ALU.mult, ALU.add).then_inc(rows_rd, 1)
                pool.wait_ge(rows_rd, k + 1)
                for t in range(NT):
                    pool.indirect_dma_start(XS, bass.IndirectOffsetOnAxis(pos[k][:, t:t + 1].bitcast(U32), 0),
                                            rows[:, t, :], None).then_inc(sent[k], 16)

            def scatter(r, i):
                for t in range(size(r, False)):
                    pool.wait_ge(y_ev, tiles(r, False) + t + 1)
                    pool.indirect_dma_start(YY, bass.IndirectOffsetOnAxis(dest[i][:, t:t + 1].bitcast(U32), 0), y[:, t, :], None,
                                            bounds_check=2 * N - 1, oob_is_err=False).then_inc(y_out, 16)

            def weights_hi(r, c):
                pool.wait_ge(ld_w[c], r * 16 + 16)
                pool.wait_ge((fc_mm, pj_mm)[c], (r + SHARED - 1) * KH)
                w = (wfc, wpj)[c][r % 2][0][:].rearrange("p k n -> p (k n)")
                n = KD * HID // 4
                for q in range(4):
                    cols = slice(q * n, (q + 1) * n)
                    nc.gpsimd.tensor_scalar(w[:, cols], wstage[:, c, cols], 1.0, 0.0, ALU.mult, ALU.add).then_inc(whi_rd[c], 1)

            for r in range(ROUTED):
                if pool_splits(r + 2, False):
                    weights_hi(r + 2, 0)
                scatter(r, r % 2)
                if pool_splits(r + 2, False):
                    weights_hi(r + 2, 1)

            with pool.Fori(0, B // PAIRS) as m:
                for i in range(PAIRS):
                    pool.wait_ge(ld_y[i], m * 32 + 32)
                    nc.gpsimd.tensor_tensor(pairs[i][:, 0:TT * D], pairs[i][:, 0:TT * D], pairs[i][:, TT * D:], ALU.add).then_inc(yy_rd, 1)

        @block.scalar
        def _(act):
            def y_results(r, i, small=False):
                act.wait_ge(pj_mm, (r + SHARED + 1) * KH)
                act.wait_ge(meta_rd, r + 1)
                need(act, y_out, tiles(r, small) * 16)
                for t in range(size(r, small)):
                    nc.scalar.activation(y[:, t, :], yb[i][t // 2][:, t % 2 * D:t % 2 * D + D], ACT.Copy,
                                         scale=gate[i][:, t:t + 1]).then_inc(y_ev, 1)

            def tokens(n, i, plan, bank0, r=None, r_next=None, small=False):
                for k, (kind, j) in enumerate(plan):
                    b = fcb[(bank0 + k) % 4]
                    cols = slice(0, P * (ST if r is None else size(r, small)))
                    if kind == "T":
                        act.wait_ge(t_mm, r_next * 2 + j + 1)
                        cols = slice(0, size(r_next, small) * P)
                        nc.scalar.activation(xh[1 - i][:, j, cols], b[:, cols], ACT.Copy).then_inc(xh_rd, 1)
                        continue
                    if j == 0 and r is not None:
                        act.wait_ge(ld_b[i], (r - i) * 16 + 32)
                    act.wait_ge(fc_mm, n * KH + j + 1)
                    need(act, hl_rd, n * KH + j - 1)
                    nc.scalar.activation(h[j % 2][:, cols], b[:, cols], ACT.Gelu_apprx_tanh,
                                         bias=bfc[1 if r is None else i][:, j:j + 1]).then_inc(h_ev, 1)
                    act.wait_ge(h_ev, n * KH + j + 1)
                    need(act, pj_mm, n * KH + j + 1 - RING)
                    nc.scalar.activation(hh[j % RING][:, cols], h[j % 2][:, cols], ACT.Copy).then_inc(hh_rd, 1)
                    if is_int(n) and n == 0 and j == 0:
                        act.wait_ge(d_rd, 1)
                        nc.scalar.activation(rt[1][:, :, :], rt[0][:, :, :], ACT.Exp).then_inc(e_rd, 1)
                    if j == 2 and r is not None and not (is_int(r) and r == 0):
                        y_results(r - 1, 1 - i, small)

            order(tokens, act)
            y_results(ROUTED - 1, (ROUTED - 1) % 2)

            with act.Fori(0, B // PAIRS) as m:
                for i in range(PAIRS):
                    b = m * PAIRS + i
                    act.wait_ge(st_rd, m * (PAIRS // 2) + i // 2 + 1)
                    for t in range(TT):
                        at = bass.ds(b * TT + t, 1)
                        nc.scalar.activation(acc[:, at, :].rearrange("p o d -> p (o d)"), pairs[i][:, t * D:(t + 1) * D],
                                             ACT.Identity, scale=rs[:, at], bias=mean[:, at]).then_inc(o_rd, 1)
                    act.wait_ge(o_rd, b * TT + TT)
                    act.dma_start(out_view[bass.ds(b, 1)].rearrange("b p t d -> (b p) t d"),
                                  acc[:, bass.ds(b * TT, TT), :]).then_inc(o_out, 16)

        @block.vector
        def _(dve):
            link = Links(dve, dve_own)
            tt, ts, stt, red = nc.vector.tensor_tensor, nc.vector.tensor_scalar, nc.vector.scalar_tensor_tensor, nc.vector.tensor_reduce
            per_expert = lambda ap: ap.rearrange("p (e t) -> p e t", e=1).to_broadcast([P, NE, NT])
            per_token = lambda ap: ap.rearrange("p (e t) -> p e t", t=1).to_broadcast([P, NE, NT])
            over_experts = lambda ap: ap.rearrange("p e t -> p t e")

            def shifted_logits():
                link(red(cnt[:, 0, :], logits[:, :, :], AX, ALU.max))
                tt(rt[0][:, :, :], logits[:, :, :].rearrange("p t e -> p e t"), per_expert(cnt[:, 0, :]), ALU.subtract).then_inc(d_rd, 1)

            def probabilities():
                dve.wait_ge(e_rd, 1)
                link(red(cnt[:, 1, :], over_experts(rt[1][:, :, :]), AX, ALU.add))
                link(nc.vector.reciprocal(cnt[:, 1, :], cnt[:, 1, :]))
                link(tt(rt[0][:, :, :], rt[1][:, :, :], per_expert(cnt[:, 1, :]), ALU.mult))

            def choose(k):
                link(red(cnt[:, 2 + k, :], over_experts(rt[0][:, :, :]), AX, ALU.max))
                link(tt(rt[2][:, :, :], rt[0][:, :, :], per_expert(cnt[:, 2 + k, :]), ALU.is_equal))
                link(tt(rt[2][:, :, :], rt[2][:, :, :], per_token(cst[:, KEY:KEY + NE]), ALU.mult))
                link(red(cnt[:, 6, :], over_experts(rt[2][:, :, :]), AX, ALU.max))
                link(tt(choice[k][:, :, :], rt[2][:, :, :], per_expert(cnt[:, 6, :]), ALU.is_equal))
                if k == 0:
                    link(stt(rt[0][:, :, :], choice[0][:, :, :], -2.0, rt[0][:, :, :], ALU.mult, ALU.add))

            def gates():
                tt(both[:, :], choice[0][:, :, :].rearrange("p e t -> p (e t)"), choice[1][:, :, :].rearrange("p e t -> p (e t)"),
                   ALU.add).then_inc(both_rd, 1)
                link(tt(cnt[:, 7, :], cnt[:, 2, :], cnt[:, 3, :], ALU.add))
                link(nc.vector.reciprocal(cnt[:, 7, :], cnt[:, 7, :]))
                for k in range(2):
                    last = tt(cnt[:, 4 + k, :], cnt[:, 2 + k, :], cnt[:, 7, :], ALU.mult)
                link(last)

            def counts():
                dve.wait_ge(cum_mm, 1)
                c = yb[1][0]
                nc.vector.tensor_copy(rt[3][:, :, :].rearrange("p e t -> p (e t)"), c[:, 0:NE * NT])
                link(nc.vector.tensor_copy(rt[1][:, :, :].rearrange("p e t -> p (e t)"), c[:, NE * NT:]))
                nc.vector.tensor_copy(cnt[:, 6, 0:1], rt[1][:, 0, 0:1]).then_inc(cum_rd, 1)
                link(nc.vector.tensor_tensor_scan(rt[2][:, :, :].rearrange("p e t -> p (e t)"), cst[:, GO_ON:GO_ON + NE * NT],
                                                  rt[1][:, :, :].rearrange("p e t -> p (e t)"), 0.0, ALU.mult, ALU.add))

            def starts():
                halves = small_t[:, 0:NE * MOST].rearrange("p (e k) -> p e k", k=MOST)
                over = small_t[:, 0:NE * NE].rearrange("p (e k) -> p e k", k=NE)
                before = cst[:, BEFORE:BEFORE + NE * NE].rearrange("p (e k) -> p e k", k=NE)
                total = rt[2][:, :, NT - 1]
                link(tt(halves, total.rearrange("p (e k) -> p e k", k=1).to_broadcast([P, NE, MOST]),
                        cst[:, FULL:FULL + MOST].rearrange("p (e k) -> p e k", e=1).to_broadcast([P, NE, MOST]), ALU.is_gt))
                red(n_small[:, :], halves, AX, ALU.add)
                link(red(n_big[:, :], halves[:, :, MOST // 2:], AX, ALU.add))
                for n, first in ((n_big, start_big), (n_small, start_small)):
                    link(tt(over, n[:, :].rearrange("p (e k) -> p e k", e=1).to_broadcast([P, NE, NE]), before, ALU.mult))
                    link(red(first[:, :], over, AX, ALU.add))
                    if n is n_big:
                        link(tt(n[:, :], n[:, :], first[:, :], ALU.add))
                        ts(n[:, :], n[:, :], float(BIG), None, ALU.min)
                        link(ts(first[:, :], first[:, :], float(BIG), None, ALU.min))
                        link(tt(n[:, :], n[:, :], first[:, :], ALU.subtract))
                        link(stt(n_small[:, :], n[:, :], -2.0, n_small[:, :], ALU.mult, ALU.add))

            def slots():
                link(tt(rt[2][:, :, :], rt[2][:, :, :], rt[1][:, :, :], ALU.subtract))
                link(tt(rt[2][:, :, :], rt[2][:, :, :], rt[3][:, :, :], ALU.add))
                link(stt(rt[1][:, :, :], per_token(n_big[:, :]), -float(S), rt[2][:, :, :], ALU.mult, ALU.add))
                link(ts(rt[3][:, :, :], rt[1][:, :, :], 0.0, None, ALU.is_ge))
                link(stt(rt[1][:, :, :], per_token(start_small[:, :]), float(HS), rt[1][:, :, :], ALU.mult, ALU.add))
                link(stt(rt[2][:, :, :], per_token(start_big[:, :]), float(S), rt[2][:, :, :], ALU.mult, ALU.add))
                link(ts(rt[1][:, :, :], rt[1][:, :, :], 1.0, float(BIG * S), ALU.mult, ALU.add))
                link(tt(rt[1][:, :, :], rt[1][:, :, :], rt[2][:, :, :], ALU.subtract))
                link(tt(rt[1][:, :, :], rt[1][:, :, :], rt[3][:, :, :], ALU.mult))
                link(tt(rt[2][:, :, :], rt[2][:, :, :], rt[1][:, :, :], ALU.add))
                for k in range(2):
                    link(tt(rt[k][:, :, :], choice[k][:, :, :], rt[2][:, :, :], ALU.mult))
                for k in range(2):
                    last = red(cnt[:, 6 + k, :], over_experts(rt[k][:, :, :]), AX, ALU.add)
                link(last)
                for k in range(2):
                    last = nc.vector.tensor_copy(pos[k][:, :], cnt[:, 6 + k, :])
                link(last)

            def owners():
                for k, (lo, n, first) in enumerate(((0, BIG, start_big), (BIG, SMALL, start_small))):
                    cmp = small_t[:, 0:n * NE].rearrange("p (r e) -> p r e", e=NE)
                    link(tt(cmp, cst[:, BLOCK:BLOCK + n].rearrange("p (r k) -> p r k", k=1).to_broadcast([P, n, NE]),
                            first[:, :].rearrange("p (r k) -> p r k", r=1).to_broadcast([P, n, NE]), ALU.is_ge))
                    link(red(owner_f[:, lo:lo + n], cmp, AX, ALU.add))
                ts(owner[:, :], owner_f[:, :], -1.0, None, ALU.add).then_inc(own_rd, 1)

            def split_piece(r, i, piece, small):
                c, q = piece // 4, piece % 4
                n = KD * HID // 4
                if q == 0:
                    dve.wait_ge(ld_w[c], r * 16 + 16)
                    dve.wait_ge((fc_mm, pj_mm)[c], (r + SHARED - 1) * KH)
                w = [p[:].rearrange("p k n -> p (k n)")[:, q * n:(q + 1) * n] for p in (wfc, wpj)[c][i]]
                src = wstage[:, c, q * n:(q + 1) * n]
                if pool_splits(r, small):
                    dve.wait_ge(whi_rd[c], (r - BIG - 1) * 4 + q + 1)
                else:
                    link(nc.vector.tensor_copy(w[0], src))
                tt(w[1], src, w[0].bitcast(F32), ALU.subtract).then_inc(w_rd[c], 1)

            def slots_meta(r, i, small):
                dve.wait_ge(ld_xb, r * 16 + 16)
                need(dve, y_out, tiles(r - 1, small) * 16)
                nt = size(r, small)
                nc.vector.tensor_copy(dest[i][:, 0:nt], xb[:, 0:nt, D])
                nc.vector.tensor_copy(gate[i][:, 0:nt], xb[:, 0:nt, D + 1]).then_inc(meta_rd, 1)
                dve.wait_ge(ld_b[i], (r - i) * 16 + 32)
                link(nc.vector.tensor_copy(row_h[:, 0:D], bpj_raw[i][:, :]))
                link(tt(row_t[:, 0:D], bpj_raw[i][:, :], row_h[:, 0:D].bitcast(F32), ALU.subtract))
                link(ts(row_t[:, 0:D], row_t[:, 0:D], mask2[:, 1:2], None, ALU.mult))
                stt(bpj[i][:, :], row_h[:, 0:D].bitcast(F32), mask2[:, 0:1], row_t[:, 0:D], ALU.mult, ALU.add).then_inc(bpj_rd, 1)

            beside = {(0, 0): lambda: (shifted_logits(), probabilities()), (0, 1): lambda: choose(0),
                      (0, 2): lambda: choose(1), (0, 3): gates,
                      (1, 0): counts, (1, 2): starts, (1, 3): slots, (1, 4): owners}

            def tokens(n, i, plan, bank0, r=None, r_next=None, small=False):
                for k, (kind, j) in enumerate(plan):
                    cols = slice(0, P * (ST if r is None else size(r, small)))
                    if kind == "T":
                        cols = slice(0, size(r_next, small) * P)
                        dve.wait_ge(xh_rd, r_next * 2 + j + 1)
                        tt(xl[1 - i][:, j, cols], fcb[(bank0 + k) % 4][:, cols], xh[1 - i][:, j, cols].bitcast(F32), ALU.subtract).then_inc(xl_rd, 1)
                        continue
                    dve.wait_ge(hh_rd, n * KH + j + 1)
                    tt(hl[j % RING][:, cols], h[j % 2][:, cols], hh[j % RING][:, cols].bitcast(F32), ALU.subtract).then_inc(hl_rd, 1)
                    if is_int(n) and (n, j) in beside:
                        beside[n, j]()
                    if j == 2 and (r is None or (is_int(r) and r == 0)) and not (is_int(n) and n == 0):
                        dve.wait_ge(pj_mm, n * KH)
                        if is_int(n) and n == 1:
                            dve.wait_ge(ld_rows, 16)
                        for t in range(ST):
                            tok = bass.ds((n - 1) * ST + t, 1)
                            tt(acc[:, tok, :].rearrange("p o d -> p (o d)"), yb[1 - i][t // 2][:, t % 2 * D:t % 2 * D + D],
                               rows[:, tok, 0:D].rearrange("p o d -> p (o d)"), ALU.add).then_inc(acc_rd, 1)
                    if r_next is not None:
                        split_piece(r_next, 1 - i, j, small)
                if r_next is not None:
                    slots_meta(r_next, 1 - i, small)

            dve.wait_ge(ld_c, 32)
            nc.vector.tensor_copy(trib[:, :, :], tri[:, :, :]).then_inc(tri_rd, 1)

            def counted(n, *args, **kw):
                if is_int(n):
                    if link.loop:
                        link.end(loop_steps.pop(0))
                    tokens(n, *args, **kw)
                else:
                    first = 2 if kw.get("r") is None else SHARED + (BIG + 1 if kw["small"] else 2)
                    link.enter(n, first, 0 if kw.get("r") is None else SMALL_LINKS if kw["small"] else BLOCK_LINKS)
                    tokens(n, *args, **kw)
                    link.leave()

            loop_steps = [SHARED - 4, BIG - 3, SMALL - 3]
            order(counted, dve)

            def total(pair, i):
                for k in range(2):
                    b = pair * 2 + k
                    dve.wait_ge(yy_rd, b + 1)
                    both_rows = pairs[i + k][:, 0:TT * D]
                    tt(both_rows, both_rows, acc[:, bass.ds(b * TT, TT), :].rearrange("p t d -> p (t d)"), ALU.add).then_inc(tot_rd, 1)
                for k in range(2):
                    dve.wait_ge(tot_rd, pair * 2 + k + 1)
                    for t in range(TT):
                        last = nc.vector.bn_stats(st[:, k * TT + t, :], pairs[i + k][:, t * D:(t + 1) * D])
                link(last)
                moments(nc, link, st[:, :, :], m_now[:, :], var[:, :], tmp[:, :])
                rsqrt(nc, link, r_now[:, :], half[:, :], var[:, :], tmp[:, :])
                now = bass.ds(pair * 2 * TT, 2 * TT)
                nc.vector.tensor_copy(rs[:, now], r_now[:, :])
                stt(mean[:, now], m_now[:, :], -1.0, r_now[:, :], ALU.mult, ALU.mult).then_inc(st_rd, 1)
                dve.wait_ge(st_rd, pair + 1)

            with dve.Fori(0, B // PAIRS) as m:
                for i in range(0, PAIRS, 2):
                    pair = m * (PAIRS // 2) + i // 2
                    link.enter(pair, 0, PAIR_LINKS)
                    total(pair, i)
                    link.leave()

        @block.tensor
        def _(pe):
            mm = nc.tensor.matmul

            def project(n, i, j, r, small):
                w = 1 if r is None else i
                pe.wait_ge(hl_rd, n * KH + j + 1)
                if j == 0:
                    if r is not None:
                        pe.wait_ge(bpj_rd, r + 1)
                        pe.wait_ge(w_rd[1], (r + 1) * 4)
                    if r is None or (is_int(r) and r < 2):
                        need(pe, acc_rd, (n - 1) * ST)
                    else:
                        pe.wait_ge(y_ev, tiles(r - 1, small))
                    if is_int(n) and n == 1:
                        pe.wait_ge(cum_rd, 1)
                for t in range(ST if r is None else size(r, small)):
                    o = yb[i][t // 2][:, t % 2 * D:t % 2 * D + D]
                    cols = slice(t * P, (t + 1) * P)
                    if j == 0:
                        mm(o, ones2[:, :], bpj[w][:, :], start=t % 2 == 0, stop=False, skip_group_check=True)
                    hs = (hh[j % RING], hl[j % RING], hh[j % RING])
                    for p, ws in enumerate((1, 0, 0)):
                        last = mm(o, hs[p][:, cols], wpj[w][ws][:, j, :], start=False,
                                  stop=j == KH - 1 and p == 2, skip_group_check=True)
                last.then_inc(pj_mm, 1)

            def tokens(n, i, plan, bank0, r=None, r_next=None, small=False):
                w = 1 if r is None else i
                first = is_int(n) and n == 0
                before = PLAIN if r is None else WITH_T
                for k, (kind, j) in enumerate(plan):
                    if k >= 4:
                        okind, oj = plan[k - 4]
                        if okind == "fc":
                            pe.wait_ge(h_ev, n * KH + oj + 1)
                        else:
                            pe.wait_ge(xl_rd, r_next * 2 + oj + 1)
                    elif not first:
                        okind, oj = before[k - 4]
                        if okind == "fc":
                            pe.wait_ge(h_ev, (n - 1) * KH + oj + 1)
                        else:
                            pe.wait_ge(xl_rd, r * 2 + oj + 1)
                    b = fcb[(bank0 + k) % 4]
                    if kind == "T":
                        if j == 0:
                            pe.wait_ge(ld_xb, r_next * 16 + 16)
                        for t in range(size(r_next, small)):
                            last = nc.tensor.transpose(b[:, t * P:(t + 1) * P], xb[:, t, j * P:(j + 1) * P], ident[:, :])
                        last.then_inc(t_mm, 1)
                        continue
                    if j == 0:
                        if r is None:
                            pe.wait_ge(ld_xT[i], (n - i) * 16 + 32)
                        else:
                            pe.wait_ge(xl_rd, r * 2 + 2)
                            pe.wait_ge(w_rd[0], (r + 1) * 4)
                    rows_ = slice(j * P, (j + 1) * P)
                    cols = slice(0, P * (ST if r is None else size(r, small)))
                    for c in range(KD):
                        for p, (ws, xs) in enumerate(((0, xl), (1, xh), (0, xh))):
                            last = mm(b[:, cols], wfc[w][ws][:, c, rows_], xs[i][:, c, cols], start=c == 0 and p == 0,
                                      stop=c == KD - 1 and p == 2)
                    last.then_inc(fc_mm, 1)
                    if j >= 2:
                        project(n, i, j - 2, r, small)
                    elif not first:
                        if r is None:
                            project(n - 1, 1 - i, KH - 2 + j, None, small)
                        else:
                            project(n - 1, 1 - i, KH - 2 + j, None if is_int(r) and r == 0 else r - 1, small)
                if first:
                    pe.wait_ge(both_rd, 1)
                    pe.wait_ge(tri_rd, 1)
                    c = yb[1][0]
                    mm(c[:, 0:NE * NT], trib[:, 0, :], both[:, :], start=True, stop=True)
                    mm(c[:, NE * NT:], trib[:, 1, :], both[:, :], start=True, stop=True).then_inc(cum_mm, 1)

            order(tokens, pe)
            for j in (KH - 2, KH - 1):
                project(SHARED + ROUTED - 1, (ROUTED - 1) % 2, j, ROUTED - 1, False)


KEY = 0
MOST = N // HS
FULL = KEY + NE
BEFORE = FULL + MOST
BLOCK = BEFORE + NE * NE
TOK = BLOCK + BIG
GO_ON = TOK + NT


def constants():
    route = np.zeros((P, GO_ON + NE * NT), np.float32)
    route[:, KEY:KEY + NE] = NE - np.arange(NE)
    route[:, FULL:FULL + MOST] = HS * np.concatenate([np.arange(0, MOST, 2), np.arange(1, MOST, 2)])
    route[:, BEFORE:BEFORE + NE * NE] = np.tril(np.ones((NE, NE)), -1).reshape(-1)
    route[:, BLOCK:BLOCK + BIG] = np.arange(BIG)
    route[:, TOK:TOK + NT] = np.arange(P)[:, None] + P * np.arange(NT)
    route[:, GO_ON:] = (np.arange(NE * NT) % NT != 0)
    tri = np.stack([np.triu(np.ones((P, P)), 1), np.ones((P, P))], 1).astype(np.float32)
    half = QK // 2
    freq = np.float32(10000.0) ** (-np.arange(half, dtype=np.float32) / np.float32(half))
    angle = (np.arange(T, dtype=np.float32)[:, None] * freq[None, :]).T.astype(np.float64)
    cos, sin = np.cos(angle), np.sin(angle)
    rope = np.stack([np.concatenate([cos] * 4), np.concatenate([-sin, sin] * 2)], 1).astype(np.float32)
    empty = np.zeros((P, ROW), np.float32)
    empty[:, D] = NOWHERE
    return {"route": route, "tri": tri, "rope": rope, "empty": empty, "ident": np.eye(P, dtype=np.float32),
            "ones": np.ones((2, P), np.float32), "mask2": np.eye(2, dtype=np.float32)}


def layout(i):
    f = {k: np.asarray(v) for k, v in i.items()}
    A, F = "L0_attn_", "L0_ffn_"
    halves = lambda x: np.concatenate([x[..., QK // 2:], x[..., :QK // 2]], -1)
    twice = lambda x, y: np.stack([np.concatenate([x, y]), np.concatenate([halves(x), halves(y)])], 1)
    chunks = lambda x: x.reshape(-1, P, x.shape[-1]).transpose(1, 0, 2)
    g, be, bqk = f[A + "gamma"], f[A + "beta"], f[A + "bqk"]
    vec = np.concatenate([twice(bqk, bqk), twice(g[0], g[1]), twice(g[2], g[3]), twice(be[0], be[1]), twice(be[2], be[3]),
                          f[A + "ln1_w"].reshape(KD, P).T, f[A + "ln1_b"].reshape(KD, P).T, f[A + "bg"].reshape(KE, P).T], 1)
    wqk = f[A + "Wqk"].T
    wqk = np.stack([chunks(np.concatenate([w, w], 1)) for w in (wqk, halves(wqk))], 1)
    rows = np.zeros((2, 2, E), np.float32)
    rows[:, 0, :] = f[A + "bv"]
    rows[:, 1, 0:D] = f[A + "bo"]
    pe = f[A + "pos_emb"]
    far = np.repeat(pe[MAX_REL:MAX_REL + 1], G - 1 - MAX_REL)
    ext = np.concatenate([far, pe[MAX_REL:0:-1], pe[0:MAX_REL + 1], far])
    wall = np.stack([np.stack([chunks(a).reshape(P, -1), chunks(b).reshape(P, -1)], 1)
                     for a, b in [*zip(f[F + "Wfc"], f[F + "Wproj"]), (f[F + "Wfc_s"], f[F + "Wproj_s"])]])
    bfc = np.concatenate([f[F + "bfc"], f[F + "bfc_s"][None]]).reshape(NE + 1, KH, P).transpose(0, 2, 1)
    bproj = np.repeat(np.concatenate([f[F + "bproj"], f[F + "bproj_s"][None]])[:, None, :], 2, 1)
    return {"x": f[A + "x"].reshape(N, D), "vec": vec, "wqk": wqk, "wv": chunks(f[A + "Wv"].T), "wg": chunks(f[A + "Wg"].T),
            "wo": chunks(f[A + "Wo"].T), "rows": rows, "ext": np.tile(ext, G),
            "ln2": np.repeat(np.stack([f[A + "ln2_w"], f[A + "ln2_b"]])[None], P, 0), "wr": chunks(f[F + "Wr"]),
            "wall": wall, "bfc": bfc, "bproj": bproj}


def kernel(**inputs):
    import concourse.bacc as bacc
    from concourse.bass_utils import run_bass_kernel_spmd

    nc = bacc.Bacc("TRN2", target_bir_lowering=False, num_devices=1)
    arrays = {k: np.ascontiguousarray(v) for k, v in {**layout(inputs), **constants()}.items()}
    aps = {k: nc.dram_tensor(k, v.shape, mybir.dt.from_np(v.dtype), kind="ExternalInput").ap() for k, v in arrays.items()}
    out = nc.dram_tensor("out", (N, D), F32, kind="ExternalOutput").ap()
    build(nc, aps, out)
    r = run_bass_kernel_spmd(nc, [arrays], core_ids=[0])
    return r.results[0]["out"].reshape(B, T, D)
```

```python
from contextlib import ExitStack

import numpy as np

import concourse.bass as bass
from concourse import mybir

F32 = mybir.dt.float32
F32R = mybir.dt.float32r
BF16 = mybir.dt.bfloat16
I32 = mybir.dt.int32
U32 = mybir.dt.uint32
ALU = mybir.AluOpType
ACT = mybir.ActivationFunctionType
AX = mybir.AxisListType.X

P = 128
B, T, D = 8, 512, 256
N = B * T
QK = 64
E = 512
G = 64
MAX_REL = 32
HID = 1024
NE = 8
KD = D // P
KE = E // P
KH = HID // P
TT = T // P
NT = N // P
S = 512
ST = S // P
HS = S // 2
HT = HS // P
SHARED = N // S
FIRST = SHARED - 2
UNITS = (2 * N - NE) // HS + NE
BIG = (UNITS - NE) // 2
SMALL = UNITS - 2 * BIG
assert SMALL >= NE
ROUTED = BIG + SMALL
assert ROUTED % 2 == 0
SLOTS = UNITS * HS
ROW = D + 2
NOWHERE = float(4 * N)
EPS = 1e-5
LO = 32
BR = LO + 1
RSQRT_SEED = float(0x5F3759DF)
BQK, GQ, GK, BQ, BK, L1W, L1B, BG = 0, 2, 4, 6, 8, 10, 12, 14
NVEC = 18


def is_int(n):
    return isinstance(n, int)


def size(r, small):
    return HT if (r >= BIG if is_int(r) else small) else ST


def tiles(r, small):
    if r >= BIG if is_int(r) else small:
        return BIG * (ST - HT) + r * HT
    return r * ST


def need(engine, sem, n):
    if not is_int(n) or n > 0:
        engine.wait_ge(sem, n)


class Links:

    def __init__(self, engine, sem):
        self.engine, self.sem, self.base, self.k, self.loop = engine, sem, 0, 0, None

    def __call__(self, instruction):
        self.k += 1
        instruction.then_inc(self.sem, 1)
        self.engine.wait_ge(self.sem, self.base + self.k)

    def total(self):
        return self.base + self.k

    def at(self, base):
        self.base, self.k = base, 0

    def enter(self, step, first, per_step):
        if not self.loop:
            self.loop = (self.total(), per_step)
        self.at(self.loop[0] + (step - first) * per_step)

    def leave(self):
        assert self.k == self.loop[1], (self.k, self.loop)

    def end(self, steps):
        self.at(self.loop[0] + steps * self.loop[1])
        self.loop = None


def rsqrt(nc, link, y, half, v, tmp):
    link(nc.vector.tensor_single_scalar(half, v.bitcast(I32), 1, ALU.logical_shift_right))
    link(nc.vector.tensor_scalar(y.bitcast(I32), half, -1.0, RSQRT_SEED, ALU.mult, ALU.add))
    for _ in range(3):
        link(nc.vector.tensor_tensor(tmp, y, y, ALU.mult))
        link(nc.vector.scalar_tensor_tensor(tmp, tmp, -0.5, v, ALU.mult, ALU.mult))
        link(nc.vector.scalar_tensor_tensor(y, tmp, 1.5, y, ALU.add, ALU.mult))


def moments(nc, link, st, mean, var, tmp):
    part = lambda i: st[:, :, i]
    nc.vector.tensor_tensor(mean, part(1), part(4), ALU.add)
    nc.vector.tensor_tensor(tmp, part(1), part(4), ALU.subtract)
    link(nc.vector.tensor_tensor(var, part(2), part(5), ALU.add))
    nc.vector.tensor_scalar(mean, mean, 0.5, None, ALU.mult)
    nc.vector.scalar_tensor_tensor(tmp, tmp, 0.25, tmp, ALU.mult, ALU.mult)
    link(nc.vector.tensor_scalar(var, var, 1.0 / D, EPS, ALU.mult, ALU.add))
    link(nc.vector.tensor_tensor(var, var, tmp, ALU.add))


def build(nc, a, out):
    ctx = ExitStack()

    def sem(name):
        return ctx.enter_context(nc.semaphore(name))

    XHL = nc.dram_tensor("x1_parts", (B, P, 2 * KD * T), F32, kind="Internal").ap()
    X1D = nc.dram_tensor("x1_rows", (N, D), F32, kind="Internal").ap()
    XS = nc.dram_tensor("slot_rows", (SLOTS, ROW), F32, kind="Internal").ap()
    YY = nc.dram_tensor("expert_results", (2 * N, D), F32, kind="Internal").ap()

    with ctx:
        keep = lambda n, s, t: ctx.enter_context(nc.sbuf_tensor("k_" + n, s, t))
        ident = keep("ident", [P, P], F32)
        ones = keep("ones", [BR, P], F32R)
        logits = keep("logits", [P, NT, NE], F32)
        wstage = keep("wstage", [P, 2, KD * HID], F32)
        SHW = 1 - FIRST % 2
        wfc1 = [keep(f"wfc1{p}", [P, KD, HID], F32R) for p in "hl"]
        wpj1 = [keep(f"wpj1{p}", [P, KH, D], F32R) for p in "hl"]
        bfc = [keep(f"bfc{i}", [P, KH], F32) for i in range(2)]
        bpj_raw = [keep(f"bpj_raw{i}", [BR, D], F32) for i in range(2)]
        bpj = [keep(f"bpj{i}", [BR, D], F32R) for i in range(2)]
        xTh, xTl = [keep(f"xT{p}", [P, KD, T], F32R) for p in "hl"]
        uh = keep("uh", [P, KE, T], F32R)
        ld_xT = [sem(f"parts_loaded{i}") for i in range(2)]
        fc_mm, h_ev, hh_rd, hl_rd, pj_mm = (sem(n) for n in ("fc_product", "h_ready", "hh_ready", "hl_ready", "proj_product"))
        bank = [ctx.enter_context(nc.psum_tensor(f"bank{i}", [P, 512], F32)) for i in range(8)]

        attention(nc, a, locals())
        experts(nc, a, out, locals())


def attention(nc, a, shared):
    ident, ones, logits = (shared[k] for k in ("ident", "ones", "logits"))
    wstage, wfc1, wpj1, bpj_raw, bpj = (shared[k] for k in ("wstage", "wfc1", "wpj1", "bpj_raw", "bpj"))
    xTh, xTl, uh, ld_xT = (shared[k] for k in ("xTh", "xTl", "uh", "ld_xT"))
    fc_mm, h_ev, hh_rd, hl_rd, pj_mm, bank = (shared[k] for k in ("fc_mm", "h_ev", "hh_rd", "hl_rd", "pj_mm", "bank"))
    bfc, SHW = shared["bfc"], shared["SHW"]
    XHL, X1D, XS = shared["XHL"], shared["X1D"], shared["XS"]
    with ExitStack() as ctx:
        sb = lambda n, s, t=F32: ctx.enter_context(nc.sbuf_tensor("s_" + n, s, t))
        sem = lambda n: ctx.enter_context(nc.semaphore(n))
        pair = lambda n, s: [sb(n + p, s, F32R) for p in "hl"]

        vec = sb("vec", [P, NVEC])
        rope = sb("rope", [P, 2, T])
        offs = sb("offs", [P, 2, T])
        bias = sb("bias", [P, G])
        ln2 = sb("ln2", [P, 2, D])
        wr = sb("wr", [P, KD, NE])
        wqk, wv, wg, wo = (pair(n, s) for n, s in (("wqk", [P, 2, KD, P]), ("wv", [P, KD, E]),
                                                   ("wg", [P, KD, E]), ("wo", [P, KE, D])))
        wrh, wrl = pair("wr", [P, KD, NE])
        bv2 = sb("bv2", [BR, E], F32R)
        bo2 = sb("bo2", [BR, D], F32R)
        ones_raw = sb("ones_raw", [BR, P])
        empty = sb("empty", [P, ROW])
        x_in = sb("x_in", [P, TT, D])
        x_res = sb("x_res", [P, TT, D])
        xn = sb("xn", [P, TT, D])
        xT = sb("xT", [P, KD, T])
        v = sb("v", [P, TT, E])
        qk = sb("qk", [P, 2, T])
        qkr = sb("qkr", [P, 2, T])
        heads = sb("heads", [P, 2, T])
        kT = sb("kT", [P, TT, P])
        att = sb("att", [P, TT, P])
        kvh, kvl = pair("kv", [P, E])
        lq = sb("lq", [P, T], F32R)
        u = sb("u", [P, KE, T])
        ul = sb("ul", [P, KE, T], F32R)
        z = sb("z", [P, TT, D])
        lgT = sb("lgT", [P, T])
        x1 = sb("x1", [P, TT, D])
        x1T = sb("x1T", [P, KD, T])
        x1h, x1l = pair("x1", [P, KD, T])
        st = sb("st", [P, 2 * TT, 6])
        mean = sb("mean", [P, 2 * TT])
        var, rs, tmp = sb("var", [P, 2 * TT]), sb("rs", [P, 2 * TT]), sb("tmp", [P, 2 * TT])
        half = sb("half", [P, 2 * TT], I32)
        raw = wstage[:, :, :].rearrange("p a n -> p (a n)")
        raw_v, raw_g = raw[:, 0:1024].rearrange("p (k n) -> p k n", k=KD), raw[:, 1024:2048].rearrange("p (k n) -> p k n", k=KD)
        raw_qk = raw[:, 2048:2560].rearrange("p (s k n) -> p s k n", s=2, k=KD)
        raw_o = raw[:, 2560:3584].rearrange("p (k n) -> p k n", k=KE)

        e_h = [xT[:, k, :] for k in range(KD)]
        e_hh, e_hl = ([w[i][:, k, :] for i in range(2) for k in range(KD)] for w in (wg, wv))
        raw_bv, raw_bo = raw[0:BR, 3584:3584 + E], shared["bpj_raw"][1 - SHW]


        ld_v0, ld_c0, ld_c1, ld_c = sem("norm_consts_loaded"), sem("bias_rows_loaded"), sem("rope_loaded"), sem("consts_loaded")
        ld_w = [sem(f"{n}_loaded") for n in ("wv", "wqk", "wg", "wo")]
        ld_x, ld_r = sem("x_loaded"), sem("residual_loaded")
        ld_s = sem("shared_weights_loaded")
        filled = sem("slots_emptied")
        wh_rd, wl_rd, split_s = sem("weights_hi_ready"), sem("weights_lo_ready"), sem("shared_weights_split")
        dve_own = sem("vector_own")
        xn_ready, xT_mm, xT_ev, xTh_rd, xTl_rd = (sem(n) for n in ("xn_ready", "xT_transposed", "xT_evacuated", "xTh_ready", "xTl_ready"))
        v_mm, v_ev, q_mm, q_ev, qkr_rd, heads_rd = (sem(n) for n in ("v_product", "v_ready", "qk_product", "qk_ready", "qk_roped", "heads_ready"))
        o_mm, o_ev, g_mm, g_ev = (sem(n) for n in ("o_product", "o_evacuated", "gate_product", "gate_ready"))
        lqh_rd, lql_rd, lq_rd, kvl_rd = (sem(n) for n in ("lin_q_hi_ready", "lin_q_lo_ready", "lin_q_lo_moved", "kv_lo_ready"))
        kT_mm, kT_ev, sc_mm, att_rd, kv_mm, kv_ev = (sem(n) for n in ("kT_transposed", "kT_ready", "scores_product", "att_ready", "kv_product", "kv_ready"))
        u_mm, u_ml, uh_rd, ul_rd = (sem(n) for n in ("u_product", "u_gated", "uh_ready", "ul_ready"))
        res_rd, res_used, x1_rd, x1T_mm, x1T_ev, lt_mm, lt_ev, lg_mm, lg_ev = (sem(n) for n in (
            "residual_ready", "residual_used", "x1_ready", "x1T_transposed", "x1T_evacuated", "logits_product", "logits_evacuated",
            "logits_transposed", "logits_ready"))
        x1h_rd, x1l_rd, sh_st, x1_st = (sem(n) for n in ("x1h_ready", "x1l_ready", "parts_stored", "x1_stored"))
        tab_rd, z_scaled = sem("tables_ready"), sem("z_scaled")

        block = ctx.enter_context(nc.Block())
        x_view = a["x"].rearrange("(b t p) d -> b p t d", b=B, p=P)
        x1_view = X1D.rearrange("(b t p) d -> b p t d", b=B, p=P)

        EMPTYINGS = B - 2
        EMPTY_ROWS = SLOTS // P // EMPTYINGS
        assert EMPTY_ROWS * EMPTYINGS * P == SLOTS
        CONSTS = 7

        def stages(b):
            is_main, ahead = (not is_int(b) or b < B), (not is_int(b) or b < B - 1)
            return is_main, ahead, not is_int(b) or 1 <= b <= B, not is_int(b) or 2 <= b <= B + 1

        def steps(engine, step, last_in_loop=B - 1, end=B + 2):
            for b in range(3):
                step(b)
            with engine.Fori(3, last_in_loop) as b:
                step(b)
            for b in range(last_in_loop, end):
                step(b)

        def bidx(ap, b):
            return ap[bass.ds(b, 1)].rearrange("b p t d -> (b p) t d")

        weights, raws = (wv, wqk, wg, wo), (raw_v, raw_qk, raw_g, raw_o)

        @block.sync
        def _(sp):
            sp.dma_start(x_in[:, :, :], bidx(x_view, 0)).then_inc(ld_x, 16)
            def load(done, *pairs):
                for dst, src in pairs:
                    sp.dma_start(dst, src).then_inc(done, 16)

            load(ld_v0, (vec[:, :], a["vec"]), (ident[:, :], a["ident"]))
            load(ld_w[0], (raw_v, a["wv"]))
            load(ld_c0, (raw_bv, a["rows"][:, 0, :]), (raw_bo[:, :], a["rows"][:, 1, 0:D]), (ones_raw[:, :], a["ones"]))
            load(ld_w[1], (raw_qk, a["wqk"]))
            load(ld_c1, (rope[:, :, :], a["rope"]))
            load(ld_w[2], (raw_g, a["wg"]))
            sp.wait_ge(xn_ready, 1)
            sp.dma_start(x_in[:, :, :], bidx(x_view, 1)).then_inc(ld_x, 16)
            load(ld_w[3], (raw_o, a["wo"]))
            load(ld_c, (ln2[:, :, :], a["ln2"]), (wr[:, :, :], a["wr"]), (empty[:, :], a["empty"]),
                 (bfc[SHW][:, :], a["bfc"][NE]), (bpj_raw[SHW][:, :], a["bproj"][NE]))
            skew = a["ext"][G - 1:G - 1 + (2 * G - 2) * G].rearrange("(j n) -> j n", n=2 * G - 2)[:, 0:G]
            for h in range(2):
                sp.dma_start(bias[h * G:(h + 1) * G, :], skew).then_inc(ld_c, 16)

            def first_parts(n):
                done, dst = (((g_mm, 4 * B), (xTh[:, :, :], xTl[:, :, :])), ((o_mm, 2 * B), (uh[:, 0:KD, :], uh[:, KD:, :])))[n]
                sp.wait_ge(*done)
                sp.wait_ge(sh_st, 32 * (B - 2))
                for q in range(2):
                    sp.dma_start(dst[q].bitcast(F32), XHL[n].rearrange("p (q k n) -> q p k n", q=2, k=KD)[q]).then_inc(ld_xT[n], 16)

            def step(b):
                main, ahead, o, last = stages(b)
                if is_int(b) and b >= B:
                    first_parts(b - B)
                if o:
                    need(sp, res_used, b - 1)
                    sp.dma_start(x_res[:, :, :], bidx(x_view, b - 1)).then_inc(ld_r, 16)
                c = b - 2
                if last:
                    sp.wait_ge(x1_rd, c + 1)
                    sp.dma_start(bidx(x1_view, c), x1[:, :, :]).then_inc(x1_st, 16)
                if ahead:
                    sp.wait_ge(xn_ready, b + 2)
                    if not is_int(b) or b + 2 < B:
                        sp.dma_start(x_in[:, :, :], bidx(x_view, b + 2)).then_inc(ld_x, 16)
                if main:
                    sp.wait_ge(lql_rd, b + 1)
                    sp.dma_start(lq[0:QK, :].bitcast(F32), qkr[QK:P, 1, :]).then_inc(lq_rd, 16)
                if last:
                    dst = XHL[bass.ds(c, 1)].rearrange("b p n -> (b p) n")
                    sp.wait_ge(x1h_rd, 2 * c + 2)
                    sp.dma_start(dst[:, 0:KD * T], x1h[:, :, :].bitcast(F32).rearrange("p k n -> p (k n)")).then_inc(sh_st, 16)
                    sp.wait_ge(x1l_rd, 2 * c + 2)
                    sp.dma_start(dst[:, KD * T:], x1l[:, :, :].bitcast(F32).rearrange("p k n -> p (k n)")).then_inc(sh_st, 16)
                if is_int(b) and b == 0:
                    sp.wait_ge(ld_c, 16 * CONSTS)
                if not is_int(b) or b < EMPTYINGS:
                    dst = XS.rearrange("(q p r) w -> q p r w", p=P, r=EMPTY_ROWS)[bass.ds(b, 1)].rearrange("q p r w -> (q p) r w")
                    sp.dma_start(dst, empty[:, :].rearrange("p (o w) -> p o w", o=1).to_broadcast([P, EMPTY_ROWS, ROW])).then_inc(filled, 16)
                if is_int(b) and b == 0:
                    sp.wait_ge(wl_rd, 4)
                    sp.dma_start(wstage[:, :, :], a["wall"][NE]).then_inc(ld_s, 16)

            steps(sp, step, B - 2)
            sp.wait_ge(x1_st, 16 * B)
            sp.wait_ge(sh_st, 32 * B)
            sp.wait_ge(filled, 16 * EMPTYINGS)

        @block.gpsimd
        def _(pool):
            nc.gpsimd.memset(lgT[:, :], 0.0)
            nc.gpsimd.memset(att[:, :, :], 0.0).then_inc(tab_rd, 1)
            pool.wait_ge(ld_s, 16)
            for c in range(2):
                w = (wfc1, wpj1)[c]
                src = wstage[:, c, :].rearrange("p (k n) -> p k n", k=w[0].shape[1])
                nc.gpsimd.tensor_scalar(w[0][:, :, :], src, 1.0, 0.0, ALU.mult, ALU.add).then_inc(split_s, 1)
                pool.wait_ge(split_s, 2 * c + 1)
                nc.gpsimd.tensor_tensor(w[1][:, :, :], src, w[0][:, :, :].bitcast(F32), ALU.subtract).then_inc(split_s, 1)

            def step(b):
                pool.wait_ge(ld_r, 16 * (b + 1))
                nc.gpsimd.tensor_tensor(x_res[:, :, :], x_res[:, :, :],
                                        ln2[:, 1:2, :].to_broadcast([P, TT, D]), ALU.add).then_inc(res_rd, 1)
                if is_int(b):
                    return
                pool.wait_ge(o_ev, 4 * b + 4)
                nc.gpsimd.tensor_tensor(z[:, :, :], z[:, :, :], ln2[:, 0:1, :].to_broadcast([P, TT, D]), ALU.mult).then_inc(z_scaled, 1)
                pool.wait_ge(res_rd, b + 1)
                pool.wait_ge(z_scaled, b + 1)
                nc.gpsimd.tensor_tensor(z[:, :, :], z[:, :, :], x_res[:, :, :], ALU.add).then_inc(res_used, 1)

            pool.wait_ge(ld_c, 16 * CONSTS)
            with pool.Fori(0, B - 1) as b:
                step(b)
            step(B - 1)
            pool.wait_ge(split_s, 4)

        @block.scalar
        def _(act):
            copy = lambda o, i: nc.scalar.activation(o, i, ACT.Copy)
            def weights_hi(n):
                act.wait_ge(ld_w[n], 16)
                copy(weights[n][0][:], raws[n]).then_inc(wh_rd, 1)

            def x_transposed(b):
                for c in range(KD):
                    act.wait_ge(xT_mm, 2 * b + c + 1)
                    nc.scalar.activation(xT[:, c, :], bank[(7, 0)[c]][:, :], ACT.Identity, scale=vec[:, L1W + c:L1W + c + 1],
                                         bias=vec[:, L1B + c:L1B + c + 1]).then_inc(xT_ev, 1)
                for c in range(KD):
                    act.wait_ge(xT_ev, 2 * b + c + 1)
                    copy(xTh[:, c, :], xT[:, c, :]).then_inc(xTh_rd, 1)

            def expert_chunk(j):
                act.wait_ge(fc_mm, j + 1)
                need(act, hl_rd, j - 1)
                nc.scalar.activation(e_h[j % 2], bank[j % 2][:, :], ACT.Gelu_apprx_tanh, bias=bfc[SHW][:, j:j + 1]).then_inc(h_ev, 1)
                act.wait_ge(h_ev, j + 1)
                need(act, pj_mm, j - 3)
                copy(e_hh[j % 4], e_h[j % 2]).then_inc(hh_rd, 1)

            def beside(*chunks):
                for j in chunks:
                    expert_chunk(j)

            def step(b):
                main, ahead, o, last = stages(b)
                at = lambda n: is_int(b) and b == n

                def keys():
                    act.wait_ge(heads_rd, 2 * b + 2)
                    copy(lq[QK:P, :], heads[QK:P, 0, :]).then_inc(lqh_rd, 1)
                    act.wait_ge(kT_mm, b + 1)
                    copy(kT[:, :, :].rearrange("p t (o n) -> p t o n", o=2),
                         bank[4][:, :].rearrange("p (t o n) -> p t o n", t=TT, o=2)[:, :, 1:2, :].to_broadcast([P, TT, 2, QK])).then_inc(kT_ev, 1)

                if main:
                    for t in range(TT):
                        act.wait_ge(v_mm, 4 * b + t + 1)
                        nc.scalar.activation(v[:, t, :], bank[t][:, :], ACT.Silu).then_inc(v_ev, 1)
                if at(B + 2):
                    beside(7)
                if not is_int(b) or b >= 3:
                    act.wait_ge(lg_mm, b - 2)
                    copy(logits[:, bass.ds((b - 3) * TT, TT), :], bank[7][:, :].rearrange("p (t n) -> p t n", t=TT)[:, :, 0:NE]).then_inc(lg_ev, 1)
                if main:
                    for s in range(2):
                        act.wait_ge(q_mm, 2 * b + s + 1)
                        need(act, qkr_rd, 2 * (b - 1) + s + 1)
                        nc.scalar.activation(qk[:, s, :], bank[4 + s][:, :], ACT.Silu,
                                             bias=vec[:, BQK + s:BQK + s + 1]).then_inc(q_ev, 1)
                    if is_int(b) and b == 0:
                        for m in range(KE):
                            act.wait_ge(g_mm, 4 * b + m + 1)
                            nc.scalar.activation(u[:, m, :], bank[m][:, :], ACT.Silu,
                                                 bias=vec[:, BG + m:BG + m + 1]).then_inc(g_ev, 1)
                        keys()
                    else:
                        keys()
                        for m in range(KE):
                            act.wait_ge(g_mm, 4 * b + m + 1)
                            nc.scalar.activation(u[:, m, :], bank[m][:, :], ACT.Silu,
                                                 bias=vec[:, BG + m:BG + m + 1]).then_inc(g_ev, 1)
                    act.wait_ge(kv_mm, b + 1)
                    nc.scalar.activation(kvh[:, :], bank[6][:, :], ACT.Copy, scale=1.0 / T).then_inc(kv_ev, 1)
                if ahead:
                    x_transposed(b + 1)
                c = b - 2
                if at(B):
                    beside(0, 1)
                if last:
                    for k in range(KD):
                        act.wait_ge(x1T_mm, 2 * c + k + 1)
                        need(act, x1l_rd, 2 * (c - 1) + k + 1)
                        copy(x1T[:, k, :], bank[4 + k][:, :]).then_inc(x1T_ev, 1)
                    need(act, sh_st, 32 * c)
                    for k in range(KD):
                        act.wait_ge(x1T_ev, 2 * c + k + 1)
                        copy(x1h[:, k, :], x1T[:, k, :]).then_inc(x1h_rd, 1)
                if main:
                    for m in range(KE):
                        act.wait_ge(u_ml, 4 * b + m + 1)
                        copy(uh[:, m, :], u[:, m, :]).then_inc(uh_rd, 1)
                if at(B):
                    beside(2)
                if at(B + 1):
                    beside(6)
                if last:
                    act.wait_ge(lt_mm, c + 1)
                    copy(lgT[0:NE, :], bank[7][0:NE, :]).then_inc(lt_ev, 1)
                if at(B):
                    beside(3, 4, 5)

            weights_hi(0)
            act.wait_ge(ld_v0, 32)
            x_transposed(0)
            for n in (1, 2, 3):
                weights_hi(n)
            steps(act, step, end=B + 3)

        @block.vector
        def _(dve):
            link = Links(dve, dve_own)
            tt = nc.vector.tensor_tensor
            stt = nc.vector.scalar_tensor_tensor

            def norm(o, i, k):
                return nc.vector.tensor_scalar(o, i, mean[:, k:k + 1], rs[:, k:k + 1], ALU.subtract, ALU.mult)

            def rstd(lo, hi):
                moments(nc, link, st[:, lo:hi, :], mean[:, lo:hi], var[:, lo:hi], tmp[:, lo:hi])
                rsqrt(nc, link, rs[:, lo:hi], half[:, lo:hi], var[:, lo:hi], tmp[:, lo:hi])

            def stats(tiles, k, wait=None):
                for t, ap in enumerate(tiles):
                    if wait:
                        wait(t)
                    last = nc.vector.bn_stats(st[:, k + t, :], ap)
                link(last)

            def x_normed(b):
                need(dve, xT_mm, 2 * b)
                for t in range(TT):
                    last = norm(xn[:, t, :], x_in[:, t, :], t)
                last.then_inc(xn_ready, 1)

            def xT_rest(b):
                for c in range(KD):
                    dve.wait_ge(xTh_rd, 2 * b + c + 1)
                    tt(xTl[:, c, :], xT[:, c, :], xTh[:, c, :].bitcast(F32), ALU.subtract).then_inc(xTl_rd, 1)

            def bias_rows(dst, src):
                link(nc.vector.tensor_copy(dst, src))
                tt(dst[LO:BR], src[LO:BR], dst[LO:BR].bitcast(F32), ALU.subtract).then_inc(tab_rd, 1)

            def beside(*chunks):
                for j in chunks:
                    dve.wait_ge(hh_rd, j + 1)
                    tt(e_hl[j % 4], e_h[j % 2], e_hh[j % 4].bitcast(F32), ALU.subtract).then_inc(hl_rd, 1)

            def step(b):
                main, ahead, o, last = stages(b)
                at = lambda n: is_int(b) and b == n
                c = b - 2
                if last:
                    if is_int(c) and c == B - 1:
                        dve.wait_ge(o_ev, 4 * B)
                        link(tt(z[:, :, :], z[:, :, :], ln2[:, 0:1, :].to_broadcast([P, TT, D]), ALU.mult))
                        dve.wait_ge(res_rd, B)
                        tt(z[:, :, :], z[:, :, :], x_res[:, :, :], ALU.add).then_inc(res_used, 1)
                    dve.wait_ge(res_used, c + 1)
                    stats([z[:, t, :] for t in range(TT)], TT)
                if ahead:
                    dve.wait_ge(ld_x, 16 * (b + 2))
                    stats([x_in[:, t, :] for t in range(TT)], 0)
                if at(B + 1):
                    beside(3)
                if ahead or last:
                    rstd(0 if ahead else TT, 2 * TT if last else TT)
                if at(B + 1):
                    beside(4)
                if last:
                    need(dve, x1_st, 16 * c)
                    for t in range(TT):
                        last_i = norm(x1[:, t, :], z[:, t, :], TT + t)
                    last_i.then_inc(x1_rd, 1)
                if at(B + 1):
                    beside(5)
                if main:
                    for s in range(2):
                        dve.wait_ge(q_ev, 2 * b + s + 1)
                        last_i = tt(qkr[:, s, :], qk[:, s, :], rope[:, s, :], ALU.mult)
                        last_i.then_inc(qkr_rd, 1)
                    dve.wait_ge(qkr_rd, 2 * b + 1)
                    stt(heads[:, 0, :], qkr[:, 0, :], vec[:, GQ:GQ + 1], offs[:, 0, :], ALU.mult, ALU.add)
                    link(stt(heads[:, 1, :], qkr[:, 0, :], vec[:, GK:GK + 1], offs[:, 1, :], ALU.mult, ALU.add))
                    dve.wait_ge(qkr_rd, 2 * b + 2)
                    stt(heads[:, 1, :], qkr[:, 1, :], vec[:, GK + 1:GK + 2], heads[:, 1, :], ALU.mult, ALU.add).then_inc(heads_rd, 1)
                    stt(heads[:, 0, :], qkr[:, 1, :], vec[:, GQ + 1:GQ + 2], heads[:, 0, :], ALU.mult, ALU.add).then_inc(heads_rd, 1)
                if o:
                    yo = [bank[6 + t // 2][:, t % 2 * D:t % 2 * D + D] for t in range(TT)]
                    stats(yo, TT, lambda t: t % 2 or dve.wait_ge(o_mm, 2 * (b - 1) + t // 2 + 1))
                    rstd(TT, 2 * TT)
                    for t in range(TT):
                        norm(z[:, t, :], yo[t], TT + t).then_inc(o_ev, 1)
                if ahead:
                    x_normed(b + 1)
                if main:
                    dve.wait_ge(lqh_rd, b + 1)
                    tt(qkr[QK:P, 1, :], heads[QK:P, 0, :], lq[QK:P, :].bitcast(F32), ALU.subtract).then_inc(lql_rd, 1)
                    if is_int(b) and b == 0:
                        dve.wait_ge(ld_c, 16 * CONSTS)
                    dve.wait_ge(sc_mm, b + 1)
                    sc = bank[5][:, :].rearrange("p (t n) -> p t n", t=TT)
                    for g in range(P // G):
                        r = slice(g * G, (g + 1) * G)
                        last_i = stt(att[r, :, r], sc[r, :, r], 1.0 / G,
                                     bias[r, :].rearrange("p (o n) -> p o n", o=1).to_broadcast([G, TT, G]), ALU.mult, ALU.add)
                    link(last_i)
                    for g in range(P // G):
                        r = slice(g * G, (g + 1) * G)
                        last_i = stt(att[r, :, r], att[r, :, r], 0.0, att[r, :, r], ALU.max, ALU.mult)
                    last_i.then_inc(att_rd, 1)
                    dve.wait_ge(kv_ev, b + 1)
                    stt(kvl[QK:P, :], bank[6][QK:P, :], 1.0 / T, kvh[QK:P, :].bitcast(F32), ALU.mult, ALU.subtract).then_inc(kvl_rd, 1)
                if ahead:
                    xT_rest(b + 1)

                def x1_rest():
                    for k in range(KD):
                        dve.wait_ge(x1h_rd, 2 * c + k + 1)
                        tt(x1l[:, k, :], x1T[:, k, :], x1h[:, k, :].bitcast(F32), ALU.subtract).then_inc(x1l_rd, 1)

                def rest(m):
                    dve.wait_ge(uh_rd, 4 * b + m + 1)
                    tt(ul[:, m, :], u[:, m, :], uh[:, m, :].bitcast(F32), ALU.subtract).then_inc(ul_rd, 1)

                if main:
                    for m in range(KE):
                        dve.wait_ge(u_mm, 4 * b + m + 1)
                        tt(u[:, m, :], u[:, m, :], bank[1 + m][:, :], ALU.mult).then_inc(u_ml, 1)
                        if m:
                            rest(m - 1)
                        elif last:
                            x1_rest()
                    rest(KE - 1)
                elif last:
                    if at(B):
                        beside(0, 1)
                    x1_rest()
                    beside(*((2,) if at(B) else (6, 7)))

            dve.wait_ge(ld_x, 16)
            stats([x_in[:, t, :] for t in range(TT)], 0)
            rstd(0, TT)
            x_normed(0)

            def weights_lo(n):
                dve.wait_ge(wh_rd, n + 1)
                tt(weights[n][1][:], raws[n], weights[n][0][:].bitcast(F32), ALU.subtract).then_inc(wl_rd, 1)

            weights_lo(0)
            dve.wait_ge(ld_c0, 48)
            nc.vector.tensor_copy(ones[:, :], ones_raw[:, :])
            bias_rows(bv2[:, :], raw_bv)
            xT_rest(0)
            weights_lo(1)
            weights_lo(2)
            dve.wait_ge(ld_v0, 32)
            dve.wait_ge(ld_c1, 16)
            for k, c in enumerate((BQ, BK)):
                link(nc.vector.tensor_scalar(offs[:, k, :], rope[:, 0, :], vec[:, c:c + 1], None, ALU.mult))
                link(stt(offs[:, k, :], rope[:, 1, :], vec[:, c + 1:c + 2], offs[:, k, :], ALU.mult, ALU.add))
            step(0)
            weights_lo(3)
            bias_rows(bo2[:, :], raw_bo[:, :])
            dve.wait_ge(ld_c, 16 * CONSTS)
            bias_rows(bpj[SHW][:, :], bpj_raw[SHW][:, :])
            link(nc.vector.tensor_copy(wrh[:, :, :], wr[:, :, :]))
            tt(wrl[:, :, :], wr[:, :, :], wrh[:, :, :].bitcast(F32), ALU.subtract).then_inc(tab_rd, 1)
            step(1)
            step(2)
            with dve.Fori(3, B - 1) as b:
                link.enter(b, 3, STEP_LINKS)
                step(b)
                link.leave()
            link.end(B - 4)
            for b in range(B - 1, B + 2):
                step(b)

        @block.tensor
        def _(pe):
            mm, tr = nc.tensor.matmul, nc.tensor.transpose

            def three(o, wh, wl, xh, xl, start, stop):
                mm(o, wh, xl, start=start, stop=False)
                mm(o, wl, xh, start=False, stop=False)
                return mm(o, wh, xh, start=False, stop=stop)

            def transposes(src, banks, done):
                for c in range(KD):
                    for t in range(TT):
                        last = tr(bank[banks[c]][:, t * P:(t + 1) * P], src[:, t, c * P:(c + 1) * P], ident[:, :])
                    last.then_inc(done, 1)

            def fc(j):
                if j == 0:
                    pe.wait_ge(ld_xT[0], 32)
                    pe.wait_ge(split_s, 4)
                    pe.wait_ge(tab_rd, 5)
                need(pe, h_ev, j - 1)
                rows = slice(j * P, (j + 1) * P)
                for k in range(KD):
                    last_i = three(bank[j % 2][:, :], wfc1[0][:, k, rows], wfc1[1][:, k, rows], xTh[:, k, :], xTl[:, k, :],
                                   k == 0, k == KD - 1)
                last_i.then_inc(fc_mm, 1)

            def proj(j):
                pe.wait_ge(hl_rd, j + 1)
                for t in range(TT):
                    out = bank[2 + t // 2][:, t % 2 * D:t % 2 * D + D]
                    cols = slice(t * P, (t + 1) * P)
                    if j == 0:
                        mm(out, ones[:, :], bpj[SHW][:, :], start=t % 2 == 0, stop=False, skip_group_check=True)
                    for p, (hs, w) in enumerate(((e_hh, 1), (e_hl, 0), (e_hh, 0))):
                        last_i = mm(out, hs[j % 4][:, cols], wpj1[w][:, j, :], start=False, stop=j == KH - 1 and p == 2,
                                    skip_group_check=True)
                last_i.then_inc(pj_mm, 1)

            def beside(*chunks):
                for j in chunks:
                    fc(j)
                    if j >= 2:
                        proj(j - 2)

            def step(b):
                main, ahead, o, last = stages(b)
                c = b - 2
                at = lambda n: is_int(b) and b == n
                if at(B + 2):
                    fc(KH - 1)
                if main:
                    if at(0):
                        pe.wait_ge(wl_rd, 1)
                    pe.wait_ge(xTh_rd, 2 * b + 2)
                    pe.wait_ge(xTl_rd, 2 * b + 2)
                    for t in range(TT):
                        if t:
                            need(pe, u_ml, 4 * (b - 1) + t)
                        cols = slice(t * P, (t + 1) * P)
                        mm(bank[t][:, :], ones[:, :], bv2[:, :], start=True, stop=False)
                        for k in range(KD):
                            last_i = three(bank[t][:, :], xTh[:, k, cols], xTl[:, k, cols], wv[0][:, k, :], wv[1][:, k, :],
                                           False, k == KD - 1)
                        last_i.then_inc(v_mm, 1)
                if not is_int(b) or b >= 3:
                    pe.wait_ge(lt_ev, b - 2)
                    for t in range(TT):
                        last_i = tr(bank[7][:, t * P:(t + 1) * P], lgT[:, t * P:(t + 1) * P], ident[:, :])
                    last_i.then_inc(lg_mm, 1)
                if main:
                    for s in range(2):
                        if at(0):
                            pe.wait_ge(wl_rd, 2)
                        if s == 0:
                            need(pe, u_ml, 4 * b)
                        else:
                            need(pe, x1T_ev, 2 * (c - 1) + 2)
                        for k in range(KD):
                            last_i = three(bank[4 + s][:, :], wqk[0][:, s, k, :], wqk[1][:, s, k, :], xTh[:, k, :], xTl[:, k, :],
                                           k == 0, k == KD - 1)
                        last_i.then_inc(q_mm, 1)
                if o:
                    if at(1):
                        pe.wait_ge(wl_rd, 4)
                        pe.wait_ge(tab_rd, 3)
                    pe.wait_ge(ul_rd, 4 * b)
                    for t in range(TT):
                        if t == 2:
                            need(pe, lg_ev, c)
                        cols = slice(t * P, (t + 1) * P)
                        out = bank[6 + t // 2][:, t % 2 * D:t % 2 * D + D]
                        mm(out, ones[:, :], bo2[:, :], start=True, stop=False)
                        for m in range(KE):
                            last_i = three(out, uh[:, m, cols], ul[:, m, cols], wo[0][:, m, :], wo[1][:, m, :], False, m == KE - 1)
                        if t % 2:
                            last_i.then_inc(o_mm, 1)

                def keys_and_scores():
                    pe.wait_ge(heads_rd, 2 * b + 1)
                    for t in range(TT):
                        last_i = tr(bank[4][:, t * P:(t + 1) * P], heads[:, 1, t * P:(t + 1) * P], ident[:, :])
                    last_i.then_inc(kT_mm, 1)
                    pe.wait_ge(heads_rd, 2 * b + 2)
                    for t in range(TT):
                        cols = slice(t * P, (t + 1) * P)
                        last_i = mm(bank[5][:, cols], heads[0:QK, 1, cols], heads[0:QK, 0, cols], start=True, stop=True)
                    last_i.then_inc(sc_mm, 1)

                def gate():
                    if at(0):
                        pe.wait_ge(wl_rd, 3)
                    for m in range(KE):
                        pe.wait_ge(v_ev, 4 * b + m + 1)
                        rows = slice(m * P, (m + 1) * P)
                        for k in range(KD):
                            last_i = three(bank[m][:, :], wg[0][:, k, rows], wg[1][:, k, rows], xTh[:, k, :], xTl[:, k, :],
                                           k == 0, k == KD - 1)
                        last_i.then_inc(g_mm, 1)

                if main:
                    for stage in (gate, keys_and_scores) if at(0) else (keys_and_scores, gate):
                        stage()
                    pe.wait_ge(kT_ev, b + 1)
                    need(pe, o_ev, 4 * (b - 1) + 2)
                    for t in range(TT):
                        last_i = mm(bank[6][:, :], kT[:, t, :], v[:, t, :], start=t == 0, stop=t == TT - 1)
                    last_i.then_inc(kv_mm, 1)
                if ahead:
                    pe.wait_ge(xn_ready, b + 2)
                    need(pe, o_ev, 4 * b)
                    pe.wait_ge(g_ev, 4 * b + 1)
                    transposes(xn, (7, 0), xT_mm)
                if main:
                    pe.wait_ge(att_rd, b + 1)
                if at(B):
                    beside(0, 1)
                if last:
                    pe.wait_ge(x1_rd, c + 1)
                    if not main:
                        pe.wait_ge(x1T_ev, 2 * c)
                    transposes(x1, (4, 5), x1T_mm)
                if main:
                    pe.wait_ge(kvl_rd, b + 1)
                    pe.wait_ge(lq_rd, 16 * b + 16)
                    for m in range(KE):
                        if m < 3:
                            pe.wait_ge(g_ev, 4 * b + m + 2)
                        elif last:
                            pe.wait_ge(x1T_ev, 2 * c + 1)
                        rows = slice(m * P, (m + 1) * P)
                        out = bank[1 + m]
                        mm(out[:, :], kvh[:, rows], lq[:, :], start=True, stop=False)
                        mm(out[:, :], kvl[QK:P, rows], lq[QK:P, :], start=False, stop=False)
                        for t in range(TT):
                            cols = slice(t * P, (t + 1) * P)
                            last_i = mm(out[:, cols], v[:, t, rows], att[:, t, :], start=False, stop=t == TT - 1)
                        last_i.then_inc(u_mm, 1)
                if at(B):
                    beside(2)
                if at(B + 1):
                    beside(6)
                if last:
                    if at(2):
                        pe.wait_ge(tab_rd, 5)
                    pe.wait_ge(x1l_rd, 2 * c + 2)
                    if ahead:
                        pe.wait_ge(xT_ev, 2 * (b + 1) + 1)
                    if at(B):
                        pe.wait_ge(o_ev, 4 * B)
                    if at(B + 1):
                        pe.wait_ge(lg_ev, c)
                    for k in range(KD):
                        last_i = three(bank[7][0:NE, :], wrh[:, k, :], wrl[:, k, :], x1h[:, k, :], x1l[:, k, :], k == 0, k == KD - 1)
                    last_i.then_inc(lt_mm, 1)
                if at(B):
                    beside(3, 4, 5)
                if at(B + 2):
                    for j in (5, 6, 7):
                        proj(j)

            pe.wait_ge(ld_v0, 32)
            pe.wait_ge(xn_ready, 1)
            transposes(xn, (7, 0), xT_mm)
            pe.wait_ge(tab_rd, 2)
            steps(pe, step, end=B + 3)


STEP_LINKS, BLOCK_LINKS, SMALL_LINKS = 33, 9, 1


def experts(nc, a, out, shared):
    ident, ones, logits = (shared[k] for k in ("ident", "ones", "logits"))
    wstage, wfc1, wpj1, bfc, bpj_raw, bpj = (shared[k] for k in ("wstage", "wfc1", "wpj1", "bfc", "bpj_raw", "bpj"))
    xTh, xTl, uh, ld_xT = (shared[k] for k in ("xTh", "xTl", "uh", "ld_xT"))
    fc_mm, h_ev, hh_rd, hl_rd, pj_mm, bank = (shared[k] for k in ("fc_mm", "h_ev", "hh_rd", "hl_rd", "pj_mm", "bank"))
    XHL, X1D, XS, YY = (shared[k] for k in ("XHL", "X1D", "XS", "YY"))
    with ExitStack() as ctx:
        sb = lambda n, s, t=F32: ctx.enter_context(nc.sbuf_tensor("s_" + n, s, t))
        sem = lambda n: ctx.enter_context(nc.semaphore(n))

        SHW = shared["SHW"]
        wfc = [[sb(f"wfc0{p}", [P, KD, HID], F32R) for p in "hl"]]
        wpj = [[sb(f"wpj0{p}", [P, KH, D], F32R) for p in "hl"]]
        wfc.insert(SHW, wfc1)
        wpj.insert(SHW, wpj1)
        rows = sb("rows", [P, NT, ROW])
        acc = sb("acc", [P, NT, D])
        xh, xl = [xTh, uh[:, 0:KD, :]], [xTl, uh[:, KD:, :]]
        xb = sb("xb", [P, ST, ROW])
        RING = 4
        h = [sb(f"h{i}", [P, S]) for i in range(2)]
        hh = [sb(f"hh{i}", [P, S], F32R) for i in range(RING)]
        hl = [sb(f"hl{i}", [P, S], F32R) for i in range(RING)]
        y = sb("y", [P, ST, D])
        dest = [sb(f"dest{i}", [P, ST], I32) for i in range(2)]
        gate = [sb(f"gate{i}", [P, ST]) for i in range(2)]
        pairs = [rows[:, :, :].rearrange("p t n -> p (t n)")[:, i * 2 * TT * D:(i + 1) * 2 * TT * D]
                 for i in range(NT * ROW // (2 * TT * D))] + [wstage[:, 0, :], wstage[:, 1, :]]
        PAIRS = len(pairs)
        rt = [y[:, i, :].rearrange("p (e t) -> p e t", e=NE) for i in range(4)]
        choice = [xb[:, i, 0:NE * NT].rearrange("p (e t) -> p e t", e=NE) for i in range(2)]
        both = sb("both", [P, NE * NT], BF16)
        cnt = sb("cnt", [P, 8, NT])
        small_t = sb("small", [P, max(NE * MOST, BIG * NE)])
        n_big, n_small, start_big, start_small = (sb(n, [P, NE]) for n in ("n_big", "n_small", "start_big", "start_small"))
        pos = [sb(f"pos{i}", [P, NT], I32) for i in range(2)]
        owner_f = sb("owner_f", [P, ROUTED])
        owner = sb("owner", [P, ROUTED], I32)
        cst = sb("cst", [P, a["route"].shape[1]])
        tri = sb("tri", [P, 2, P])
        trib = sb("trib", [P, 2, P], BF16)
        st = sb("mst", [P, 2 * TT, 6])
        m_now, r_now, var, tmp = (sb(n, [P, 2 * TT]) for n in ("m_now", "r_now", "mvar", "mtmp"))
        half = sb("mhalf", [P, 2 * TT], I32)
        mean, rs = sb("mmean", [P, NT]), sb("mrs", [P, NT])

        fcb, yb = [bank[i] for i in (0, 1, 4, 5)], [bank[2:4], bank[6:8]]

        ld_tri = sem("masks_loaded")
        ld_c, ld_rows, ld_rows0 = sem("route_consts_loaded"), sem("rows_loaded"), sem("first_rows_loaded")
        ld_acc = sem("acc_loaded")
        ld_w = [sem(f"expert_{n}_loaded") for n in ("fc", "pj")]
        ld_b, ld_xb, ld_y = [sem(f"expert_biases_loaded{i}") for i in range(2)], sem("slots_loaded"), [sem(f"results_loaded{i}") for i in range(PAIRS)]
        whi_rd = [sem(f"expert_{n}_hi_ready") for n in ("fc", "pj")]
        w_rd, bpj_rd = [sem(f"expert_{n}_split") for n in ("fc", "pj")], sem("expert_bias_split")
        t_mm, xh_rd, xl_rd = sem("slots_transposed"), sem("slots_hi_ready"), sem("slots_lo_ready")
        y_ev, y_out = sem("y_evacuated"), sem("results_scattered")
        cum_rd, tri_rd, st_rd = sem("counts_read"), sem("masks_ready"), sem("statistics_ready")
        meta_rd = sem("slots_meta_ready")
        acc_rd = sem("acc_ready")
        e_rd, both_rd, cum_mm, own_rd = sem("exp_ready"), sem("choices_ready"), sem("counts_product"), sem("owners_ready")
        d_rd, rows_rd = sem("logits_shifted"), sem("rows_ready")
        sent = [[sem(f"rows_sent{i}{k}") for k in range(2)] for i in range(2)]
        pos_rd = sem("slots_known")
        dve_own = sem("vector_own2")
        tot_rd, o_rd, o_out = sem("totals_ready"), sem("out_ready"), sem("out_stored")
        yy_rd, all_rd, last_rd = sem("pairs_summed"), sem("rows_summed"), sem("last_row_ready")

        block = ctx.enter_context(nc.Block())
        x1_view = X1D.rearrange("(t p) d -> p t d", p=P)
        xs_view = (XS[0:BIG * S, :].rearrange("(r t p) w -> r p t w", t=ST, p=P),
                   XS[BIG * S:, :].rearrange("(r t p) w -> r p t w", t=HT, p=P))
        yy_view = YY.rearrange("(k t p) d -> k p t d", k=2, p=P)
        out_view = out.rearrange("(b t p) d -> b p t d", b=B, p=P)

        PLAIN = [("fc", j) for j in range(KH)]
        FIRST_T = PLAIN[0:6] + [("T", 0), ("T", 1)] + PLAIN[6:8]
        LATE = range(FIRST + ROUTED, SHARED + ROUTED)
        WITH_T = PLAIN[0:4] + [("T", 0)] + PLAIN[4:6] + [("T", 1)] + PLAIN[6:8]

        def side(r):
            return (r + FIRST) % 2

        def uses(r, i):
            return (r - side(i)) * 16

        def buffer(n, i, r):
            return i if r is not None else side(ROUTED) if late(n) else SHW

        def late(n):
            return is_int(n) and n in LATE

        def pool_splits(r, small):
            return BIG < r <= ROUTED if is_int(r) else small

        PIECES = [("sum", (0, 1)), ("statistics", (0, 1)), ("rstd", (0, 1)), ("statistics", (2, 3)), ("rstd", (2, 3)),
                  ("statistics", (4, 5)), ("rstd", (4, 5)), ("sum", (6,)), ("statistics", (6,)),
                  ("sum", (7,)), ("statistics", (7,)), ("rstd", (6, 7))]
        AFTER = [(-1, 7), (0, 0), (0, 2), (0, 3), (0, 5), (0, 6)]
        SUMS = {(LATE[-1] + n, j): piece for (n, j), piece in zip(AFTER, PIECES)}
        NORMS = {(LATE[-1] + n, j): b for b, (n, j) in enumerate([(0, 6)])}
        POOL_ADDS = (2, 3, 4, 5)

        def order(blocks_fn, engine):
            for n in range(1, FIRST - 1):
                blocks_fn(n, n % 2, PLAIN, 0)
            blocks_fn(FIRST - 1, (FIRST - 1) % 2, FIRST_T, 0, r_next=0)
            blocks_fn(FIRST, side(0), WITH_T, 2, r=0, r_next=1)
            blocks_fn(FIRST + 1, side(1), WITH_T, 0, r=1, r_next=2)
            for first, rounds, small in ((2, (BIG - 3) // 2, False), (BIG + 1, (SMALL - 3) // 2, True)):
                with engine.Fori(0, rounds) as m:
                    for i in range(2):
                        r = m * 2 + first + i
                        blocks_fn(r + FIRST, side(i), WITH_T, 2 * (1 - i), r=r, r_next=r + 1, small=small)
                for r in (first + 2 * rounds, first + 2 * rounds + 1):
                    blocks_fn(r + FIRST, side(r), WITH_T if r < ROUTED - 1 else PLAIN, 2 * (1 - r % 2), r=r, r_next=r + 1)
            for n in LATE:
                blocks_fn(n, n % 2, PLAIN, 0)

        @block.sync
        def _(sp):
            def parts(n, i):
                src = XHL[bass.ds(n, 1)].rearrange("b p (q n) -> (b p) q n", q=2)
                for q, dst in enumerate((xh, xl)):
                    sp.dma_start(dst[i][:, :, :].bitcast(F32).rearrange("p k n -> p (k n)"), src[:, q, :]).then_inc(ld_xT[i], 16)

            sp.dma_start(cst[:, :], a["route"]).then_inc(ld_c, 16)
            sp.dma_start(tri[:, :, :], a["tri"]).then_inc(ld_tri, 16)
            sp.dma_start(rows[:, 0:ST, 0:D], x1_view[:, 0:ST, :]).then_inc(ld_rows0, 16)
            sp.dma_start(rows[:, ST:, 0:D], x1_view[:, ST:, :]).then_inc(ld_rows, 16)
            sp.dma_start(acc[:, FIRST * ST:, :], x1_view[:, FIRST * ST:, :]).then_inc(ld_acc, 16)
            for n in range(2, FIRST):
                sp.wait_ge(fc_mm, (n - 1) * KH)
                parts(n, n % 2)
            sp.wait_ge(own_rd, 1)

            def expert(r, i, small=False):
                e = sp.value_load(owner[0:1, bass.ds(r, 1)], min_val=0, max_val=NE - 1)
                w = a["wall"][bass.ds(e, 1)].rearrange("e p a n -> (e p) a n")
                for c in range(2):
                    need(sp, w_rd[c], r * 4)
                    sp.dma_start(wstage[:, c, :], w[:, c, :]).then_inc(ld_w[c], 16)
                    if c == 0:
                        if is_int(r) and r == 0:
                            for k in range(2):
                                for part in range(2):
                                    sp.wait_ge(sent[k][part], 16 * NT // 2)
                        need(sp, t_mm, r * 2)
                        need(sp, meta_rd, r)
                        nt = size(r, small)
                        src = xs_view[0][bass.ds(r, 1)] if nt == ST else xs_view[1][bass.ds(r - BIG, 1)]
                        sp.dma_start(xb[:, 0:nt, :], src.rearrange("r p t w -> (r p) t w")).then_inc(ld_xb, 16)
                sp.wait_ge(h_ev, (r + FIRST - 1) * KH)
                sp.dma_start(bfc[i][:, :], a["bfc"][bass.ds(e, 1)].rearrange("e p n -> (e p) n")).then_inc(ld_b[i], 16)
                sp.dma_start(bpj_raw[i][:, :], a["bproj"][bass.ds(e, 1)].rearrange("e p n -> (e p) n")).then_inc(ld_b[i], 16)

            expert(0, side(0))
            expert(1, side(1))
            for first, rounds, small in ((2, (BIG - 3) // 2, False), (BIG + 1, (SMALL - 3) // 2, True)):
                with sp.Fori(0, rounds) as m:
                    for i in range(2):
                        expert(m * 2 + first + i, side(i), small)
                for r in (first + 2 * rounds, first + 2 * rounds + 1):
                    expert(r, side(r))

            for c in range(2):
                sp.wait_ge(w_rd[c], ROUTED * 4)
                sp.dma_start(wstage[:, c, :], a["wall"][NE][:, c, :]).then_inc(ld_w[c], 16)
            sp.wait_ge(h_ev, LATE[0] * KH - KH)
            w = side(ROUTED)
            sp.dma_start(bfc[w][:, :], a["bfc"][NE]).then_inc(ld_b[w], 16)
            sp.dma_start(bpj_raw[w][:, :], a["bproj"][NE]).then_inc(ld_b[w], 16)
            for n in LATE:
                sp.wait_ge(fc_mm, (n - 1) * KH)
                parts(n - ROUTED, n % 2)

            sp.wait_ge(y_out, 16 * UNITS * HT)

            for b in range(B):
                for k in (1, 0):
                    if b >= PAIRS:
                        sp.wait_ge(*((o_rd, (b - PAIRS + 1) * TT) if k == 0 else (yy_rd, b - PAIRS + 1)))
                    src = yy_view[k].rearrange("p (b t) d -> b p t d", t=TT)[b]
                    sp.dma_start(pairs[b % PAIRS][:, k * TT * D:(k + 1) * TT * D].rearrange("p (t d) -> p t d", t=TT),
                                 src).then_inc(ld_y[b % PAIRS], 16)
            sp.wait_ge(last_rd, TT)
            sp.dma_start(out_view[B - 1], acc[:, (B - 1) * TT:, :]).then_inc(o_out, 16)
            sp.wait_ge(o_out, 16 * B)

        @block.gpsimd
        def _(pool):
            pool.wait_ge(pos_rd, 1)
            pool.wait_ge(ld_rows0, 16)
            pool.wait_ge(ld_rows, 16)
            for m, (k, part) in enumerate(((0, range(NT)), (1, range(NT // 2)), (1, range(NT // 2, NT)))):
                tiles_ = slice(part.start, part.stop)
                if k:
                    pool.wait_ge(sent[0][m - 1], 16 * len(part))
                nc.gpsimd.tensor_scalar(rows[:, tiles_, D], cst[:, TOK:TOK + NT][:, tiles_], 1.0, float(k * N), ALU.mult, ALU.add)
                nc.gpsimd.tensor_scalar(rows[:, tiles_, D + 1], cnt[:, 4 + k, tiles_], 1.0, 0.0, ALU.mult, ALU.add).then_inc(rows_rd, 1)
                pool.wait_ge(rows_rd, m + 1)
                for t in part:
                    pool.indirect_dma_start(XS, bass.IndirectOffsetOnAxis(pos[k][:, t:t + 1].bitcast(U32), 0),
                                            rows[:, t, :], None).then_inc(sent[k][2 * t // NT], 16)

            def scatter(r, i):
                for t in range(size(r, False)):
                    pool.wait_ge(y_ev, tiles(r, False) + t + 1)
                    pool.indirect_dma_start(YY, bass.IndirectOffsetOnAxis(dest[i][:, t:t + 1].bitcast(U32), 0), y[:, t, :], None,
                                            bounds_check=2 * N - 1, oob_is_err=False).then_inc(y_out, 16)

            def weights_hi(r, c):
                pool.wait_ge(ld_w[c], r * 16 + 16)
                pool.wait_ge((fc_mm, pj_mm)[c], (r + FIRST - 1) * KH)
                w = (wfc, wpj)[c][side(r)][0][:].rearrange("p k n -> p (k n)")
                n = KD * HID // 4
                for q in range(4):
                    cols = slice(q * n, (q + 1) * n)
                    nc.gpsimd.tensor_scalar(w[:, cols], wstage[:, c, cols], 1.0, 0.0, ALU.mult, ALU.add).then_inc(whi_rd[c], 1)

            for r in range(ROUTED):
                if pool_splits(r + 2, False):
                    weights_hi(r + 2, 0)
                scatter(r, side(r))
                if pool_splits(r + 2, False):
                    weights_hi(r + 2, 1)

            for b in range(B):
                sums = pairs[b % PAIRS]
                pool.wait_ge(ld_y[b % PAIRS], b // PAIRS * 32 + 32)
                nc.gpsimd.tensor_tensor(sums[:, 0:TT * D], sums[:, 0:TT * D], sums[:, TT * D:], ALU.add).then_inc(yy_rd, 1)
                if b in POOL_ADDS:
                    pool.wait_ge(yy_rd, b + 1)
                    pool.wait_ge(acc_rd, max(FIRST, b + 1) * ST)
                    nc.gpsimd.tensor_tensor(sums[:, 0:TT * D], sums[:, 0:TT * D], acc[:, b * TT:(b + 1) * TT, :].rearrange("p t d -> p (t d)"),
                                            ALU.add).then_inc(all_rd, 1)

        @block.scalar
        def _(act):
            def y_results(r, i, small=False):
                act.wait_ge(pj_mm, (r + FIRST + 1) * KH)
                act.wait_ge(meta_rd, r + 1)
                need(act, y_out, tiles(r, small) * 16)
                for t in range(size(r, small)):
                    nc.scalar.activation(y[:, t, :], yb[i][t // 2][:, t % 2 * D:t % 2 * D + D], ACT.Copy,
                                         scale=gate[i][:, t:t + 1]).then_inc(y_ev, 1)

            def tokens(n, i, plan, bank0, r=None, r_next=None, small=False):
                w = buffer(n, i, r)
                for k, (kind, j) in enumerate(plan):
                    b = fcb[(bank0 + k) % 4]
                    cols = slice(0, P * (ST if r is None else size(r, small)))
                    if kind == "T":
                        act.wait_ge(t_mm, r_next * 2 + j + 1)
                        cols = slice(0, size(r_next, small) * P)
                        nc.scalar.activation(xh[1 - i][:, j, cols], b[:, cols], ACT.Copy).then_inc(xh_rd, 1)
                        continue
                    if j == 0 and (r is not None or late(n)):
                        act.wait_ge(ld_b[w], uses(ROUTED if late(n) else r, w) + 32)
                    act.wait_ge(fc_mm, n * KH + j + 1)
                    need(act, hl_rd, n * KH + j - 1)
                    nc.scalar.activation(h[j % 2][:, cols], b[:, cols], ACT.Gelu_apprx_tanh,
                                         bias=bfc[w][:, j:j + 1]).then_inc(h_ev, 1)
                    act.wait_ge(h_ev, n * KH + j + 1)
                    need(act, pj_mm, n * KH + j + 1 - RING)
                    nc.scalar.activation(hh[j % RING][:, cols], h[j % 2][:, cols], ACT.Copy).then_inc(hh_rd, 1)
                    if j == 2 and is_int(n) and n == LATE[0]:
                        y_results(ROUTED - 1, 1 - i)
                    if j == 1 and r is not None and not (is_int(r) and r == 0):
                        y_results(r - 1, 1 - i, small)
                    if is_int(n) and (n, j) in NORMS:
                        normed(NORMS[n, j])

            def normed(b):
                act.wait_ge(st_rd, [b in rows_ for kind, rows_ in PIECES if kind == "rstd"].index(True) + 1)
                for t in range(TT):
                    at = b * TT + t
                    nc.scalar.activation(acc[:, at, :], pairs[b % PAIRS][:, t * D:(t + 1) * D],
                                         ACT.Identity, scale=rs[:, at:at + 1], bias=mean[:, at:at + 1]).then_inc(o_rd, 1)
                act.wait_ge(o_rd, b * TT + TT)
                act.dma_start(out_view[b], acc[:, b * TT:(b + 1) * TT, :]).then_inc(o_out, 16)

            act.wait_ge(d_rd, 1)
            nc.scalar.activation(rt[1][:, :, :], rt[0][:, :, :], ACT.Exp).then_inc(e_rd, 1)
            order(tokens, act)
            for b in range(B - 1):
                if b not in NORMS.values():
                    normed(b)

        @block.vector
        def _(dve):
            link = Links(dve, dve_own)
            tt, ts, stt, red = nc.vector.tensor_tensor, nc.vector.tensor_scalar, nc.vector.scalar_tensor_tensor, nc.vector.tensor_reduce
            per_expert = lambda ap: ap.rearrange("p (e t) -> p e t", e=1).to_broadcast([P, NE, NT])
            per_token = lambda ap: ap.rearrange("p (e t) -> p e t", t=1).to_broadcast([P, NE, NT])
            over_experts = lambda ap: ap.rearrange("p e t -> p t e")

            def shifted_logits():
                link(red(cnt[:, 0, :], logits[:, :, :], AX, ALU.max))
                tt(rt[0][:, :, :], logits[:, :, :].rearrange("p t e -> p e t"), per_expert(cnt[:, 0, :]), ALU.subtract).then_inc(d_rd, 1)

            def probabilities():
                dve.wait_ge(e_rd, 1)
                link(red(cnt[:, 1, :], over_experts(rt[1][:, :, :]), AX, ALU.add))
                link(nc.vector.reciprocal(cnt[:, 1, :], cnt[:, 1, :]))
                link(tt(rt[0][:, :, :], rt[1][:, :, :], per_expert(cnt[:, 1, :]), ALU.mult))

            def choose(k):
                link(red(cnt[:, 2 + k, :], over_experts(rt[0][:, :, :]), AX, ALU.max))
                link(tt(rt[2][:, :, :], rt[0][:, :, :], per_expert(cnt[:, 2 + k, :]), ALU.is_equal))
                link(tt(rt[2][:, :, :], rt[2][:, :, :], per_token(cst[:, KEY:KEY + NE]), ALU.mult))
                link(red(cnt[:, 6, :], over_experts(rt[2][:, :, :]), AX, ALU.max))
                link(tt(choice[k][:, :, :], rt[2][:, :, :], per_expert(cnt[:, 6, :]), ALU.is_equal))
                if k == 0:
                    link(stt(rt[0][:, :, :], choice[0][:, :, :], -2.0, rt[0][:, :, :], ALU.mult, ALU.add))

            def gates():
                tt(both[:, :], choice[0][:, :, :].rearrange("p e t -> p (e t)"), choice[1][:, :, :].rearrange("p e t -> p (e t)"),
                   ALU.add).then_inc(both_rd, 1)
                link(tt(cnt[:, 7, :], cnt[:, 2, :], cnt[:, 3, :], ALU.add))
                link(nc.vector.reciprocal(cnt[:, 7, :], cnt[:, 7, :]))
                for k in range(2):
                    last = tt(cnt[:, 4 + k, :], cnt[:, 2 + k, :], cnt[:, 7, :], ALU.mult)
                link(last)

            def counts():
                dve.wait_ge(cum_mm, 1)
                c = yb[0][0]
                nc.vector.tensor_copy(rt[3][:, :, :].rearrange("p e t -> p (e t)"), c[:, 0:NE * NT])
                link(nc.vector.tensor_copy(rt[1][:, :, :].rearrange("p e t -> p (e t)"), c[:, NE * NT:]))
                nc.vector.tensor_copy(cnt[:, 6, 0:1], rt[1][:, 0, 0:1]).then_inc(cum_rd, 1)
                link(nc.vector.tensor_tensor_scan(rt[2][:, :, :].rearrange("p e t -> p (e t)"), cst[:, GO_ON:GO_ON + NE * NT],
                                                  rt[1][:, :, :].rearrange("p e t -> p (e t)"), 0.0, ALU.mult, ALU.add))

            def starts():
                halves = small_t[:, 0:NE * MOST].rearrange("p (e k) -> p e k", k=MOST)
                over = small_t[:, 0:NE * NE].rearrange("p (e k) -> p e k", k=NE)
                before = cst[:, BEFORE:BEFORE + NE * NE].rearrange("p (e k) -> p e k", k=NE)
                total = rt[2][:, :, NT - 1]
                link(tt(halves, total.rearrange("p (e k) -> p e k", k=1).to_broadcast([P, NE, MOST]),
                        cst[:, FULL:FULL + MOST].rearrange("p (e k) -> p e k", e=1).to_broadcast([P, NE, MOST]), ALU.is_gt))
                red(n_small[:, :], halves, AX, ALU.add)
                link(red(n_big[:, :], halves[:, :, MOST // 2:], AX, ALU.add))
                for n, first in ((n_big, start_big), (n_small, start_small)):
                    link(tt(over, n[:, :].rearrange("p (e k) -> p e k", e=1).to_broadcast([P, NE, NE]), before, ALU.mult))
                    link(red(first[:, :], over, AX, ALU.add))
                    if n is n_big:
                        link(tt(n[:, :], n[:, :], first[:, :], ALU.add))
                        ts(n[:, :], n[:, :], float(BIG), None, ALU.min)
                        link(ts(first[:, :], first[:, :], float(BIG), None, ALU.min))
                        link(tt(n[:, :], n[:, :], first[:, :], ALU.subtract))
                        link(stt(n_small[:, :], n[:, :], -2.0, n_small[:, :], ALU.mult, ALU.add))

            def slots_in_blocks():
                link(tt(rt[2][:, :, :], rt[2][:, :, :], rt[1][:, :, :], ALU.subtract))
                link(tt(rt[2][:, :, :], rt[2][:, :, :], rt[3][:, :, :], ALU.add))
                link(stt(rt[1][:, :, :], per_token(n_big[:, :]), -float(S), rt[2][:, :, :], ALU.mult, ALU.add))
                link(ts(rt[3][:, :, :], rt[1][:, :, :], 0.0, None, ALU.is_ge))
                link(stt(rt[1][:, :, :], per_token(start_small[:, :]), float(HS), rt[1][:, :, :], ALU.mult, ALU.add))
                link(stt(rt[2][:, :, :], per_token(start_big[:, :]), float(S), rt[2][:, :, :], ALU.mult, ALU.add))
                link(ts(rt[1][:, :, :], rt[1][:, :, :], 1.0, float(BIG * S), ALU.mult, ALU.add))
                link(tt(rt[1][:, :, :], rt[1][:, :, :], rt[2][:, :, :], ALU.subtract))
                link(tt(rt[1][:, :, :], rt[1][:, :, :], rt[3][:, :, :], ALU.mult))
                link(tt(rt[2][:, :, :], rt[2][:, :, :], rt[1][:, :, :], ALU.add))

            def slots():
                for k in range(2):
                    link(tt(rt[k][:, :, :], choice[k][:, :, :], rt[2][:, :, :], ALU.mult))
                for k in range(2):
                    last = red(cnt[:, 6 + k, :], over_experts(rt[k][:, :, :]), AX, ALU.add)
                link(last)
                for k in range(2):
                    last = nc.vector.tensor_copy(pos[k][:, :], cnt[:, 6 + k, :])
                last.then_inc(pos_rd, 1)

            def owners():
                for k, (lo, n, first) in enumerate(((0, BIG, start_big), (BIG, SMALL, start_small))):
                    cmp = small_t[:, 0:n * NE].rearrange("p (r e) -> p r e", e=NE)
                    link(tt(cmp, cst[:, BLOCK:BLOCK + n].rearrange("p (r k) -> p r k", k=1).to_broadcast([P, n, NE]),
                            first[:, :].rearrange("p (r k) -> p r k", r=1).to_broadcast([P, n, NE]), ALU.is_ge))
                    link(red(owner_f[:, lo:lo + n], cmp, AX, ALU.add))
                ts(owner[:, :], owner_f[:, :], -1.0, None, ALU.add).then_inc(own_rd, 1)

            def split_piece(r, i, piece, small):
                c, q = piece // 4, piece % 4
                n = KD * HID // 4
                if q == 0:
                    dve.wait_ge(ld_w[c], r * 16 + 16)
                    dve.wait_ge((fc_mm, pj_mm)[c], (r + FIRST - 1) * KH)
                w = [p[:].rearrange("p k n -> p (k n)")[:, q * n:(q + 1) * n] for p in (wfc, wpj)[c][i]]
                src = wstage[:, c, q * n:(q + 1) * n]
                if pool_splits(r, small):
                    dve.wait_ge(whi_rd[c], (r - BIG - 1) * 4 + q + 1)
                else:
                    link(nc.vector.tensor_copy(w[0], src))
                tt(w[1], src, w[0].bitcast(F32), ALU.subtract).then_inc(w_rd[c], 1)

            def slots_meta(r, i, small):
                nt = size(r, small)
                if not late(r + FIRST):
                    dve.wait_ge(ld_xb, r * 16 + 16)
                    need(dve, y_out, tiles(r - 1, small) * 16)
                    nc.vector.tensor_copy(dest[i][:, 0:nt], xb[:, 0:nt, D])
                    nc.vector.tensor_copy(gate[i][:, 0:nt], xb[:, 0:nt, D + 1]).then_inc(meta_rd, 1)
                dve.wait_ge(ld_b[i], uses(r, i) + 32)
                link(nc.vector.tensor_copy(bpj[i][:, :], bpj_raw[i][:, :]))
                tt(bpj[i][LO:BR, :], bpj_raw[i][LO:BR, :], bpj[i][LO:BR, :].bitcast(F32), ALU.subtract).then_inc(bpj_rd, 1)

            def masks():
                dve.wait_ge(ld_tri, 16)
                nc.vector.tensor_copy(trib[:, :, :], tri[:, :, :]).then_inc(tri_rd, 1)

            beside = {(1, 0): lambda: choose(0), (1, 1): lambda: choose(1), (1, 2): lambda: (masks(), gates()),
                      (1, 4): counts, (1, 5): starts, (1, 6): slots_in_blocks, (1, 7): slots, (2, 0): owners}

            def shared_result(n, i):
                dve.wait_ge(pj_mm, (n + 1) * KH)
                if late(n):
                    dve.wait_ge(ld_acc, 16)
                for t in range(ST):
                    tok = bass.ds((n - ROUTED if late(n) else n) * ST + t, 1)
                    x1 = acc[:, tok, :] if late(n) else rows[:, tok, 0:D]
                    tt(acc[:, tok, :].rearrange("p o d -> p (o d)"), yb[i][t // 2][:, t % 2 * D:t % 2 * D + D],
                       x1.rearrange("p o d -> p (o d)"), ALU.add).then_inc(acc_rd, 1)

            def total(piece, batch_rows):
                for b in batch_rows:
                    sums = pairs[b % PAIRS]
                    if piece == "sum":
                        dve.wait_ge(yy_rd, b + 1)
                        if b >= FIRST:
                            dve.wait_ge(acc_rd, b * TT + TT)
                        tt(sums[:, 0:TT * D], sums[:, 0:TT * D], acc[:, b * TT:(b + 1) * TT, :].rearrange("p t d -> p (t d)"),
                           ALU.add).then_inc(tot_rd, 1)
                    if piece == "statistics":
                        if b in POOL_ADDS:
                            dve.wait_ge(all_rd, POOL_ADDS.index(b) + 1)
                        else:
                            dve.wait_ge(tot_rd, b + 1 - sum(other < b for other in POOL_ADDS))
                        for t in range(TT):
                            last = nc.vector.bn_stats(st[:, b % 2 * TT + t, :], sums[:, t * D:(t + 1) * D])
                if piece == "statistics":
                    link(last)
                if piece == "rstd":
                    b, n = batch_rows[0], len(batch_rows) * TT
                    at, now = slice(b % 2 * TT, b % 2 * TT + n), slice(b * TT, b * TT + n)
                    moments(nc, link, st[:, at, :], m_now[:, at], var[:, at], tmp[:, at])
                    rsqrt(nc, link, r_now[:, at], half[:, at], var[:, at], tmp[:, at])
                    nc.vector.tensor_copy(rs[:, now], r_now[:, at])
                    stt(mean[:, now], m_now[:, at], -1.0, r_now[:, at], ALU.mult, ALU.mult).then_inc(st_rd, 1)

            def tokens(n, i, plan, bank0, r=None, r_next=None, small=False):
                for k, (kind, j) in enumerate(plan):
                    cols = slice(0, P * (ST if r is None else size(r, small)))
                    if kind == "T":
                        cols = slice(0, size(r_next, small) * P)
                        dve.wait_ge(xh_rd, r_next * 2 + j + 1)
                        tt(xl[1 - i][:, j, cols], fcb[(bank0 + k) % 4][:, cols], xh[1 - i][:, j, cols].bitcast(F32), ALU.subtract).then_inc(xl_rd, 1)
                        continue
                    dve.wait_ge(hh_rd, n * KH + j + 1)
                    tt(hl[j % RING][:, cols], h[j % 2][:, cols], hh[j % RING][:, cols].bitcast(F32), ALU.subtract).then_inc(hl_rd, 1)
                    if is_int(n) and (n, j) in beside:
                        beside[n, j]()
                    if j == 1 and (r is None or (is_int(r) and r == 0)) and not (is_int(n) and n in (0, LATE[0])):
                        if is_int(n) and n == 1:
                            dve.wait_ge(ld_rows0, 16)
                        if is_int(n) and n == 2:
                            dve.wait_ge(ld_rows, 16)
                        shared_result(n - 1, 1 - i)
                    if is_int(n) and (n, j) in SUMS:
                        total(*SUMS[n, j])
                    if r_next is not None:
                        split_piece(r_next, 1 - i, j, small)
                if r_next is not None:
                    slots_meta(r_next, 1 - i, small)

            def counted(n, *args, small=False, **kw):
                if is_int(n):
                    if link.loop:
                        link.end(loops.pop(0))
                    tokens(n, *args, small=small, **kw)
                else:
                    link.enter(n, FIRST + (BIG + 1 if small else 2), SMALL_LINKS if small else BLOCK_LINKS)
                    tokens(n, *args, small=small, **kw)
                    link.leave()

            loops = [BIG - 3, SMALL - 3]
            shifted_logits()
            probabilities()
            dve.wait_ge(ld_c, 16)
            order(counted, dve)

            done = len(SUMS)
            for piece in PIECES[done:done + PIECES[done:].index(("sum", (B - 1,)))]:
                total(*piece)
            shared_result(LATE[-1], LATE[-1] % 2)
            for piece in PIECES[-3:]:
                total(*piece)
            dve.wait_ge(st_rd, [kind for kind, rows_ in PIECES].count("rstd"))
            for t in range((B - 1) * TT, B * TT):
                ts(acc[:, t, :], pairs[(B - 1) % PAIRS][:, t % TT * D:(t % TT + 1) * D], rs[:, t:t + 1], mean[:, t:t + 1],
                   ALU.mult, ALU.add).then_inc(last_rd, 1)

        @block.tensor
        def _(pe):
            mm = nc.tensor.matmul

            def project(n, i, j, r, small):
                w = buffer(n, i, r)
                pe.wait_ge(hl_rd, n * KH + j + 1)
                if j == 0:
                    if r is not None or late(n):
                        e = ROUTED if late(n) else r
                        pe.wait_ge(bpj_rd, e + 1)
                        pe.wait_ge(w_rd[1], (e + 1) * 4)
                    if late(n) and n < LATE[0] + 2:
                        pe.wait_ge(y_ev, tiles(n - FIRST - 1, False))
                    elif late(n):
                        pe.wait_ge(acc_rd, (n - 1 - ROUTED) * ST)
                    elif r is None or (is_int(r) and r < 2):
                        need(pe, acc_rd, (n - 1) * ST)
                    else:
                        pe.wait_ge(y_ev, tiles(r - 1, small))
                    if is_int(n) and n == 2:
                        pe.wait_ge(cum_rd, 1)
                for t in range(ST if r is None else size(r, small)):
                    o = yb[i][t // 2][:, t % 2 * D:t % 2 * D + D]
                    cols = slice(t * P, (t + 1) * P)
                    if j == 0:
                        mm(o, ones[:, :], bpj[w][:, :], start=t % 2 == 0, stop=False, skip_group_check=True)
                    hs = (hh[j % RING], hl[j % RING], hh[j % RING])
                    for p, ws in enumerate((1, 0, 0)):
                        last = mm(o, hs[p][:, cols], wpj[w][ws][:, j, :], start=False,
                                  stop=j == KH - 1 and p == 2, skip_group_check=True)
                last.then_inc(pj_mm, 1)

            def tokens(n, i, plan, bank0, r=None, r_next=None, small=False):
                w = buffer(n, i, r)
                before = PLAIN if r is None else FIRST_T if is_int(r) and r == 0 else WITH_T
                for k, (kind, j) in enumerate(plan):
                    if k >= 4:
                        okind, oj = plan[k - 4]
                        if okind == "fc":
                            pe.wait_ge(h_ev, n * KH + oj + 1)
                        else:
                            pe.wait_ge(xl_rd, r_next * 2 + oj + 1)
                    else:
                        okind, oj = before[k - 4]
                        if okind == "fc":
                            pe.wait_ge(h_ev, (n - 1) * KH + oj + 1)
                        else:
                            pe.wait_ge(xl_rd, r * 2 + oj + 1)
                    b = fcb[(bank0 + k) % 4]
                    if kind == "T":
                        if j == 0:
                            pe.wait_ge(ld_xb, r_next * 16 + 16)
                        for t in range(size(r_next, small)):
                            last = nc.tensor.transpose(b[:, t * P:(t + 1) * P], xb[:, t, j * P:(j + 1) * P], ident[:, :])
                        last.then_inc(t_mm, 1)
                        continue
                    if j == 0:
                        if r is None:
                            pe.wait_ge(ld_xT[i], ((n - ROUTED if late(n) else n) - i) * 16 + 32)
                        if late(n):
                            pe.wait_ge(w_rd[0], (ROUTED + 1) * 4)
                        if r is not None:
                            pe.wait_ge(xl_rd, r * 2 + 2)
                            pe.wait_ge(w_rd[0], (r + 1) * 4)
                    rows_ = slice(j * P, (j + 1) * P)
                    cols = slice(0, P * (ST if r is None else size(r, small)))
                    for c in range(KD):
                        for p, (ws, xs) in enumerate(((0, xl), (1, xh), (0, xh))):
                            last = mm(b[:, cols], wfc[w][ws][:, c, rows_], xs[i][:, c, cols], start=c == 0 and p == 0,
                                      stop=c == KD - 1 and p == 2)
                    last.then_inc(fc_mm, 1)
                    if is_int(n) and n == 1 and j == 4:
                        pe.wait_ge(both_rd, 1)
                        pe.wait_ge(tri_rd, 1)
                        c = yb[0][0]
                        pe.wait_ge(acc_rd, ST)
                        mm(c[:, 0:NE * NT], trib[:, 0, :], both[:, :], start=True, stop=True)
                        mm(c[:, NE * NT:], trib[:, 1, :], both[:, :], start=True, stop=True).then_inc(cum_mm, 1)
                    if j >= 2:
                        project(n, i, j - 2, r, small)
                    elif not (is_int(n) and n == 1):
                        if is_int(n) and n == LATE[0]:
                            project(n - 1, 1 - i, KH - 2 + j, ROUTED - 1, small)
                        elif r is None:
                            project(n - 1, 1 - i, KH - 2 + j, None, small)
                        else:
                            project(n - 1, 1 - i, KH - 2 + j, None if is_int(r) and r == 0 else r - 1, small)

            order(tokens, pe)
            for j in (KH - 2, KH - 1):
                project(LATE[-1], LATE[-1] % 2, j, None, False)


KEY = 0
MOST = N // HS
FULL = KEY + NE
BEFORE = FULL + MOST
BLOCK = BEFORE + NE * NE
TOK = BLOCK + BIG
GO_ON = TOK + NT


def constants():
    route = np.zeros((P, GO_ON + NE * NT), np.float32)
    route[:, KEY:KEY + NE] = NE - np.arange(NE)
    route[:, FULL:FULL + MOST] = HS * np.concatenate([np.arange(0, MOST, 2), np.arange(1, MOST, 2)])
    route[:, BEFORE:BEFORE + NE * NE] = np.tril(np.ones((NE, NE)), -1).reshape(-1)
    route[:, BLOCK:BLOCK + BIG] = np.arange(BIG)
    route[:, TOK:TOK + NT] = np.arange(P)[:, None] + P * np.arange(NT)
    route[:, GO_ON:] = (np.arange(NE * NT) % NT != 0)
    tri = np.stack([np.triu(np.ones((P, P)), 1), np.ones((P, P))], 1).astype(np.float32)
    half = QK // 2
    freq = np.float32(10000.0) ** (-np.arange(half, dtype=np.float32) / np.float32(half))
    angle = (np.arange(T, dtype=np.float32)[:, None] * freq[None, :]).T.astype(np.float64)
    cos, sin = np.cos(angle), np.sin(angle)
    rope = np.stack([np.concatenate([cos] * 4), np.concatenate([-sin, sin] * 2)], 1).astype(np.float32)
    empty = np.zeros((P, ROW), np.float32)
    empty[:, D] = NOWHERE
    return {"route": route, "tri": tri, "rope": rope, "empty": empty, "ident": np.eye(P, dtype=np.float32),
            "ones": np.ones((BR, P), np.float32)}


def layout(i):
    f = {k: np.asarray(v) for k, v in i.items()}
    A, F = "L0_attn_", "L0_ffn_"
    halves = lambda x: np.concatenate([x[..., QK // 2:], x[..., :QK // 2]], -1)
    twice = lambda x, y: np.stack([np.concatenate([x, y]), np.concatenate([halves(x), halves(y)])], 1)
    chunks = lambda x: x.reshape(-1, P, x.shape[-1]).transpose(1, 0, 2)
    g, be, bqk = f[A + "gamma"], f[A + "beta"], f[A + "bqk"]
    vec = np.concatenate([twice(bqk, bqk), twice(g[0], g[1]), twice(g[2], g[3]), twice(be[0], be[1]), twice(be[2], be[3]),
                          f[A + "ln1_w"].reshape(KD, P).T, f[A + "ln1_b"].reshape(KD, P).T, f[A + "bg"].reshape(KE, P).T], 1)
    wqk = f[A + "Wqk"].T
    wqk = np.stack([chunks(np.concatenate([w, w], 1)) for w in (wqk, halves(wqk))], 1)
    rows = np.zeros((BR, 2, E), np.float32)
    rows[::LO, 0, :] = f[A + "bv"]
    rows[::LO, 1, 0:D] = f[A + "bo"]
    pe = f[A + "pos_emb"]
    far = np.repeat(pe[MAX_REL:MAX_REL + 1], G - 1 - MAX_REL)
    ext = np.concatenate([far, pe[MAX_REL:0:-1], pe[0:MAX_REL + 1], far])
    wall = np.stack([np.stack([chunks(a).reshape(P, -1), chunks(b).reshape(P, -1)], 1)
                     for a, b in [*zip(f[F + "Wfc"], f[F + "Wproj"]), (f[F + "Wfc_s"], f[F + "Wproj_s"])]])
    bfc = np.concatenate([f[F + "bfc"], f[F + "bfc_s"][None]]).reshape(NE + 1, KH, P).transpose(0, 2, 1)
    bproj = np.zeros((NE + 1, BR, D), np.float32)
    bproj[:, ::LO] = np.concatenate([f[F + "bproj"], f[F + "bproj_s"][None]])[:, None, :]
    return {"x": f[A + "x"].reshape(N, D), "vec": vec, "wqk": wqk, "wv": chunks(f[A + "Wv"].T), "wg": chunks(f[A + "Wg"].T),
            "wo": chunks(f[A + "Wo"].T), "rows": rows, "ext": np.tile(ext, G),
            "ln2": np.repeat(np.stack([f[A + "ln2_w"], f[A + "ln2_b"]])[None], P, 0), "wr": chunks(f[F + "Wr"]),
            "wall": wall, "bfc": bfc, "bproj": bproj}


def kernel(**inputs):
    import concourse.bacc as bacc
    from concourse.bass_utils import run_bass_kernel_spmd

    nc = bacc.Bacc("TRN2", target_bir_lowering=False, num_devices=1)
    arrays = {k: np.ascontiguousarray(v) for k, v in {**layout(inputs), **constants()}.items()}
    aps = {k: nc.dram_tensor(k, v.shape, mybir.dt.from_np(v.dtype), kind="ExternalInput").ap() for k, v in arrays.items()}
    out = nc.dram_tensor("out", (N, D), F32, kind="ExternalOutput").ap()
    build(nc, aps, out)
    r = run_bass_kernel_spmd(nc, [arrays], core_ids=[0])
    return r.results[0]["out"].reshape(B, T, D)
```
